# Optimizing a Trainium2 kernel written in Bass

```python
import numpy as np
import jax
import jax.numpy as jnp

def _softmax(x, axis=-1):
    return jax.nn.softmax(x, axis=axis)

def _gelu(x):
    return jax.nn.gelu(x, approximate=True)

def _silu(x):
    return jax.nn.silu(x)

def _sigmoid(x):
    return jax.nn.sigmoid(x)

def _layernorm(x, axis=-1, eps=1e-05):
    m = jnp.mean(x, axis=axis, keepdims=True)
    v = jnp.var(x, axis=axis, keepdims=True)
    return (x - m) / jnp.sqrt(v + eps)

def _scatter_add(tgt, idx, src, axis=0):
    return tgt.at[idx].add(src)

def _segment_sum(src, seg, n):
    return jax.ops.segment_sum(src, seg, n)
kernel_name = 'mk_hybrid_d2_jaxref_r8_6f3aae'

def setup_inputs(seed: int=0):
    np.random.seed(seed)
    _w = jnp.asarray

    def _L0_attn_a_setup():
        import jax, jax.numpy as jnp
        import numpy as np
        B, S, HID = (1, 256, 256)
        H, KVH, HD = (32, 8, 64)
        THETA = 10000.0

        def _rotate_half(x):
            x1, x2 = jnp.split(x, 2, axis=-1)
            return jnp.concatenate([-x2, x1], axis=-1)

        def _rope_cos_sin(seq_len, head_dim, theta, dtype):
            inv_freq = 1.0 / theta ** (jnp.arange(0, head_dim, 2, dtype=jnp.float32) / head_dim)
            pos = jnp.arange(seq_len, dtype=jnp.float32)
            freqs = pos[:, None] * inv_freq[None, :]
            emb = jnp.concatenate([freqs, freqs], axis=-1)
            return (jnp.cos(emb).astype(dtype), jnp.sin(emb).astype(dtype))
        key = jax.random.key(seed)
        k0, k1, k2, k3, k4 = jax.random.split(key, 5)
        w = lambda k, shape: jax.random.normal(k, shape, dtype=jnp.float32) * 0.02
        return {'hidden_states': jax.random.normal(k0, (B, S, HID), dtype=jnp.float32), 'Wq': w(k1, (H * HD, HID)), 'Wk': w(k2, (KVH * HD, HID)), 'Wv': w(k3, (KVH * HD, HID)), 'Wo': w(k4, (HID, H * HD))}
    _L0_attn_a_in = _L0_attn_a_setup()

    def _L0_attn_b_setup():
        import jax, jax.numpy as jnp
        import numpy as np
        BATCH, SEQ, D_MODEL, N_HEADS, D_HEAD = (2, 256, 256, 16, 128)
        ATTN_SCALE = np.sqrt(D_HEAD).astype(np.float32)
        IGNORE = jnp.float32(-100000.0)
        key = jax.random.key(seed)
        ks = jax.random.split(key, 5)
        init = 1.0 / np.sqrt(D_MODEL)
        return {'x': jax.random.normal(ks[0], (BATCH, SEQ, D_MODEL), jnp.float32), 'W_Q': jax.random.normal(ks[1], (N_HEADS, D_MODEL, D_HEAD), jnp.float32) * init, 'W_K': jax.random.normal(ks[2], (N_HEADS, D_MODEL, D_HEAD), jnp.float32) * init, 'W_V': jax.random.normal(ks[3], (N_HEADS, D_MODEL, D_HEAD), jnp.float32) * init, 'W_O': jax.random.normal(ks[4], (N_HEADS, D_HEAD, D_MODEL), jnp.float32) * init, 'b_Q': jnp.zeros((N_HEADS, D_HEAD), jnp.float32), 'b_K': jnp.zeros((N_HEADS, D_HEAD), jnp.float32), 'b_V': jnp.zeros((N_HEADS, D_HEAD), jnp.float32), 'b_O': jnp.zeros((D_MODEL,), jnp.float32)}
    _L0_attn_b_in = _L0_attn_b_setup()

    def _L0_ffn_setup():
        import jax, jax.numpy as jnp
        import numpy as np
        CAPACITY = 0.125
        HEAD_DIM = 128
        N_HEADS = 16
        N_KV_HEADS = 8
        ROPE_THETA = 10000.0
        EPS = 1e-06

        def _rms_norm(x, w):
            return x * jax.lax.rsqrt(jnp.mean(x * x, axis=-1, keepdims=True) + EPS) * w

        def _rotate_half(t):
            h = t.shape[-1] // 2
            return jnp.concatenate([-t[..., h:], t[..., :h]], axis=-1)
        key = jax.random.key(seed)
        ks = jax.random.split(key, 12)
        B, T, D = (4, 512, 256)
        I = 1024
        s = 0.02
        return {'hidden_states': jax.random.normal(ks[0], (B, T, D), jnp.float32), 'w_router': jax.random.normal(ks[1], (D,), jnp.float32) * s, 'wq': jax.random.normal(ks[2], (D, N_HEADS * HEAD_DIM), jnp.float32) * s, 'bq': jnp.zeros((N_HEADS * HEAD_DIM,), jnp.float32), 'wk': jax.random.normal(ks[3], (D, N_KV_HEADS * HEAD_DIM), jnp.float32) * s, 'bk': jnp.zeros((N_KV_HEADS * HEAD_DIM,), jnp.float32), 'wv': jax.random.normal(ks[4], (D, N_KV_HEADS * HEAD_DIM), jnp.float32) * s, 'bv': jnp.zeros((N_KV_HEADS * HEAD_DIM,), jnp.float32), 'wo': jax.random.normal(ks[5], (N_HEADS * HEAD_DIM, D), jnp.float32) * s, 'w_gate': jax.random.normal(ks[6], (D, I), jnp.float32) * s, 'w_up': jax.random.normal(ks[7], (D, I), jnp.float32) * s, 'w_down': jax.random.normal(ks[8], (I, D), jnp.float32) * s, 'ln1_w': jnp.ones((D,), jnp.float32), 'ln2_w': jnp.ones((D,), jnp.float32)}
    _L0_ffn_in = _L0_ffn_setup()

    def _L1_attn_a_setup():
        import jax, jax.numpy as jnp
        import numpy as np
        B, T, C = (4, 512, 256)

        def _scan_op(a, bb):
            g_i, v_i = a
            g_j, v_j = bb
            return (g_j * g_i, g_j * v_i + v_j)
        key = jax.random.key(seed)
        k1, k2 = jax.random.split(key)
        x = jax.random.normal(k1, (B, T, C), dtype=jnp.float32)
        W = jax.random.normal(k2, (2 * C, C), dtype=jnp.float32) * (1.0 / np.sqrt(C))
        b = jnp.zeros((2 * C,), dtype=jnp.float32)
        return {'x': x, 'W': W, 'b': b}
    _L1_attn_a_in = _L1_attn_a_setup()

    def _L1_attn_b_setup():
        import jax, jax.numpy as jnp
        import numpy as np
        EPS = 1e-08
        C_RGLRU = 8.0

        def rmsnorm(x, w):
            rms = jnp.sqrt(jnp.mean(x * x, axis=-1, keepdims=True) + EPS)
            return w * (x / rms)

        def causal_depthwise_conv(x, conv_w, conv_b):
            K = conv_w.shape[0]
            S = x.shape[1]
            xp = jnp.pad(x, ((0, 0), (K - 1, 0), (0, 0)))
            y = sum((conv_w[k] * xp[:, k:k + S, :] for k in range(K)))
            return y + conv_b

        def rg_lru(x, ga_W, ga_b, gx_W, gx_b, a_param):
            r = jax.nn.sigmoid(x @ ga_W + ga_b)
            i = jax.nn.sigmoid(x @ gx_W + gx_b)
            log_a = -C_RGLRU * jax.nn.softplus(a_param) * r
            a = jnp.exp(log_a)
            mult = jnp.sqrt(-jnp.expm1(2.0 * log_a))
            b = mult * (i * x)

            def combine(c1, c2):
                a1, b1 = c1
                a2, b2 = c2
                return (a1 * a2, a2 * b1 + b2)
            _, h = jax.lax.associative_scan(combine, (a, b), axis=1)
            return h
        D, H, F, K, B, S = (256, 256, 768, 4, 2, 256)
        key = jax.random.key(seed)
        ks = jax.random.split(key, 16)

        def lin(k, fan_in, shape):
            return jax.random.normal(k, shape, jnp.float32) * fan_in ** (-0.5)
        return {'x': jax.random.normal(ks[0], (B, S, D), jnp.float32), 'norm1_w': jnp.ones((D,), jnp.float32), 'left_W': lin(ks[1], D, (D, H)), 'left_b': jnp.zeros((H,), jnp.float32), 'right_W': lin(ks[2], D, (D, H)), 'right_b': jnp.zeros((H,), jnp.float32), 'conv_w': lin(ks[3], K, (K, H)), 'conv_b': jnp.zeros((H,), jnp.float32), 'ga_W': lin(ks[4], H, (H, H)), 'ga_b': jnp.zeros((H,), jnp.float32), 'gx_W': lin(ks[5], H, (H, H)), 'gx_b': jnp.zeros((H,), jnp.float32), 'a_param': jax.random.uniform(ks[6], (H,), jnp.float32, 0.5, 3.0), 'out_W': lin(ks[7], H, (H, D)), 'out_b': jnp.zeros((D,), jnp.float32), 'norm2_w': jnp.ones((D,), jnp.float32), 'up1_W': lin(ks[8], D, (D, F)), 'up1_b': jnp.zeros((F,), jnp.float32), 'up2_W': lin(ks[9], D, (D, F)), 'up2_b': jnp.zeros((F,), jnp.float32), 'down_W': lin(ks[10], F, (F, D)), 'down_b': jnp.zeros((D,), jnp.float32)}
    _L1_attn_b_in = _L1_attn_b_setup()

    def _L1_ffn_setup():
        import jax, jax.numpy as jnp
        import numpy as np
        D_MODEL = 256
        D_EXPERT = 1024
        EPS = 1e-08

        def ternary_quant(w):
            scale = jnp.mean(jnp.abs(w)) + EPS
            q = jnp.clip(jnp.round(w / scale), -1.0, 1.0) * scale
            return w + jax.lax.stop_gradient(q - w)
        key = jax.random.key(seed)
        k_x, k_up, k_gate, k_down = jax.random.split(key, 4)
        std_in = 1.0 / np.sqrt(D_MODEL)
        std_exp = 1.0 / np.sqrt(D_EXPERT)
        return {'x': jax.random.normal(k_x, (4, 256, D_MODEL), dtype=jnp.float32), 'W_up': jax.random.normal(k_up, (D_EXPERT, D_MODEL), dtype=jnp.float32) * std_in, 'W_gate': jax.random.normal(k_gate, (D_EXPERT, D_MODEL), dtype=jnp.float32) * std_in, 'W_down': jax.random.normal(k_down, (D_MODEL, D_EXPERT), dtype=jnp.float32) * std_exp}
    _L1_ffn_in = _L1_ffn_setup()
    _d = {'L0_attn_a_hidden_states': _L0_attn_a_in['hidden_states'], 'L0_attn_a_Wq': _L0_attn_a_in['Wq'], 'L0_attn_a_Wk': _L0_attn_a_in['Wk'], 'L0_attn_a_Wv': _L0_attn_a_in['Wv'], 'L0_attn_a_Wo': _L0_attn_a_in['Wo'], 'L0_attn_b_W_Q': _L0_attn_b_in['W_Q'], 'L0_attn_b_W_K': _L0_attn_b_in['W_K'], 'L0_attn_b_W_V': _L0_attn_b_in['W_V'], 'L0_attn_b_W_O': _L0_attn_b_in['W_O'], 'L0_attn_b_b_Q': _L0_attn_b_in['b_Q'], 'L0_attn_b_b_K': _L0_attn_b_in['b_K'], 'L0_attn_b_b_V': _L0_attn_b_in['b_V'], 'L0_attn_b_b_O': _L0_attn_b_in['b_O'], 'L0_ffn_w_router': _L0_ffn_in['w_router'], 'L0_ffn_wq': _L0_ffn_in['wq'], 'L0_ffn_bq': _L0_ffn_in['bq'], 'L0_ffn_wk': _L0_ffn_in['wk'], 'L0_ffn_bk': _L0_ffn_in['bk'], 'L0_ffn_wv': _L0_ffn_in['wv'], 'L0_ffn_bv': _L0_ffn_in['bv'], 'L0_ffn_wo': _L0_ffn_in['wo'], 'L0_ffn_w_gate': _L0_ffn_in['w_gate'], 'L0_ffn_w_up': _L0_ffn_in['w_up'], 'L0_ffn_w_down': _L0_ffn_in['w_down'], 'L0_ffn_ln1_w': _L0_ffn_in['ln1_w'], 'L0_ffn_ln2_w': _L0_ffn_in['ln2_w'], 'L1_attn_a_W': _L1_attn_a_in['W'], 'L1_attn_a_b': _L1_attn_a_in['b'], 'L1_attn_b_norm1_w': _L1_attn_b_in['norm1_w'], 'L1_attn_b_left_W': _L1_attn_b_in['left_W'], 'L1_attn_b_left_b': _L1_attn_b_in['left_b'], 'L1_attn_b_right_W': _L1_attn_b_in['right_W'], 'L1_attn_b_right_b': _L1_attn_b_in['right_b'], 'L1_attn_b_conv_w': _L1_attn_b_in['conv_w'], 'L1_attn_b_conv_b': _L1_attn_b_in['conv_b'], 'L1_attn_b_ga_W': _L1_attn_b_in['ga_W'], 'L1_attn_b_ga_b': _L1_attn_b_in['ga_b'], 'L1_attn_b_gx_W': _L1_attn_b_in['gx_W'], 'L1_attn_b_gx_b': _L1_attn_b_in['gx_b'], 'L1_attn_b_a_param': _L1_attn_b_in['a_param'], 'L1_attn_b_out_W': _L1_attn_b_in['out_W'], 'L1_attn_b_out_b': _L1_attn_b_in['out_b'], 'L1_attn_b_norm2_w': _L1_attn_b_in['norm2_w'], 'L1_attn_b_up1_W': _L1_attn_b_in['up1_W'], 'L1_attn_b_up1_b': _L1_attn_b_in['up1_b'], 'L1_attn_b_up2_W': _L1_attn_b_in['up2_W'], 'L1_attn_b_up2_b': _L1_attn_b_in['up2_b'], 'L1_attn_b_down_W': _L1_attn_b_in['down_W'], 'L1_attn_b_down_b': _L1_attn_b_in['down_b'], 'L1_ffn_W_up': _L1_ffn_in['W_up'], 'L1_ffn_W_gate': _L1_ffn_in['W_gate'], 'L1_ffn_W_down': _L1_ffn_in['W_down']}
    _x0 = _d['L0_attn_a_hidden_states']
    _d['L0_attn_a_hidden_states'] = jax.random.normal(jax.random.fold_in(jax.random.key(seed), 1), (1, 1024, 256), dtype=_x0.dtype)
    del _x0
    return _d

def reference(L0_attn_a_hidden_states, L0_attn_a_Wq, L0_attn_a_Wk, L0_attn_a_Wv, L0_attn_a_Wo, L0_attn_b_W_Q, L0_attn_b_W_K, L0_attn_b_W_V, L0_attn_b_W_O, L0_attn_b_b_Q, L0_attn_b_b_K, L0_attn_b_b_V, L0_attn_b_b_O, L0_ffn_w_router, L0_ffn_wq, L0_ffn_bq, L0_ffn_wk, L0_ffn_bk, L0_ffn_wv, L0_ffn_bv, L0_ffn_wo, L0_ffn_w_gate, L0_ffn_w_up, L0_ffn_w_down, L0_ffn_ln1_w, L0_ffn_ln2_w, L1_attn_a_W, L1_attn_a_b, L1_attn_b_norm1_w, L1_attn_b_left_W, L1_attn_b_left_b, L1_attn_b_right_W, L1_attn_b_right_b, L1_attn_b_conv_w, L1_attn_b_conv_b, L1_attn_b_ga_W, L1_attn_b_ga_b, L1_attn_b_gx_W, L1_attn_b_gx_b, L1_attn_b_a_param, L1_attn_b_out_W, L1_attn_b_out_b, L1_attn_b_norm2_w, L1_attn_b_up1_W, L1_attn_b_up1_b, L1_attn_b_up2_W, L1_attn_b_up2_b, L1_attn_b_down_W, L1_attn_b_down_b, L1_ffn_W_up, L1_ffn_W_gate, L1_ffn_W_down):

    def _L0_attn_a_ref(hidden_states, Wq, Wk, Wv, Wo):
        import jax, jax.numpy as jnp
        import numpy as np
        B, S, HID = (1, 256, 256)
        H, KVH, HD = (32, 8, 64)
        THETA = 10000.0

        def _rotate_half(x):
            x1, x2 = jnp.split(x, 2, axis=-1)
            return jnp.concatenate([-x2, x1], axis=-1)

        def _rope_cos_sin(seq_len, head_dim, theta, dtype):
            inv_freq = 1.0 / theta ** (jnp.arange(0, head_dim, 2, dtype=jnp.float32) / head_dim)
            pos = jnp.arange(seq_len, dtype=jnp.float32)
            freqs = pos[:, None] * inv_freq[None, :]
            emb = jnp.concatenate([freqs, freqs], axis=-1)
            return (jnp.cos(emb).astype(dtype), jnp.sin(emb).astype(dtype))
        b, s, _ = hidden_states.shape
        dtype = hidden_states.dtype
        q = (hidden_states @ Wq.T).reshape(b, s, H, HD).transpose(0, 2, 1, 3)
        k = (hidden_states @ Wk.T).reshape(b, s, KVH, HD).transpose(0, 2, 1, 3)
        v = (hidden_states @ Wv.T).reshape(b, s, KVH, HD).transpose(0, 2, 1, 3)
        cos, sin = _rope_cos_sin(s, HD, THETA, dtype)
        apply_rope = lambda x: x * cos + _rotate_half(x) * sin
        q = apply_rope(q)
        k = apply_rope(k)
        groups = H // KVH
        k = jnp.repeat(k, groups, axis=1)
        v = jnp.repeat(v, groups, axis=1)
        scale = 1.0 / jnp.sqrt(jnp.asarray(HD, dtype=dtype))
        logits = jnp.einsum('bhqd,bhkd->bhqk', q, k) * scale
        causal = jnp.tril(jnp.ones((s, s), dtype=bool))
        logits = jnp.where(causal, logits, jnp.finfo(dtype).min)
        attn = jax.nn.softmax(logits, axis=-1)
        out = jnp.einsum('bhqk,bhkd->bhqd', attn, v)
        out = out.transpose(0, 2, 1, 3).reshape(b, s, H * HD)
        return out @ Wo.T

    def _L0_attn_b_ref(x, W_Q, W_K, W_V, W_O, b_Q, b_K, b_V, b_O):
        import jax, jax.numpy as jnp
        import numpy as np
        BATCH, SEQ, D_MODEL, N_HEADS, D_HEAD = (2, 256, 256, 16, 128)
        ATTN_SCALE = np.sqrt(D_HEAD).astype(np.float32)
        IGNORE = jnp.float32(-100000.0)
        q = jnp.einsum('bpd,hde->bphe', x, W_Q) + b_Q
        k = jnp.einsum('bpd,hde->bphe', x, W_K) + b_K
        v = jnp.einsum('bpd,hde->bphe', x, W_V) + b_V
        scores = jnp.einsum('bqhe,bkhe->bhqk', q, k) / ATTN_SCALE
        S = x.shape[1]
        causal = jnp.tril(jnp.ones((S, S), bool))
        scores = jnp.where(causal, scores, IGNORE)
        attn = jax.nn.softmax(scores, axis=-1)
        z = jnp.einsum('bkhe,bhqk->bqhe', v, attn)
        out = jnp.einsum('bqhe,hed->bqd', z, W_O) + b_O
        return out

    def _L0_ffn_ref(hidden_states, w_router, wq, bq, wk, bk, wv, bv, wo, w_gate, w_up, w_down, ln1_w, ln2_w):
        import jax, jax.numpy as jnp
        import numpy as np
        CAPACITY = 0.125
        HEAD_DIM = 128
        N_HEADS = 16
        N_KV_HEADS = 8
        ROPE_THETA = 10000.0
        EPS = 1e-06

        def _rms_norm(x, w):
            return x * jax.lax.rsqrt(jnp.mean(x * x, axis=-1, keepdims=True) + EPS) * w

        def _rotate_half(t):
            h = t.shape[-1] // 2
            return jnp.concatenate([-t[..., h:], t[..., :h]], axis=-1)
        B, T, D = hidden_states.shape
        k = max(1, int(T * CAPACITY))
        scores = jnp.einsum('btd,d->bt', hidden_states, w_router)
        _, idx = jax.lax.top_k(scores, k)
        idx = jnp.sort(idx, axis=-1)
        b = jnp.arange(B)[:, None]
        sel = hidden_states[b, idx]
        sel_scores = scores[b, idx]
        S = B * k
        x = sel.reshape(S, D)
        pos = idx.reshape(S)
        inv_freq = 1.0 / ROPE_THETA ** (jnp.arange(0, HEAD_DIM, 2, dtype=jnp.float32) / HEAD_DIM)
        ang = pos.astype(jnp.float32)[:, None] * inv_freq
        cos = jnp.concatenate([jnp.cos(ang), jnp.cos(ang)], axis=-1)[:, None, :]
        sin = jnp.concatenate([jnp.sin(ang), jnp.sin(ang)], axis=-1)[:, None, :]
        h = _rms_norm(x, ln1_w)
        q = (h @ wq + bq).reshape(S, N_HEADS, HEAD_DIM)
        kk = (h @ wk + bk).reshape(S, N_KV_HEADS, HEAD_DIM)
        v = (h @ wv + bv).reshape(S, N_KV_HEADS, HEAD_DIM)
        q = q * cos + _rotate_half(q) * sin
        kk = kk * cos + _rotate_half(kk) * sin
        rep = N_HEADS // N_KV_HEADS
        kk = jnp.repeat(kk, rep, axis=1)
        v = jnp.repeat(v, rep, axis=1)
        att = jnp.einsum('shd,thd->hst', q, kk) / np.sqrt(HEAD_DIM)
        causal = jnp.tril(jnp.ones((S, S), bool))
        att = jnp.where(causal[None], att, jnp.finfo(att.dtype).min)
        att = jax.nn.softmax(att, axis=-1)
        attn_out = jnp.einsum('hst,thd->shd', att, v).reshape(S, N_HEADS * HEAD_DIM) @ wo
        x1 = x + attn_out
        h2 = _rms_norm(x1, ln2_w)
        mlp = jax.nn.silu(h2 @ w_gate) * (h2 @ w_up) @ w_down
        processed = x1 + mlp
        gate = jax.nn.sigmoid(sel_scores).reshape(S, 1)
        gated = gate * processed + (1.0 - gate) * x
        output = hidden_states.at[b, idx].set(gated.reshape(B, k, D))
        return output

    def _L1_attn_a_ref(x, W, b):
        import jax, jax.numpy as jnp
        import numpy as np
        B, T, C = (4, 512, 256)

        def _scan_op(a, bb):
            g_i, v_i = a
            g_j, v_j = bb
            return (g_j * g_i, g_j * v_i + v_j)
        params = jnp.einsum('btc,dc->btd', x, W) + b
        gates, values = jnp.split(params, 2, axis=-1)
        gates = jax.nn.sigmoid(gates)
        values = jnp.tanh(values)
        _, hidden = jax.lax.associative_scan(_scan_op, (gates, values), axis=1)
        return hidden

    def _L1_attn_b_ref(x, norm1_w, left_W, left_b, right_W, right_b, conv_w, conv_b, ga_W, ga_b, gx_W, gx_b, a_param, out_W, out_b, norm2_w, up1_W, up1_b, up2_W, up2_b, down_W, down_b):
        import jax, jax.numpy as jnp
        import numpy as np
        EPS = 1e-08
        C_RGLRU = 8.0

        def rmsnorm(x, w):
            rms = jnp.sqrt(jnp.mean(x * x, axis=-1, keepdims=True) + EPS)
            return w * (x / rms)

        def causal_depthwise_conv(x, conv_w, conv_b):
            K = conv_w.shape[0]
            S = x.shape[1]
            xp = jnp.pad(x, ((0, 0), (K - 1, 0), (0, 0)))
            y = sum((conv_w[k] * xp[:, k:k + S, :] for k in range(K)))
            return y + conv_b

        def rg_lru(x, ga_W, ga_b, gx_W, gx_b, a_param):
            r = jax.nn.sigmoid(x @ ga_W + ga_b)
            i = jax.nn.sigmoid(x @ gx_W + gx_b)
            log_a = -C_RGLRU * jax.nn.softplus(a_param) * r
            a = jnp.exp(log_a)
            mult = jnp.sqrt(-jnp.expm1(2.0 * log_a))
            b = mult * (i * x)

            def combine(c1, c2):
                a1, b1 = c1
                a2, b2 = c2
                return (a1 * a2, a2 * b1 + b2)
            _, h = jax.lax.associative_scan(combine, (a, b), axis=1)
            return h
        gelu = lambda t: jax.nn.gelu(t, approximate=False)
        xn = rmsnorm(x, norm1_w)
        left = gelu(xn @ left_W + left_b)
        right = rg_lru(causal_depthwise_conv(xn @ right_W + right_b, conv_w, conv_b), ga_W, ga_b, gx_W, gx_b, a_param)
        x1 = left * right @ out_W + out_b + x
        x1n = rmsnorm(x1, norm2_w)
        mlp = gelu(x1n @ up1_W + up1_b) * (x1n @ up2_W + up2_b) @ down_W + down_b
        return mlp + x1

    def _L1_ffn_ref(x, W_up, W_gate, W_down):
        import jax, jax.numpy as jnp
        import numpy as np
        D_MODEL = 256
        D_EXPERT = 1024
        EPS = 1e-08

        def ternary_quant(w):
            scale = jnp.mean(jnp.abs(w)) + EPS
            q = jnp.clip(jnp.round(w / scale), -1.0, 1.0) * scale
            return w + jax.lax.stop_gradient(q - w)
        wu = ternary_quant(W_up)
        wg = ternary_quant(W_gate)
        wd = ternary_quant(W_down)
        up = jnp.einsum('bsd,ed->bse', x, wu)
        gate = jnp.einsum('bsd,ed->bse', x, wg)
        hidden = jax.nn.silu(up) * gate
        return jnp.einsum('bse,de->bsd', hidden, wd)
    x = L0_attn_a_hidden_states
    x = x + _L0_attn_a_ref(_layernorm(x, axis=-1), L0_attn_a_Wq, L0_attn_a_Wk, L0_attn_a_Wv, L0_attn_a_Wo)
    x = x + _L0_ffn_ref(_layernorm(x, axis=-1), L0_ffn_w_router, L0_ffn_wq, L0_ffn_bq, L0_ffn_wk, L0_ffn_bk, L0_ffn_wv, L0_ffn_bv, L0_ffn_wo, L0_ffn_w_gate, L0_ffn_w_up, L0_ffn_w_down, L0_ffn_ln1_w, L0_ffn_ln2_w)
    x = x + _L0_attn_b_ref(_layernorm(x, axis=-1), L0_attn_b_W_Q, L0_attn_b_W_K, L0_attn_b_W_V, L0_attn_b_W_O, L0_attn_b_b_Q, L0_attn_b_b_K, L0_attn_b_b_V, L0_attn_b_b_O)
    x = x + _L0_ffn_ref(_layernorm(x, axis=-1), L0_ffn_w_router, L0_ffn_wq, L0_ffn_bq, L0_ffn_wk, L0_ffn_bk, L0_ffn_wv, L0_ffn_bv, L0_ffn_wo, L0_ffn_w_gate, L0_ffn_w_up, L0_ffn_w_down, L0_ffn_ln1_w, L0_ffn_ln2_w)
    x = x + _L1_attn_a_ref(_layernorm(x, axis=-1), L1_attn_a_W, L1_attn_a_b)
    x = x + _L1_ffn_ref(_layernorm(x, axis=-1), L1_ffn_W_up, L1_ffn_W_gate, L1_ffn_W_down)
    x = x + _L1_attn_b_ref(_layernorm(x, axis=-1), L1_attn_b_norm1_w, L1_attn_b_left_W, L1_attn_b_left_b, L1_attn_b_right_W, L1_attn_b_right_b, L1_attn_b_conv_w, L1_attn_b_conv_b, L1_attn_b_ga_W, L1_attn_b_ga_b, L1_attn_b_gx_W, L1_attn_b_gx_b, L1_attn_b_a_param, L1_attn_b_out_W, L1_attn_b_out_b, L1_attn_b_norm2_w, L1_attn_b_up1_W, L1_attn_b_up1_b, L1_attn_b_up2_W, L1_attn_b_up2_b, L1_attn_b_down_W, L1_attn_b_down_b)
    x = x + _L1_ffn_ref(_layernorm(x, axis=-1), L1_ffn_W_up, L1_ffn_W_gate, L1_ffn_W_down)
    return x

_drawn_inputs = setup_inputs


def setup_inputs(seed=0):
    import zlib

    import numpy as np

    out = dict(_drawn_inputs(seed))
    spreads = {'L0_attn_b_b_Q': (0.0, 0.468),
     'L0_attn_b_b_K': (0.0, 2.0),
     'L0_attn_b_b_V': (0.0, 0.1),
     'L0_attn_b_b_O': (0.0, 0.1),
     'L0_ffn_bq': (0.0, 0.8),
     'L0_ffn_bk': (0.0, 0.8),
     'L0_ffn_bv': (0.0, 0.433),
     'L0_ffn_ln1_w': (1.0, 0.6),
     'L0_ffn_ln2_w': (1.0, 0.6),
     'L1_attn_a_b': (0.0, 0.8),
     'L1_attn_b_norm1_w': (1.0, 0.6),
     'L1_attn_b_left_b': (0.0, 0.693),
     'L1_attn_b_right_b': (0.0, 0.582),
     'L1_attn_b_conv_b': (0.0, 0.628),
     'L1_attn_b_ga_b': (0.0, 2.0),
     'L1_attn_b_gx_b': (0.0, 2.0),
     'L1_attn_b_out_b': (0.0, 0.8),
     'L1_attn_b_norm2_w': (1.0, 0.6),
     'L1_attn_b_up1_b': (0.0, 1.77),
     'L1_attn_b_up2_b': (0.0, 1.839),
     'L1_attn_b_down_b': (0.0, 1.492)}
    factors = {'L0_attn_a_Wq': 8.0,
     'L0_attn_a_Wk': 8.0,
     'L0_ffn_wq': 8.0,
     'L0_ffn_wk': 8.0,
     'L0_ffn_wv': 3.36,
     'L0_ffn_w_gate': 8.0,
     'L0_ffn_w_up': 8.0,
     'L0_ffn_w_down': 8.0,
     'L1_attn_b_ga_W': 8.0,
     'L1_attn_b_a_param': 64.0,
     'L1_attn_b_gx_W': 2.744}
    for name, (base, spread) in spreads.items():
        noise = np.random.default_rng([zlib.crc32(name.encode()), seed]).standard_normal(out[name].shape)
        drawn = base * np.exp(spread * noise) if base else spread * noise
        out[name] = jnp.asarray(drawn.astype(out[name].dtype))
    for name, factor in factors.items():
        out[name] = (out[name] * factor).astype(out[name].dtype)
    return out
```

```python
import math
from contextlib import ExitStack, contextmanager

import numpy as np

import concourse.bass as bass
from concourse import mybir
from concourse.alu_op_type import AluOpType as ALU

F32 = mybir.dt.float32
F32R = mybir.dt.float32r
ACT = mybir.ActivationFunctionType
AX = mybir.AxisListType

P = 128
N = 1024
D = 256
KT = D // P
TT = N // P
HALF = 512
NH2 = N // HALF
MASKED = -1e30


class Count:

    def __init__(self, prog, sem, start=0):
        self.prog, self.sem, self.n = prog, sem, start
        self.per = 0
        prog.counts.append(self)

    def add(self, k):
        self.n += k
        return Token(self, self.n, self.prog.loop)


class Token:

    def __init__(self, count, value, loop):
        self.count, self.value, self.loop = count, value, loop

    def prev(self):
        return Token(self.count, self.value - self.count.per, self.loop)

    def last(self):
        return Token(self.count, self.value + (self.loop.turns - 1) * self.loop.per[self.count], None)


class Loop:
    def __init__(self, turns):
        self.turns, self.i, self.per = turns, None, {}


class Lane:

    def __init__(self, prog, eng, sem, gate=None):
        self.prog, self.e, self.gate = prog, eng, gate
        self.count = Count(prog, sem, START)
        self.seen = {}
        prog.lanes.append(self)
        eng.sem_inc(sem, START)

    def wait(self, *tokens):
        prog, gated = self.prog, False
        for t in tokens:
            if t is None:
                continue
            if isinstance(t, (list, tuple)):
                self.wait(*t)
                continue
            key = (t.count, t.loop)
            if self.seen.get(key, -1) >= t.value:
                continue
            self.seen[key] = t.value
            if prog.dry:
                continue
            if t.loop is None:
                self.e.wait_ge(t.count.sem, t.value)
            else:
                self.e.wait_ge(t.count.sem, prog.loop.i * prog.loop.per[t.count] + t.value)
                gated = self.gate is not None
        if gated:
            self.e.sem_inc(self.gate, 1)

    def do(self, instruction, *tokens, signal=True):
        self.wait(*tokens)
        if self.prog.dry:
            return self.count.add(1) if signal else None
        ins = instruction(self.e)
        if not signal:
            return None
        ins.then_inc(self.count.sem, 1)
        return self.count.add(1)

    def last(self):
        return Token(self.count, self.count.n, self.prog.loop)

    def dma(self, slot, out, in_, *tokens):
        self.wait(*tokens)
        if not self.prog.dry:
            self.e.dma_start(out(), in_()).then_inc(slot.sem, 16)
        return slot.add(16)


START = 1024


class Prog:
    def __init__(self, nc, ctx):
        self.nc, self.ctx = nc, ctx
        self.counts, self.lanes = [], []
        self.loop, self.dry = None, False
        self.bufs = ctx
        self.readers = {}
        sem = self.sem
        self.pe = Lane(self, nc.tensor, sem("pe_done"))
        self.dve = Lane(self, nc.vector, sem("dve_done"))
        self.act = Lane(self, nc.scalar, sem("act_done"))
        self.pool = Lane(self, nc.gpsimd, sem("pool_done"), gate=sem("pool_gate"))
        self.sp = Lane(self, nc.sync, sem("sp_done"))

    def sem(self, name):
        return self.ctx.enter_context(self.nc.semaphore(name))

    def slot(self, name):
        return Count(self, self.sem(name))

    def sb(self, name, shape, dt=F32):
        return self.bufs.enter_context(self.nc.sbuf_tensor(name, shape, dt))

    def fence(self):
        ends = [Token(c, c.n, self.loop) for c in self.counts if c is not self.sp.count and c.n]
        for lane in self.lanes:
            lane.wait(*ends)

    @contextmanager
    def phase(self):
        outer = self.bufs
        with ExitStack() as bufs:
            self.bufs = bufs
            yield
            self.fence()
        self.bufs = outer

    def run_loop(self, turns, body):
        self.fence()
        self.readers.clear()
        loop = Loop(turns)
        base = {c: c.n for c in self.counts}
        held = [dict(lane.seen) for lane in self.lanes]
        self.loop, self.dry = loop, True
        body(0)
        self.dry = False
        for c in self.counts:
            c.per = loop.per[c] = c.n - base[c]
            assert c.per <= START
            c.n = base[c]
        for lane, seen in zip(self.lanes, held):
            lane.seen = seen
        for name, tokens in self.readers.items():
            self.readers[name] = [t.prev() for t in tokens]
        with self.nc.Fori(0, turns) as i:
            loop.i = i
            body(i)
        for c in self.counts:
            assert c.n == base[c] + c.per
            c.n = base[c] + turns * c.per
        self.loop = None
        self.readers.clear()
        self.fence()


def fr(ap):
    return ap.bitcast(F32)


class Env:
    pass


def setup(g, ins, x_tok):
    pr, pool, dve, sp = g.pr, g.pr.pool, g.pr.dve, g.pr.sp
    g.x = pr.sb("x", [P, KT, N])
    g.x_slot = pr.slot("x_loaded")
    g.x_ready = [sp.dma(g.x_slot, lambda: g.x[:], lambda: ins["x"].rearrange("(k p) n -> p k n", p=P))]
    g.ident = pr.sb("ident", [P, P])
    g.ident_r = pr.sb("ident_r", [P, P], F32R)
    g.mask = pr.sb("mask", [P, P])
    g.mask_r = pr.sb("mask_r", [P, P], F32R)
    g.avg = pr.sb("avg", [P, P])
    g.eps = pr.sb("eps", [P, 3])
    g.EPS = {1e-5: 0, 1e-6: 1, 1e-8: 2}
    z = pool.do(lambda e: e.memset(g.ident[:], 0.0))
    z2 = pool.do(lambda e: e.memset(g.mask[:], 0.0))
    t1 = pool.do(lambda e: e.affine_select(out=g.ident[:], in_=g.ident[:], compare_op=ALU.not_equal, fill=1.0,
                                           base=0, pattern=[[-1, P]], channel_multiplier=1), z)
    t2 = pool.do(lambda e: e.affine_select(out=g.mask[:], in_=g.mask[:], compare_op=ALU.is_ge, fill=MASKED,
                                           base=0, pattern=[[-1, P]], channel_multiplier=1), z2)
    dve.do(lambda e: e.memset(g.avg[:], 1.0 / D))
    for eps, c in g.EPS.items():
        dve.do(lambda e, c=c, eps=eps: e.memset(g.eps[:, c:c + 1], eps))
    dve.do(lambda e: e.tensor_copy(g.ident_r[:], g.ident[:]), t1)
    dve.do(lambda e: e.tensor_copy(g.mask_r[:], g.mask[:]), t2)
    pr.fence()


def norm_scratch(pr, name, cols):
    w = min(cols, HALF)
    return pr.sb(name + "_sq", [P, cols // w, KT, w]), pr.sb(name + "_inv", [P, cols // w, w])


def normalise(g, name, src, dst, cols, eps, src_ready=(), dst_free=(), centre=False, weight=None, split=None,
              scratch=None):
    pr, pe, dve, act = g.pr, g.pr.pe, g.pr.dve, g.pr.act
    w = min(cols, HALF)
    done = []
    sq, inv = scratch or norm_scratch(pr, name, cols)
    steps = []
    for b in range(cols // w):
        c = slice(b * w, b * w + w)
        ps_mean, ps_var = g.bank[2 * b][:, 0:w], g.bank[2 * b + 1][:, 0:w]
        base, ready = src, list(src_ready)
        if centre:
            for k in range(KT):
                t = pe.do(lambda e: e.matmul(ps_mean, g.avg[:], src[:, k, c], start=(k == 0), stop=(k == KT - 1)),
                          ready, signal=(k == KT - 1))
            t = dve.do(lambda e: e.tensor_tensor(dst[:, :, c], src[:, :, c],
                                                 ps_mean.unsqueeze(1).broadcast_to([P, KT, w]), ALU.subtract),
                       t, list(dst_free))
            base, ready = dst, [t]
        t = act.do(lambda e: e.activation(sq[:, b], base[:, :, c], ACT.Square), ready)
        for k in range(KT):
            t = pe.do(lambda e: e.matmul(ps_var, g.avg[:], sq[:, b, k], start=(k == 0), stop=(k == KT - 1)),
                      t, signal=(k == KT - 1))
        steps.append((b, c, ps_var, base, ready, t))
    for b, c, ps_var, base, ready, t in steps:
        k0 = g.EPS[eps]
        t = act.do(lambda e: e.activation(inv[:, b], ps_var, ACT.Sqrt, bias=g.eps[:, k0:k0 + 1]), t)
        t = dve.do(lambda e: e.reciprocal(inv[:, b], inv[:, b]), t)
        if weight is None:
            t = dve.do(lambda e: e.tensor_tensor(dst[:, :, c], base[:, :, c],
                                                 inv[:, b].unsqueeze(1).broadcast_to([P, KT, w]), ALU.mult),
                       t, ready, list(dst_free))
        else:
            for k in range(KT):
                t2 = dve.do(lambda e: e.scalar_tensor_tensor(dst[:, k, c], base[:, k, c], weight[:, k:k + 1],
                                                             inv[:, b], ALU.mult, ALU.mult),
                            t, ready, list(dst_free))
            t = t2
        out = [t]
        if split:
            hi, lo = split
            th = act.do(lambda e: e.activation(hi[:, :, c], dst[:, :, c], ACT.Copy), t)
            tl = dve.do(lambda e: e.tensor_tensor(lo[:, :, c], dst[:, :, c], fr(hi[:, :, c]), ALU.subtract), th)
            out += [th, tl]
        done.append(out)
    return done


def matmul3(lane, out, pairs, *tokens, start=True, stop=True, signal=True):
    passes = []
    for lh, ll, rh, rl in pairs:
        passes.append((lh, rh))
        if ll is not None:
            passes.append((ll, rh))
        if rl is not None:
            passes.append((lh, rl))
    for n, (a, b) in enumerate(passes):
        last = n == len(passes) - 1
        t = lane.do(lambda e: e.matmul(out, a, b, start=start and n == 0, stop=stop and last, skip_group_check=True),
                    *(tokens if n == 0 else ()), signal=signal and last)
    return t


class Softmax:

    def __init__(self, g, heads, score_passes, value_passes, take_output, ready):
        self.g, self.heads = g, heads
        self.score_passes, self.value_passes = score_passes, value_passes
        self.take_output, self.ready = take_output, ready
        self.units = [(h, i) for h in range(heads) for i in range(TT)]
        self.st = {}

    def scores(self, u):
        g, pe, dve, act, pool = self.g, self.g.pr.pe, self.g.pr.dve, self.g.pr.act, self.g.pr.pool
        rd = g.pr.readers
        h, i = self.units[u]
        bank, slot = 2 * (u % 2), u % NPROB
        width = (i + 1) * P
        key = f"scores{u % 2}"
        first = True
        for c in range(0, width, HALF):
            n = min(HALF, width - c)
            out = g.ps[:, bank + c // HALF, 0:n]
            t = matmul3(pe, out, self.score_passes(h, i, slice(c, c + n)),
                        self.ready, rd.get(key) if first else None, stop=(c + n != width),
                        signal=(c + n != width))
            first = False
        t = pe.do(lambda e: e.matmul(g.ps[:, bank + (width - P) // HALF, (width - P) % HALF:(width - P) % HALF + P],
                                     g.ident_r[:], g.mask_r[:], start=False, stop=True, skip_group_check=True))
        s = self.flat(bank, width)
        neg = g.negmax[:, slot:slot + 1]
        prob = g.prob[:, slot, 0:width]
        tm = [dve.do(lambda e: e.tensor_reduce(neg, s, AX.X if width <= HALF else AX.X, ALU.max, negate=True),
                     t, rd.get(f"prob{slot}"))]
        te = act.do(lambda e: e.activation(prob, s, ACT.Exp, bias=neg, accum_out=g.rowsum[:, slot:slot + 1]),
                    tm, rd.get(f"prob{slot}"))
        rd[key] = [te]
        ti = dve.do(lambda e: e.reciprocal(g.rowinv[:, slot:slot + 1], g.rowsum[:, slot:slot + 1]), te)
        tp = pool.do(lambda e: e.tensor_scalar(prob, prob, g.rowinv[:, slot:slot + 1], 1.0,
                                                  ALU.mult, ALU.mult), ti)
        self.st[u] = tp

    def flat(self, bank, width):
        return self.g.ps_flat[:, bank * HALF:bank * HALF + width]

    def transposes(self, u):
        g, pe, dve, act = self.g, self.g.pr.pe, self.g.pr.dve, self.g.pr.act
        rd = g.pr.readers
        h, i = self.units[u]
        slot, qb = u % NPROB, i // 4
        cols = slice(i % 4 * P, i % 4 * P + P)
        used = []
        for j0 in range(0, i + 1, 4):
            n = min(4, i + 1 - j0)
            b = 4 + self.g.turn % 2
            self.g.turn += 1
            out = g.ps[:, b, :]
            for j in range(n):
                t = pe.do(lambda e: e.transpose(out[:, j * P:j * P + P],
                                                g.prob[:, slot, (j0 + j) * P:(j0 + j + 1) * P], g.ident[:]),
                          self.st[u], rd.get(f"bank{b}"), signal=(j == n - 1))
            used.append(t)
            src = out[:, 0:n * P].rearrange("p (j q) -> p j q", j=n)
            hi, lo = g.pT_hi[qb][:, j0:j0 + n, cols], g.pT_lo[qb][:, j0:j0 + n, cols]
            th = act.do(lambda e: e.activation(hi, src, ACT.Copy), t, rd.get(f"pT{qb}"))
            tl = dve.do(lambda e: e.tensor_tensor(lo, src, fr(hi), ALU.subtract), th, rd.get(f"pT{qb}"))
            rd[f"bank{b}"] = [th, tl]
            self.st.setdefault(("pT", h, qb), []).extend([th, tl])
        rd[f"prob{slot}"] = used

    def values(self, h, qb):
        g, pe = self.g, self.g.pr.pe
        rd = g.pr.readers
        out = g.ps[:, 6, :]
        tiles = 4 * qb + 4
        tokens = [self.st[("pT", h, qb)], rd.get("bank6"), self.ready]
        for j in range(tiles):
            q = max(0, j - 4 * qb) * P
            hi, lo = g.pT_hi[qb][:, j, q:HALF], g.pT_lo[qb][:, j, q:HALF]
            passes = self.value_passes(h, j, hi, lo)
            for n, (a, b) in enumerate(passes):
                end = j == tiles - 1 and n == len(passes) - 1
                t = pe.do(lambda e: e.matmul(out[:, q:HALF], a, b, start=(j == 0 and n == 0), stop=end,
                                             skip_group_check=True), *tokens, signal=end)
                tokens = []
        rd[f"pT{qb}"] = [t]
        rd["bank6"] = self.take_output(h, qb, out, t)

    def run(self):
        n, due = len(self.units), []
        for s in range(n + LAG + 1):
            if s < n:
                self.scores(s)
            if 0 <= s - LAG < n:
                self.transposes(s - LAG)
            if due:
                self.values(*due.pop(0))
            if 0 <= s - LAG < n:
                h, i = self.units[s - LAG]
                if i % 4 == 3:
                    due.append((h, i // 4))
        for d in due:
            self.values(*d)


NPROB = 4
LAG = 2


def softmax_buffers(g, tag):
    pr = g.pr
    g.prob = pr.sb(tag + "prob", [P, NPROB, N])
    g.negmax = pr.sb(tag + "negmax", [P, NPROB])
    g.rowsum = pr.sb(tag + "rowsum", [P, NPROB])
    g.rowinv = pr.sb(tag + "rowinv", [P, NPROB])
    g.pT_hi = [pr.sb(f"{tag}pT_hi{qb}", [P, 4 * qb + 4, HALF], F32R) for qb in range(NH2)]
    g.pT_lo = [pr.sb(f"{tag}pT_lo{qb}", [P, 4 * qb + 4, HALF], F32R) for qb in range(NH2)]
    g.turn = 0


A_HEADS, A_KV, A_HD = 32, 8, 64
A_GRP = A_HEADS // A_KV
A_W = (A_GRP + 2) * A_HD


def attn_a(g, ins):
    pr = g.pr
    pe, dve, act, pool, sp, rd = pr.pe, pr.dve, pr.act, pr.pool, pr.sp, pr.readers
    with pr.phase():
        h = pr.sb("a_h", [P, KT, N])
        h_hi, h_lo = pr.sb("a_h_hi", [P, KT, N], F32R), pr.sb("a_h_lo", [P, KT, N], F32R)
        cos, sin = pr.sb("a_cos", [P, TT, A_HD]), pr.sb("a_sin", [P, TT, A_HD])
        w_raw = pr.sb("a_w_raw", [P, KT, A_W])
        w_hi, w_lo = pr.sb("a_w_hi", [P, KT, A_W], F32R), pr.sb("a_w_lo", [P, KT, A_W], F32R)
        o_raw = pr.sb("a_o_raw", [P, 2, D])
        o_hi, o_lo = pr.sb("a_o_hi", [P, 2, D], F32R), pr.sb("a_o_lo", [P, 2, D], F32R)
        t1 = pr.sb("a_t1", [P, 2, (A_GRP + 1) * A_HD])
        t2 = pr.sb("a_t2", [P, 2, (A_GRP + 1) * A_HD])
        qk = h[:, :, :].rearrange("p k n -> p (k n)")
        q_st = pr.sb("a_q", [P, A_GRP, N], F32R)
        k_hi, k_lo = pr.sb("a_k_hi", [P, N], F32R), pr.sb("a_k_lo", [P, N], F32R)
        v_st = pr.sb("a_v", [P, TT, 2 * A_HD], F32R)
        o_low = pr.sb("a_o_low", [P, HALF])
        o_sum = pr.sb("a_o_sum", [P, 2, HALF])
        oT_hi, oT_lo = pr.sb("a_oT_hi", [P, 2, N], F32R), pr.sb("a_oT_lo", [P, 2, N], F32R)
        qk_sb = pr.sb("a_qk", [P, TT, A_W])
        softmax_buffers(g, "a_")
        s_tab, s_w, s_o = pr.slot("a_tables"), pr.slot("a_w_loaded"), pr.slot("a_o_loaded")

        tab = sp.dma(s_tab, lambda: cos[:], lambda: ins["a_cos"])
        tab = sp.dma(s_tab, lambda: sin[:], lambda: ins["a_sin"])
        normalise(g, "a_n", g.x, h, N, 1e-5, src_ready=g.x_ready, centre=True, split=(h_hi, h_lo))
        for lane in (dve,):
            lane.wait(tab)

        def split_w(i, *tokens):
            a = pool.do(lambda e: e.tensor_copy(w_hi[:], w_raw[:]), *tokens)
            b = pool.do(lambda e: e.tensor_tensor(w_lo[:], w_raw[:], fr(w_hi[:]), ALU.subtract), a)
            return b

        first = sp.dma(s_w, lambda: w_raw[:], lambda: ins["a_w"][0])
        w_first = split_w(0, first)
        sp.dma(s_w, lambda: w_raw[:], lambda: ins["a_w"][1], w_first)
        sp.dma(s_o, lambda: o_raw[:], lambda: ins["a_o"][0])
        heads = A_GRP + 1
        rows = (slice(0, 64), slice(64, 128))

        def group(i):
            g.turn = 0
            o_loaded = Token(s_o, s_o.n, pr.loop)
            ta = pool.do(lambda e: e.tensor_copy(o_hi[:], o_raw[:]), o_loaded, rd.get("a_o"))
            o_split = pool.do(lambda e: e.tensor_tensor(o_lo[:], o_raw[:], fr(o_hi[:]), ALU.subtract), ta)
            sp.dma(s_o, lambda: o_raw[:], lambda: ins["a_o"][bass.ds((i + 1) % A_KV, 1)].rearrange("o p a b -> (o p) a b"), o_split)

            v_ready, qk_ready = [], []
            for t in range(TT):
                b, par = t % 4, t % 2
                out = g.ps[:, b, 0:A_W]
                tok = slice(t * P, t * P + P)
                tp = matmul3(pe, out, [(h_hi[:, k, tok], h_lo[:, k, tok], w_hi[:, k], w_lo[:, k]) for k in range(KT)],
                             rd.get("w_split"), rd.get(f"scores{b // 2}"), rd.get(f"proj{b}"))
                x3 = out[:, 0:heads * A_HD].rearrange("p (h d) -> p h d", d=A_HD)
                c3 = cos[:, t].unsqueeze(1).broadcast_to([P, heads, A_HD])
                s3 = sin[:, t].unsqueeze(1)
                r1 = t1[:, par].rearrange("p (h d) -> p h d", d=A_HD)
                r2 = t2[:, par].rearrange("p (h d) -> p h d", d=A_HD)
                HH = A_HD // 2
                vs = out[:, heads * A_HD:A_W]
                vh = act.do(lambda e: e.activation(v_st[:, t, 0:A_HD], vs, ACT.Copy), tp, rd.get("v"))
                a1 = dve.do(lambda e: e.tensor_tensor(r1, x3, c3, ALU.mult), vh, rd.get(f"rope{par}"))
                a2 = dve.do(lambda e: e.tensor_tensor(r2[:, :, 0:HH], x3[:, :, HH:], s3[:, :, 0:HH].broadcast_to([P, heads, HH]),
                                                      ALU.mult))
                a3 = dve.do(lambda e: e.tensor_tensor(r2[:, :, HH:], x3[:, :, 0:HH], s3[:, :, HH:].broadcast_to([P, heads, HH]),
                                                      ALU.mult))
                a4 = pool.do(lambda e: e.tensor_tensor(qk_sb[:, t, 0:heads * A_HD], t1[:, par], t2[:, par], ALU.add),
                             a1, a3, rd.get("qk"))
                a4 = pool.do(lambda e: e.tensor_tensor(qk_sb[:, t, heads * A_HD:], t1[:, par, A_GRP * A_HD:],
                                                       t2[:, par, A_GRP * A_HD:], ALU.add))
                rd[f"rope{par}"] = [a4]
                qk_ready.append(a4)
                vl = dve.do(lambda e: e.tensor_tensor(v_st[:, t, A_HD:], vs, fr(v_st[:, t, 0:A_HD]), ALU.subtract), vh)
                rd[f"proj{b}"] = [vl, vh]
                v_ready = [vh, vl]
            w_loaded = Token(s_w, s_w.n, pr.loop)
            rd["w_split"] = [split_w(i, w_loaded, tp)]
            sp.dma(s_w, lambda: w_raw[:], lambda: ins["a_w"][bass.ds((i + 2) % A_KV, 1)].rearrange("o p a b -> (o p) a b"), rd["w_split"])

            ready = list(v_ready)
            for c in range(NH2):
                for pair in range(3):
                    b = (4, 5, 7)[pair]
                    out = g.ps[:, b, :]
                    for t in range(4):
                        tt = c * 4 + t
                        tp = pe.do(lambda e: e.transpose(out[:, t * P:t * P + P], qk_sb[:, tt, pair * P:pair * P + P],
                                                         g.ident[:]),
                                   qk_ready[tt], rd.get(f"bank{b}"), rd.get("attn"), signal=(t == 3))
                    cc = slice(c * HALF, c * HALF + HALF)
                    used = []
                    if pair < 2:
                        for e2 in range(2):
                            hd, mine, other = 2 * pair + e2, rows[e2], rows[1 - e2]
                            hi = act.do(lambda e: e.activation(q_st[mine, hd, cc], out[mine], ACT.Copy, scale=A_HD ** -0.5),
                                        tp, rd.get("attn"))
                            lo = dve.do(lambda e: e.scalar_tensor_tensor(q_st[other, hd, cc], out[mine], A_HD ** -0.5,
                                                                         fr(q_st[mine, hd, cc]), ALU.mult, ALU.subtract), hi)
                            used += [hi, lo]
                    else:
                        hi = act.do(lambda e: e.activation(k_hi[:, cc], out, ACT.Copy), tp, rd.get("attn"))
                        lo = dve.do(lambda e: e.tensor_tensor(k_lo[:, cc], out, fr(k_hi[:, cc]), ALU.subtract), hi,
                                    rd.get("attn"))
                        used += [hi, lo]
                    rd[f"bank{b}"] = used
                    ready += used
            rd["qk"] = [tp]
            for b in range(2):
                rd[f"scores{b}"] = rd[f"proj{2 * b}"] + rd[f"proj{2 * b + 1}"]

            out_ready = []

            def score_passes(hd, t, keys):
                q = q_st[:, hd, t * P:t * P + P]
                return [(q, None, k_hi[:, keys], None), (q, None, k_lo[:, keys], None)]

            def value_passes(hd, j, hi, lo):
                return [(v_st[:, j], hi), (v_st[:, j], lo)]

            def take_output(hd, qb, out, t):
                pair, half = hd // 2, rows[hd % 2]
                cc = slice(qb * HALF, qb * HALF + HALF)
                a = act.do(lambda e: e.activation(o_low[64:128], out[64:128], ACT.Copy), t, rd.get("o_low"))
                b = dve.do(lambda e: e.tensor_tensor(o_sum[half, qb], out[0:64], o_low[64:128], ALU.add), a, rd.get(f"o_sum{qb}"))
                rd["o_low"] = [b]
                if hd % 2 == 1:
                    c = pool.do(lambda e: e.tensor_copy(oT_hi[:, pair, cc], o_sum[:, qb]), b, rd.get("oT"))
                    d = pool.do(lambda e: e.tensor_tensor(oT_lo[:, pair, cc], o_sum[:, qb], fr(oT_hi[:, pair, cc]),
                                                          ALU.subtract), c)
                    rd[f"o_sum{qb}"] = [d]
                    out_ready.append(d)
                return [b]

            sm = Softmax(g, A_GRP, score_passes, value_passes, take_output, ready)
            sm.run()
            rd["attn"] = [pe.last()] if not pr.dry or True else None
            rd["v"] = rd["attn"]
            for m in range(KT):
                for qb in range(NH2):
                    b = 2 * m + qb
                    cc = slice(qb * HALF, qb * HALF + HALF)
                    tp = matmul3(pe, g.ps[:, b, :],
                                 [(o_hi[:, pr2, m * P:m * P + P], o_lo[:, pr2, m * P:m * P + P],
                                   oT_hi[:, pr2, cc], oT_lo[:, pr2, cc]) for pr2 in range(2)],
                                 o_split, out_ready, rd.get(f"scores{m}"))
                    tx = dve.do(lambda e: e.tensor_tensor(g.x[:, m, cc], g.x[:, m, cc], g.ps[:, b, :], ALU.add), tp, rd.get("x"))
                    rd[f"proj{b}"] = [tx]
            rd["x"] = [tx]
            rd["oT"] = [tp]
            rd["a_o"] = [tp]

        pr.run_loop(A_KV, group)


B_HEADS, B_HD = 16, 128
B_GRP = 2
B_C = B_GRP * B_HD
B_SCALE = 1.0 / math.sqrt(B_HD)


def attn_b(g, ins):
    pr = g.pr
    pe, dve, act, pool, sp, rd = pr.pe, pr.dve, pr.act, pr.pool, pr.sp, pr.readers
    turns = B_HEADS // B_GRP
    with pr.phase():
        h = pr.sb("b_h", [P, KT, N])
        h_hi, h_lo = pr.sb("b_h_hi", [P, KT, N], F32R), pr.sb("b_h_lo", [P, KT, N], F32R)
        w_raw = pr.sb("b_w_raw", [P, KT, 3 * B_C])
        w_hi, w_lo = pr.sb("b_w_hi", [P, KT, 3 * B_C], F32R), pr.sb("b_w_lo", [P, KT, 3 * B_C], F32R)
        bias = pr.sb("b_bias", [P, turns, 3, B_GRP])
        bias_now = pr.sb("b_bias_now", [P, 3, B_GRP])
        b_out = pr.sb("b_bias_out", [P, KT])
        o_raw = pr.sb("b_o_raw", [P, B_GRP, D])
        o_hi, o_lo = pr.sb("b_o_hi", [P, B_GRP, D], F32R), pr.sb("b_o_lo", [P, B_GRP, D], F32R)
        q_hi, q_lo = pr.sb("b_q_hi", [P, B_GRP, N], F32R), pr.sb("b_q_lo", [P, B_GRP, N], F32R)
        k_hi, k_lo = pr.sb("b_k_hi", [P, B_GRP, N], F32R), pr.sb("b_k_lo", [P, B_GRP, N], F32R)
        v_hi, v_lo = pr.sb("b_v_hi", [P, TT, B_C], F32R), pr.sb("b_v_lo", [P, TT, B_C], F32R)
        oT_hi, oT_lo = pr.sb("b_oT_hi", [P, B_GRP, N], F32R), pr.sb("b_oT_lo", [P, B_GRP, N], F32R)
        softmax_buffers(g, "b_")
        s_b, s_w, s_o = pr.slot("b_bias_loaded"), pr.slot("b_w_loaded"), pr.slot("b_o_loaded")
        sp.dma(s_b, lambda: bias[:], lambda: ins["b_bias"])
        biases = sp.dma(s_b, lambda: b_out[:], lambda: ins["b_bias_out"])
        first = sp.dma(s_w, lambda: w_raw[:], lambda: ins["b_w"][0])
        sp.dma(s_o, lambda: o_raw[:], lambda: ins["b_o"][0])

        normalise(g, "b_n", g.x, h, N, 1e-5, src_ready=g.x_ready, centre=True, split=(h_hi, h_lo))
        act.wait(biases)
        for k in range(KT):
            dve.do(lambda e: e.tensor_scalar(g.x[:, k], g.x[:, k], b_out[:, k:k + 1], None, ALU.add), biases, dve.last())

        def split_w(*tokens):
            q = w_raw[:, :, 0:B_C]
            a = pool.do(lambda e: e.tensor_scalar(q, q, B_SCALE, 1.0, ALU.mult, ALU.mult), *tokens)
            a = pool.do(lambda e: e.tensor_copy(w_hi[:], w_raw[:]), a)
            return pool.do(lambda e: e.tensor_tensor(w_lo[:], w_raw[:], fr(w_hi[:]), ALU.subtract), a)

        w_first = split_w(first)
        sp.dma(s_w, lambda: w_raw[:], lambda: ins["b_w"][1], w_first)

        def group(i):
            g.turn = 0
            o_loaded = Token(s_o, s_o.n, pr.loop)
            ta = pool.do(lambda e: e.tensor_copy(o_hi[:], o_raw[:]), o_loaded, rd.get("o_w"))
            o_split = pool.do(lambda e: e.tensor_tensor(o_lo[:], o_raw[:], fr(o_hi[:]), ALU.subtract), ta)
            sp.dma(s_o, lambda: o_raw[:],
                   lambda: ins["b_o"][bass.ds((i + 1) % turns, 1)].rearrange("o p a b -> (o p) a b"), o_split)
            tb = act.do(lambda e: e.activation(bias_now[:], bias[:, bass.ds(i, 1)].rearrange("p o a b -> p (o a) b"), ACT.Copy),
                        rd.get("bias"))
            tb = act.do(lambda e: e.activation(bias_now[:, 0], bias_now[:, 0], ACT.Copy, scale=B_SCALE), tb)

            ready, n = [], 0
            for which, hi_t, lo_t in ((0, q_hi, q_lo), (1, k_hi, k_lo)):
                for e2 in range(B_GRP):
                    for c in range(NH2):
                        b = n % 4
                        n += 1
                        cc = slice(c * HALF, c * HALF + HALF)
                        col = slice(which * B_C + e2 * B_HD, which * B_C + (e2 + 1) * B_HD)
                        out = g.ps[:, b, :]
                        tp = matmul3(pe, out, [(w_hi[:, k, col], w_lo[:, k, col], h_hi[:, k, cc], h_lo[:, k, cc])
                                               for k in range(KT)],
                                     rd.get("w_split"), rd.get(f"scores{b // 2}"), rd.get(f"proj{b}"))
                        bb = bias_now[:, which, e2:e2 + 1]
                        hi = act.do(lambda e: e.activation(hi_t[:, e2, cc], out, ACT.Identity, bias=bb), tp, tb, rd.get("attn"))
                        lo = dve.do(lambda e: e.scalar_tensor_tensor(lo_t[:, e2, cc], out, bb, fr(hi_t[:, e2, cc]),
                                                                     ALU.add, ALU.subtract), hi, rd.get("attn"))
                        rd[f"proj{b}"] = [lo]
                        ready += [hi, lo]
            for t in range(TT):
                b = n % 4
                n += 1
                out = g.ps[:, b, 0:B_C]
                tok = slice(t * P, t * P + P)
                tp = matmul3(pe, out, [(h_hi[:, k, tok], h_lo[:, k, tok], w_hi[:, k, 2 * B_C:], w_lo[:, k, 2 * B_C:])
                                       for k in range(KT)], rd.get(f"proj{b}"))
                hi = act.do(lambda e: e.activation(v_hi[:, t], out, ACT.Copy), tp, rd.get("attn"))
                lo = dve.do(lambda e: e.tensor_tensor(v_lo[:, t], out, fr(v_hi[:, t]), ALU.subtract), hi, rd.get("attn"))
                rd[f"proj{b}"] = [lo]
                ready = ready[-8:] + [hi, lo]
            w_loaded = Token(s_w, s_w.n, pr.loop)
            rd["w_split"] = [split_w(w_loaded, tp)]
            sp.dma(s_w, lambda: w_raw[:],
                   lambda: ins["b_w"][bass.ds((i + 2) % turns, 1)].rearrange("o p a b -> (o p) a b"), rd["w_split"])
            for b in range(2):
                rd[f"scores{b}"] = rd[f"proj{2 * b}"] + rd[f"proj{2 * b + 1}"]
            out_ready = []

            def score_passes(hd, t, keys):
                tok = slice(t * P, t * P + P)
                return [(q_hi[:, hd, tok], q_lo[:, hd, tok], k_hi[:, hd, keys], k_lo[:, hd, keys])]

            def value_passes(hd, j, hi, lo):
                vh, vl = v_hi[:, j, hd * B_HD:(hd + 1) * B_HD], v_lo[:, j, hd * B_HD:(hd + 1) * B_HD]
                return [(vh, hi), (vh, lo), (vl, hi)]

            def take_output(hd, qb, out, t):
                cc = slice(qb * HALF, qb * HALF + HALF)
                bb = bias_now[:, 2, hd:hd + 1]
                a = act.do(lambda e: e.activation(oT_hi[:, hd, cc], out, ACT.Identity, bias=bb), t, rd.get("oT"))
                b = dve.do(lambda e: e.scalar_tensor_tensor(oT_lo[:, hd, cc], out, bb, fr(oT_hi[:, hd, cc]),
                                                            ALU.add, ALU.subtract), a, rd.get("oT"))
                out_ready.extend([a, b])
                return [b]

            Softmax(g, B_GRP, score_passes, value_passes, take_output, ready).run()
            rd["bias"] = [dve.last()]
            rd["attn"] = [pe.last()]
            for m in range(KT):
                for qb in range(NH2):
                    b = 2 * m + qb
                    cc = slice(qb * HALF, qb * HALF + HALF)
                    mm = slice(m * P, m * P + P)
                    tp = matmul3(pe, g.ps[:, b, :], [(o_hi[:, e2, mm], o_lo[:, e2, mm], oT_hi[:, e2, cc], oT_lo[:, e2, cc])
                                                     for e2 in range(B_GRP)],
                                 o_split, out_ready, rd.get(f"scores{m}"))
                    tx = dve.do(lambda e: e.tensor_tensor(g.x[:, m, cc], g.x[:, m, cc], g.ps[:, b, :], ALU.add), tp, rd.get("x"))
                    rd[f"proj{b}"] = [tx]
            rd["x"] = [tx]
            rd["oT"] = [tp]
            rd["o_w"] = [tp]

        pr.run_loop(turns, group)


F_HEADS, F_KV, F_HD, F_I = 16, 8, 128, 1024
F_S = int(N * 0.125)
F_SCALE = 1.0 / math.sqrt(F_HD)
FI_T = F_I // P


def ffn(g, ins, tag):
    assert F_S == P
    pr = g.pr
    pe, dve, act, pool, sp = pr.pe, pr.dve, pr.act, pr.pool, pr.sp
    ps = g.ps
    with pr.phase():
        def sb(name, shape, dt=F32):
            return pr.sb(f"{tag}_{name}", shape, dt)

        def load(name, shape):
            buf, slot = sb(name, shape), pr.slot(f"{tag}_{name}_loaded")
            return buf, sp.dma(slot, lambda: buf[:], lambda: ins["f_" + name])

        wr, l_wr = load("wr", [P, KT])
        trope, l_trope = load("rope", [P, TT, 2, P])
        ln, l_ln = load("ln", [P, 2, KT])
        bqk, l_bqk = load("bqk", [P, F_HEADS + F_KV])
        bv, l_bv = load("bv", [1, F_KV * F_HD])
        wq, l_wq = load("wq", [P, KT, F_HEADS * F_HD])
        wk, l_wk = load("wk", [P, KT, F_KV * F_HD])
        wv, l_wv = load("wv", [P, KT, F_KV * F_HD])
        wo, l_wo = load("wo", [P, F_HEADS, D])
        wg, l_wg = load("wg", [P, KT, F_I])
        wu, l_wu = load("wu", [P, KT, F_I])
        wd, l_wd = load("wd", [P, FI_T, D])

        tri, upper, ramp, ones = sb("tri", [P, P]), sb("upper", [P, P]), sb("ramp", [P, P]), sb("ones", [P, P])
        c0 = pool.do(lambda e: e.memset(tri[:], 1.0))
        c1 = pool.do(lambda e: e.memset(upper[:], 1.0))
        tri_t = pool.do(lambda e: e.affine_select(out=tri[:], in_=tri[:], compare_op=ALU.is_ge, fill=0.0, base=-1,
                                                  pattern=[[-1, P]], channel_multiplier=1), c0)
        upper_t = pool.do(lambda e: e.affine_select(out=upper[:], in_=upper[:], compare_op=ALU.is_ge, fill=0.0, base=-1,
                                                    pattern=[[1, P]], channel_multiplier=-1), c1)
        ramp_t = pool.do(lambda e: e.iota(ramp[:], pattern=[[1, P]], base=0, channel_multiplier=0,
                                          allow_small_or_imprecise_dtypes=True))
        ones_t = pool.do(lambda e: e.memset(ones[:], 1.0))

        h = sb("h", [P, KT, N])
        hn = normalise(g, f"{tag}_n0", g.x, h, N, 1e-5, centre=True)
        h_ready = [o[0] for o in hn]
        x_plus = pool.do(lambda e: e.tensor_tensor(g.x[:], g.x[:], h[:], ALU.add), h_ready)

        wrb = sb("wrb", [P, KT, P])
        t = dve.do(lambda e: e.tensor_copy(wrb[:], wr[:, :].unsqueeze(2).broadcast_to([P, KT, P])), l_wr)
        for c in range(NH2):
            for k in range(KT):
                s_mm = pe.do(lambda e: e.matmul(ps[:, 4 + c, :], wrb[:, k], h[:, k, c * HALF:(c + 1) * HALF],
                                                start=(k == 0), stop=(k == KT - 1)), t, h_ready)
        s = sb("s", [P, N])
        s_t = dve.do(lambda e: e.tensor_copy(s[:], g.ps_flat[:, 4 * HALF:6 * HALF]), s_mm)
        h_tok = sb("h_tok", [P, TT, D])
        h_tok_t = []
        for b in range(4):
            for j in range(4):
                c, k = 2 * b + j // 2, j % 2
                t = pe.do(lambda e: e.transpose(ps[:, b, j * P:j * P + P], h[:, k, c * P:c * P + P], g.ident[:]), h_ready)
            h_tok_t.append(act.do(lambda e: e.activation(h_tok[:, 2 * b:2 * b + 2].rearrange("p a b -> p (a b)"), ps[:, b, :],
                                                         ACT.Copy), t))
        diag, s_col = sb("diag", [P, TT, P]), sb("s_col", [P, TT])
        t = dve.do(lambda e: e.tensor_tensor(diag[:], s[:, :].rearrange("p (c q) -> p c q", q=P),
                                             g.ident[:].unsqueeze(1).broadcast_to([P, TT, P]), ALU.mult), s_t)
        t = dve.do(lambda e: e.tensor_reduce(s_col[:], diag[:], AX.X, ALU.add), t)
        junk, cnt = diag[:, :, :].rearrange("p c q -> p (c q)"), sb("cnt", [P, TT, 4])
        z = dve.do(lambda e: e.memset(cnt[:], 0.0))
        for c in range(TT):
            own, lo, up = s_col[:, c:c + 1], c * P, N - c * P
            if c:
                t = dve.do(lambda e: e.tensor_scalar(junk[:, 0:lo], s[:, 0:lo], own, None, ALU.is_ge, ALU.add,
                                                     accum_out=cnt[:, c, 0:1]), t, z)
            t = dve.do(lambda e: e.tensor_scalar(junk[:, lo:N], s[:, lo:N], own, None, ALU.is_gt, ALU.add,
                                                 accum_out=cnt[:, c, 1:2]), t, z)
            t = dve.do(lambda e: e.scalar_tensor_tensor(junk[:, lo:lo + P], s[:, lo:lo + P], own, tri[:],
                                                        ALU.is_equal, ALU.mult, accum_out=cnt[:, c, 2:3]), t, tri_t)
        rank, sel = sb("rank", [P, TT]), sb("sel", [P, TT])
        t = dve.do(lambda e: e.tensor_reduce(rank[:], cnt[:], AX.X, ALU.add), t)
        sel_t = dve.do(lambda e: e.tensor_scalar(sel[:], rank[:], F_S - 0.5, None, ALU.is_lt), t)
        within, total = ps[:, 6, 0:TT], ps[:, 7, 0:TT]
        t1 = pe.do(lambda e: e.matmul(within, upper[:], sel[:], start=True, stop=True), sel_t, upper_t)
        t2 = pe.do(lambda e: e.matmul(total, ones[:], sel[:], start=True, stop=True), ones_t)
        upto, pos = sb("upto", [P, TT]), sb("pos", [P, TT])
        t = dve.do(lambda e: e.tensor_tensor_scan(upto[:], ones[:, 0:TT], total, 0.0, ALU.mult, ALU.add), t2)
        t = dve.do(lambda e: e.tensor_tensor(upto[:], upto[:], total, ALU.subtract), t)
        t = dve.do(lambda e: e.tensor_tensor(pos[:], upto[:], within, ALU.add), t)
        take = sb("take", [P, TT, P])
        for c in range(TT):
            take_t = dve.do(lambda e: e.tensor_scalar(take[:, c], ramp[:], pos[:, c:c + 1], sel[:, c:c + 1],
                                                      ALU.is_equal, ALU.mult), t, ramp_t)
        t = None
        for m in range(4):
            for c in range(TT):
                lhs = h_tok[:, c, m * P:m * P + P] if m < 2 else trope[:, c, m - 2]
                t = pe.do(lambda e: e.matmul(ps[:, 0, m * P:m * P + P], lhs, take[:, c], start=(c == 0), stop=(c == TT - 1)),
                          take_t, h_tok_t, l_trope)
        xs, rope = sb("xs", [P, KT, P]), sb("ropes", [P, 2, P])
        flat2 = "p a b -> p (a b)"
        xs_t = dve.do(lambda e: e.tensor_copy(xs[:, :].rearrange(flat2), ps[:, 0, 0:2 * P]), t)
        rope_t = dve.do(lambda e: e.tensor_copy(rope[:, :].rearrange(flat2), ps[:, 0, 2 * P:]))
        takeT = sb("takeT", [P, N])
        for b in range(2):
            for j in range(4):
                t = pe.do(lambda e: e.transpose(ps[:, 1 + b, j * P:j * P + P], take[:, 4 * b + j], g.ident[:]), h_tok_t)
            takeT_t = act.do(lambda e: e.activation(takeT[:, b * HALF:(b + 1) * HALF], ps[:, 1 + b, :], ACT.Copy), t)
        gate = sb("gate", [P, P])
        for k in range(KT):
            gate_mm = pe.do(lambda e: e.matmul(ps[:, 6, 0:P], wrb[:, k], xs[:, k], start=(k == 0), stop=(k == KT - 1)), xs_t,
                            dve.last())

        def rms(name, src, ready, which):
            dst, sq, inv = sb(name, [P, KT, P]), sb(name + "_sq", [P, KT, P]), sb(name + "_inv", [P, P])
            t = act.do(lambda e: e.activation(sq[:], src[:], ACT.Square), ready)
            for k in range(KT):
                t = pe.do(lambda e: e.matmul(ps[:, 7, 0:P], g.avg[:], sq[:, k], start=(k == 0), stop=(k == KT - 1)), t,
                          dve.last())
            t = act.do(lambda e: e.activation(inv[:], ps[:, 7, 0:P], ACT.Sqrt, bias=g.eps[:, 1:2]), t)
            t = dve.do(lambda e: e.reciprocal(inv[:], inv[:]), t)
            for k in range(KT):
                t2 = dve.do(lambda e: e.scalar_tensor_tensor(dst[:, k], src[:, k], ln[:, which, k:k + 1], inv[:],
                                                             ALU.mult, ALU.mult), t, l_ln, ready)
            return dst, t2

        h1, h1_t = rms("h1", xs, xs_t, 0)

        nqk = F_HEADS + F_KV
        qk = sb("qk", [P, nqk, P])
        qkb, r1, r2 = sb("qkb", [P, 2, 4, P]), sb("r1", [P, 2, 4, P]), sb("r2", [P, 2, 4, P])
        rope_free, bank_free, qk_t = [None, None], {}, []
        up_rows, down_rows = slice(64, 128), slice(0, 64)
        for n in range(nqk // 4):
            b, par = (0, 3, 4, 5)[n % 4], n % 2
            for j in range(4):
                hd = 4 * n + j
                w, col = (wq, hd) if hd < F_HEADS else (wk, hd - F_HEADS)
                for k in range(KT):
                    t = pe.do(lambda e: e.matmul(ps[:, b, j * P:j * P + P], w[:, k, col * P:col * P + P], h1[:, k],
                                                 start=(k == 0), stop=(k == KT - 1)), h1_t, l_wq, l_wk, s_t, rope_t,
                              bank_free.get(b))
            t = dve.do(lambda e: e.tensor_tensor(qkb[:, par], ps[:, b, :].rearrange("p (j q) -> p j q", j=4),
                                                 bqk[:, 4 * n:4 * n + 4].unsqueeze(2).broadcast_to([P, 4, P]), ALU.add),
                       t, l_bqk, rope_free[par])
            bank_free[b] = t
            a1 = pool.do(lambda e: e.tensor_tensor(r1[:, par], qkb[:, par], rope[:, 0].unsqueeze(1).broadcast_to([P, 4, P]),
                                                   ALU.mult), t, rope_t)
            for src, dst in ((up_rows, down_rows), (down_rows, up_rows)):
                a2 = dve.do(lambda e: e.tensor_tensor(r2[dst, par], qkb[src, par],
                                                      rope[src, 1].unsqueeze(1).broadcast_to([64, 4, P]), ALU.mult), t, rope_t)
            t = pool.do(lambda e: e.tensor_tensor(qk[:, 4 * n:4 * n + 4], r1[:, par], r2[:, par], ALU.add), a1, a2)
            rope_free[par] = t
            qk_t.append(t)
        v = sb("v", [P, F_KV * F_HD])
        for c in range(2):
            cc = slice(c * HALF, (c + 1) * HALF)
            for k in range(KT):
                pe.do(lambda e: e.matmul(ps[:, 1 + c, :], h1[:, k], wv[:, k, cc], start=(k == 0), stop=False), l_wv, l_bv,
                      takeT_t)
            t = pe.do(lambda e: e.matmul(ps[:, 1 + c, :], ones[0:1, :], bv[0:1, cc], start=False, stop=True))
            v_t = act.do(lambda e: e.activation(v[:, cc], ps[:, 1 + c, :], ACT.Copy), t)

        prob, probT, oT = sb("prob", [P, F_HEADS, P]), sb("probT", [P, F_HEADS, P]), sb("oT", [P, F_HEADS, P])
        neg, rsum = sb("neg", [P, F_HEADS]), sb("rsum", [P, F_HEADS])
        nb = F_HEADS // 4
        stage = {}
        for n in range(nb):
            b, hs = (0, 3, 4, 5)[n], slice(4 * n, 4 * n + 4)
            for j in range(4):
                hd = 4 * n + j
                kv = F_HEADS + hd * F_KV // F_HEADS
                t = pe.do(lambda e: e.matmul(ps[:, b, j * P:j * P + P], qk[:, hd], qk[:, kv], start=True, stop=True),
                          qk_t, bank_free.get(b))
            t = dve.do(lambda e: e.tensor_tensor(prob[:, hs], ps[:, b, :].rearrange("p (j q) -> p j q", j=4),
                                                 g.mask[:].unsqueeze(1).broadcast_to([P, 4, P]), ALU.add), t)
            bank_free[b] = t
            stage[n] = t
        for n in range(nb):
            hs = slice(4 * n, 4 * n + 4)
            t = dve.do(lambda e: e.tensor_reduce(neg[:, hs], prob[:, hs], AX.X, ALU.max, negate=True), stage[n])
            stage[n] = dve.do(lambda e: e.tensor_scalar(neg[:, hs], neg[:, hs], F_SCALE, None, ALU.mult), t)
        for n in range(nb):
            hs = slice(4 * n, 4 * n + 4)
            for hd in range(4 * n, 4 * n + 4):
                t = act.do(lambda e: e.activation(prob[:, hd], prob[:, hd], ACT.Exp, bias=neg[:, hd:hd + 1], scale=F_SCALE,
                                                  accum_out=rsum[:, hd:hd + 1]), stage[n])
            t = dve.do(lambda e: e.reciprocal(rsum[:, hs], rsum[:, hs]), t)
            t = dve.do(lambda e: e.tensor_tensor(prob[:, hs], prob[:, hs], rsum[:, hs].unsqueeze(2).broadcast_to([P, 4, P]),
                                                 ALU.mult), t)
            b = (0, 3, 4, 5)[n]
            for j in range(4):
                t = pe.do(lambda e: e.transpose(ps[:, b, j * P:j * P + P], prob[:, 4 * n + j], g.ident[:]), t, bank_free.get(b))
            pT = act.do(lambda e: e.activation(probT[:, hs].rearrange(flat2), ps[:, b, :], ACT.Copy), t)
            stage[n] = pT
        for n in range(nb):
            b, hs = (0, 3, 4, 5)[n], slice(4 * n, 4 * n + 4)
            for j in range(4):
                hd = 4 * n + j
                kv = hd * F_KV // F_HEADS
                t = pe.do(lambda e: e.matmul(ps[:, b, j * P:j * P + P], v[:, kv * F_HD:(kv + 1) * F_HD], probT[:, hd],
                                             start=True, stop=True), stage[n], v_t)
            oT_t = dve.do(lambda e: e.tensor_copy(oT[:, hs].rearrange(flat2), ps[:, b, :]), t)
        for m in range(KT):
            for hd in range(F_HEADS):
                t = pe.do(lambda e: e.matmul(ps[:, 1, m * P:m * P + P], wo[:, hd, m * P:m * P + P], oT[:, hd],
                                             start=(hd == 0), stop=(hd == F_HEADS - 1)), oT_t, l_wo, v_t)
        x1 = sb("x1", [P, KT, P])
        x1_t = dve.do(lambda e: e.tensor_tensor(x1[:, :].rearrange(flat2), xs[:, :].rearrange(flat2), ps[:, 1, 0:2 * P],
                                                ALU.add), t)

        h2, h2_t = rms("h2", x1, x1_t, 1)
        sig_gate = act.do(lambda e: e.activation(gate[:], ps[:, 6, 0:P], ACT.Sigmoid), gate_mm)
        hid, sg = s[:, :].rearrange("p (f q) -> p f q", q=P), diag
        for half in range(2):
            fs = slice(4 * half, 4 * half + 4)
            bg, bu = (0, 3)[half], (4, 5)[half]
            for w, lw, b in ((wg, l_wg, bg), (wu, l_wu, bu)):
                for j in range(4):
                    f = 4 * half + j
                    for k in range(KT):
                        t = pe.do(lambda e: e.matmul(ps[:, b, j * P:j * P + P], w[:, k, f * P:f * P + P], h2[:, k],
                                                     start=(k == 0), stop=(k == KT - 1)), h2_t, lw, oT_t)
                if w is wg:
                    tg = act.do(lambda e: e.activation(sg[:, fs].rearrange(flat2), ps[:, b, :], ACT.Sigmoid), t)
            tg = dve.do(lambda e: e.tensor_tensor(sg[:, fs].rearrange(flat2), sg[:, fs].rearrange(flat2), ps[:, bg, :], ALU.mult), tg)
            hid_t = dve.do(lambda e: e.tensor_tensor(hid[:, fs].rearrange(flat2), sg[:, fs].rearrange(flat2), ps[:, bu, :],
                                                     ALU.mult), tg, t)
        for m in range(KT):
            for f in range(FI_T):
                t = pe.do(lambda e: e.matmul(ps[:, 2, m * P:m * P + P], wd[:, f, m * P:m * P + P], hid[:, f],
                                             start=(f == 0), stop=(f == FI_T - 1)), hid_t, l_wd, v_t)
        ch = sb("ch", [P, KT, P])
        a = pool.do(lambda e: e.tensor_tensor(ch[:], x1[:], xs[:], ALU.subtract), x1_t, xs_t)
        t = dve.do(lambda e: e.tensor_tensor(ch[:, :].rearrange(flat2), ch[:, :].rearrange(flat2), ps[:, 2, 0:2 * P], ALU.add), t, a)
        t = dve.do(lambda e: e.tensor_tensor(ch[:], ch[:], gate[:].unsqueeze(1).broadcast_to([P, KT, P]), ALU.mult), t, sig_gate)
        chT = sb("chT", [P, D])
        for m in range(KT):
            tp = pe.do(lambda e: e.transpose(ps[:, 6, m * P:m * P + P], ch[:, m], g.ident[:]), t)
        t = act.do(lambda e: e.activation(chT[:], ps[:, 6, 0:D], ACT.Copy), tp)
        for m in range(KT):
            for c in range(NH2):
                b, cc = (0, 3, 4, 5)[2 * m + c], slice(c * HALF, (c + 1) * HALF)
                tp = pe.do(lambda e: e.matmul(ps[:, b, :], chT[:, m * P:m * P + P], takeT[:, cc], start=True, stop=True),
                           t, takeT_t, hid_t)
                dve.do(lambda e: e.tensor_tensor(g.x[:, m, cc], g.x[:, m, cc], ps[:, b, :], ALU.add), tp, x_plus)


def ffn_first(g, ins):
    ffn(g, ins, "f1")


def ffn_second(g, ins):
    ffn(g, ins, "f2")


def halves():
    return [(c, slice(c * HALF, (c + 1) * HALF)) for c in range(NH2)]


def linear(g, w, acts, m_tiles, banks, take, *tokens, only=None, at=None):
    pe = g.pr.pe
    w_hi, w_lo = w
    a_hi, a_lo = acts
    free = {}
    n = 0
    for m in m_tiles:
        for c, cc in halves() if only is None else [halves()[only]]:
            b = banks[n % len(banks)]
            n += 1
            mm = slice(m * P, m * P + P)
            ac = at or cc
            t = matmul3(pe, g.ps[:, b, :],
                        [(w_hi[:, k, mm], None if w_lo is None else w_lo[:, k, mm], a_hi[:, k, ac], a_lo[:, k, ac])
                         for k in range(w_hi.shape[1])], tokens, free.get(b))
            free[b] = take(m, c, cc, g.ps[:, b, :], t)
    return [t for ts in free.values() for t in ts]


def split(g, hi, lo, src, *tokens):
    th = g.pr.act.do(lambda e: e.activation(hi, src, ACT.Copy), *tokens)
    return g.pr.dve.do(lambda e: e.tensor_tensor(lo, src, fr(hi), ALU.subtract), th, *tokens)


def recurrence(g, ins):
    pr = g.pr
    pe, dve, act, pool, sp = pr.pe, pr.dve, pr.act, pr.pool, pr.sp
    with pr.phase():
        h = pr.sb("r_h", [P, KT, N])
        h_hi, h_lo = pr.sb("r_h_hi", [P, KT, N], F32R), pr.sb("r_h_lo", [P, KT, N], F32R)
        w = pr.sb("r_w", [P, KT, 2 * D])
        w_hi, w_lo = pr.sb("r_w_hi", [P, KT, 2 * D], F32R), pr.sb("r_w_lo", [P, KT, 2 * D], F32R)
        bias = pr.sb("r_bias", [P, 2 * KT])
        gates, values, hidden = pr.sb("r_gates", [P, KT, N]), pr.sb("r_values", [P, KT, N]), pr.sb("r_hidden", [P, KT, N])
        s_w = pr.slot("r_loaded")
        sp.dma(s_w, lambda: bias[:], lambda: ins["r_b"])
        t = sp.dma(s_w, lambda: w[:], lambda: ins["r_w"])
        w_t = split(g, w_hi[:], w_lo[:], w[:], t)
        hn = normalise(g, "r_n", g.x, h, N, 1e-5, centre=True, split=(h_hi, h_lo))
        done = {}

        def take(m, c, cc, ps, t):
            dst, func = (gates, ACT.Sigmoid) if m < KT else (values, ACT.Tanh)
            a = act.do(lambda e: e.activation(dst[:, m % KT, cc], ps, func, bias=bias[:, m:m + 1]), t)
            done[m, c] = a
            if m >= KT:
                f = m - KT
                first = 0.0 if c == 0 else hidden[:, f, c * HALF - 1:c * HALF]
                s = dve.do(lambda e: e.tensor_tensor_scan(hidden[:, f, cc], gates[:, f, cc], values[:, f, cc], first,
                                                          ALU.mult, ALU.add), a, done[f, c], done.get(("scan", f, c - 1)))
                done["scan", f, c] = s
                dve.do(lambda e: e.tensor_tensor(g.x[:, f, cc], g.x[:, f, cc], hidden[:, f, cc], ALU.add), s)
            return [a]

        linear(g, (w_hi, w_lo), (h_hi, h_lo), (0, 2, 1, 3), (4, 5, 6, 7), take, w_t, hn)


R_F, R_TAPS, R_C = 768, 4, 8.0
RF_T = R_F // P


def rglru(g, ins):
    pr = g.pr
    pe, dve, act, pool, sp = pr.pe, pr.dve, pr.act, pr.pool, pr.sp
    with pr.phase():
        def sb(name, shape, dt=F32):
            return pr.sb("l_" + name, shape, dt)

        bias = sb("bias", [P, 10, KT])
        LEFT, RIGHT, CONV, GA, GX, AP, OUT, DOWN, NORM1, NORM2 = range(10)
        up_b = sb("up_b", [P, 2, RF_T])
        taps = sb("taps", [P, R_TAPS, KT])
        s_b = pr.slot("l_bias_loaded")
        sp.dma(s_b, lambda: bias[:], lambda: ins["l_bias"])
        sp.dma(s_b, lambda: up_b[:], lambda: ins["l_up_b"])
        b_t = sp.dma(s_b, lambda: taps[:], lambda: ins["l_taps"])

        raw = [sb("raw0", [P, KT * R_F]), sb("raw1", [P, KT * R_F])]
        raw_slot = [pr.slot("l_raw0_loaded"), pr.slot("l_raw1_loaded")]
        raw_free = [None, None]
        w, w_t = {}, {}
        for n, (name, kt, cols) in enumerate((("left", KT, D), ("right", KT, D), ("ga", KT, D), ("gx", KT, D), ("out", KT, D),
                                              ("up1", KT, R_F), ("up2", KT, R_F), ("down", RF_T, D))):
            r = raw[n % 2][:, 0:kt * cols].rearrange("p (k n) -> p k n", k=kt)
            hi, lo = sb(name + "_hi", [P, kt, cols], F32R), sb(name + "_lo", [P, kt, cols], F32R)
            t = sp.dma(raw_slot[n % 2], lambda: r, lambda: ins["l_" + name], raw_free[n % 2])
            th = pool.do(lambda e: e.tensor_copy(hi[:], r), t)
            tl = pool.do(lambda e: e.tensor_tensor(lo[:], r, fr(hi[:]), ALU.subtract), th)
            raw_free[n % 2] = [tl]
            w[name], w_t[name] = (hi, lo), tl

        sm = sb("softplus", [P, 6, KT])
        a_par = bias[:, AP]
        t = act.do(lambda e: e.activation(sm[:, 0], a_par, ACT.Abs), b_t)
        t = act.do(lambda e: e.activation(sm[:, 1], sm[:, 0], ACT.Exp, scale=-1.0), t)
        t = dve.do(lambda e: e.tensor_scalar(sm[:, 2], sm[:, 1], 1.0, None, ALU.add), t)
        tw = act.do(lambda e: e.activation(sm[:, 3], sm[:, 2], ACT.Ln), t)
        t = dve.do(lambda e: e.tensor_scalar(sm[:, 4], sm[:, 2], -1.0, None, ALU.add), t)
        t = dve.do(lambda e: e.tensor_scalar(sm[:, 5], sm[:, 4], 0.0, None, ALU.is_equal), t)
        t = dve.do(lambda e: e.tensor_tensor(sm[:, 4], sm[:, 4], sm[:, 5], ALU.add), t)
        t = dve.do(lambda e: e.reciprocal(sm[:, 4], sm[:, 4]), t)
        t = dve.do(lambda e: e.tensor_tensor(sm[:, 4], sm[:, 4], sm[:, 3], ALU.mult), t, tw)
        t = dve.do(lambda e: e.tensor_tensor(sm[:, 4], sm[:, 4], sm[:, 5], ALU.add), t)
        t = dve.do(lambda e: e.tensor_tensor(sm[:, 4], sm[:, 4], sm[:, 1], ALU.mult), t)
        t = dve.do(lambda e: e.scalar_tensor_tensor(sm[:, 0], a_par, 0.0, sm[:, 4], ALU.max, ALU.add), t)
        rate_t = dve.do(lambda e: e.tensor_scalar(sm[:, 0], sm[:, 0], -R_C, None, ALU.mult), t)
        rate = sm[:, 0]

        u = sb("u", [P, KT, N])
        xn, xn_hi, xn_lo = sb("xn", [P, KT, N]), sb("xn_hi", [P, KT, N], F32R), sb("xn_lo", [P, KT, N], F32R)
        scratch = norm_scratch(pr, "l_norm", N)
        un = normalise(g, "l_n0", g.x, u, N, 1e-5, centre=True, scratch=scratch)
        un = [o[0] for o in un]
        nn = normalise(g, "l_n1", u, xn, N, 1e-8, src_ready=un + [b_t], weight=bias[:, NORM1], split=(xn_hi, xn_lo),
                       scratch=scratch)
        left = sb("left", [P, KT, N])
        PAD = R_TAPS - 1
        right = sb("right", [P, KT, PAD + N])
        z = dve.do(lambda e: e.memset(right[:, :, 0:PAD], 0.0))
        left_t, right_t = [], [z]

        def take_left(m, c, cc, ps, t):
            a = act.do(lambda e: e.activation(left[:, m, cc], ps, ACT.Gelu, bias=bias[:, LEFT, m:m + 1]), t)
            left_t.append(a)
            return [a]

        def take_right(m, c, cc, ps, t):
            a = dve.do(lambda e: e.tensor_scalar(right[:, m, PAD + c * HALF:PAD + (c + 1) * HALF], ps,
                                                 bias[:, RIGHT, m:m + 1], None, ALU.add), t)
            right_t.append(a)
            return [a]

        linear(g, w["right"], (xn_hi, xn_lo), range(KT), (4, 5, 6, 7), take_right, w_t["right"], nn)
        linear(g, w["left"], (xn_hi, xn_lo), range(KT), (0, 1, 2, 3), take_left, w_t["left"])
        xn_read = pe.last()
        y = xn
        y_hi, y_lo = xn_hi, xn_lo
        y_t = []
        for m in range(KT):
            t = dve.do(lambda e: e.tensor_scalar(y[:, m], right[:, m, 0:N], taps[:, 0, m:m + 1], bias[:, CONV, m:m + 1],
                                                 ALU.mult, ALU.add), right_t, nn)
            for j in range(1, R_TAPS):
                t = dve.do(lambda e: e.scalar_tensor_tensor(y[:, m], right[:, m, j:j + N], taps[:, j, m:m + 1], y[:, m],
                                                            ALU.mult, ALU.add), t)
            y_t.append(split(g, y_hi[:, m], y_lo[:, m], y[:, m], t, xn_read))
        rg, ig, th = sb("rg", [P, KT, N]), sb("ig", [P, KT, N]), right[:, :, PAD:]
        a_ = scratch[0][:, :, :, :].rearrange("p a k w -> p (a k w)").rearrange("p (k n) -> p k n", k=KT)
        sig_t = []
        for dst, name, bb, banks in ((rg, "ga", GA, (0, 1, 2, 3)), (ig, "gx", GX, (4, 5, 6, 7))):
            def take(m, c, cc, ps, t):
                a = act.do(lambda e: e.activation(dst[:, m, cc], ps, ACT.Sigmoid, bias=bias[:, bb, m:m + 1]), t)
                sig_t.append(a)
                return [a]
            linear(g, w[name], (y_hi, y_lo), range(KT), banks, take, w_t[name], y_t, left_t)
        for m in range(KT):
            ta = act.do(lambda e: e.activation(a_[:, m], rg[:, m], ACT.Exp, scale=rate[:, m:m + 1]), sig_t, rate_t)
            tt = act.do(lambda e: e.activation(th[:, m], rg[:, m], ACT.Tanh, scale=rate[:, m:m + 1]), y_t)
            tr = dve.do(lambda e: e.tensor_tensor(rg[:, m], a_[:, m], a_[:, m], ALU.mult), ta, tt)
            t = dve.do(lambda e: e.scalar_tensor_tensor(rg[:, m], rg[:, m], 1.0, th[:, m], ALU.add, ALU.mult), tr, tt)
            sig_t.append(t)
            ti = pool.do(lambda e: e.tensor_tensor(ig[:, m], ig[:, m], y[:, m], ALU.mult), sig_t[:-1], y_t)
            sig_t.append(ti)
        prod_t = []
        for m in range(KT):
            t = act.do(lambda e: e.activation(rg[:, m], rg[:, m], ACT.Sqrt, scale=-1.0), sig_t)
            t = dve.do(lambda e: e.tensor_tensor(ig[:, m], ig[:, m], rg[:, m], ALU.mult), t, sig_t)
            t = dve.do(lambda e: e.tensor_tensor_scan(th[:, m], a_[:, m], ig[:, m], 0.0, ALU.mult, ALU.add), t)
            t = dve.do(lambda e: e.tensor_tensor(left[:, m], left[:, m], th[:, m], ALU.mult), t, left_t)
            prod_t.append(split(g, y_hi[:, m], y_lo[:, m], left[:, m], t, sig_t))
        x1, x1_t = y, []

        def take_out(m, c, cc, ps, t):
            a = dve.do(lambda e: e.scalar_tensor_tensor(x1[:, m, cc], ps, bias[:, OUT, m:m + 1], u[:, m, cc],
                                                        ALU.add, ALU.add), t)
            x1_t.append(a)
            return [a]

        linear(g, w["out"], (y_hi, y_lo), range(KT), (0, 1, 2, 3), take_out, w_t["out"], prod_t)
        out_read = pe.last()
        x_t = pool.do(lambda e: e.tensor_tensor(g.x[:], g.x[:], x1[:], ALU.add), x1_t)
        nn2 = normalise(g, "l_n2", x1, left, N, 1e-8, src_ready=x1_t, dst_free=[out_read] + prod_t,
                        weight=bias[:, NORM2], split=(y_hi, y_lo), scratch=scratch)
        mid_hi, mid_lo = sb("mid_hi", [P, RF_T, HALF], F32R), sb("mid_lo", [P, RF_T, HALF], F32R)
        gel, down_read, free = {}, None, [x_t, None]
        bufs = [rg[:, 0], ig[:, 0]], [rg[:, 1], ig[:, 1]]
        f1 = {0: None, 1: None}
        f2 = {0: None, 1: None}
        for half in range(NH2):
            mid_t = []
            for f in range(RF_T):
                par = f % 2
                gb, pb = bufs[0][par][:, 0:HALF], bufs[1][par][:, 0:HALF]

                def take1(m, c, cc, ps, t):
                    gel["gelu"] = act.do(lambda e: e.activation(gb, ps, ACT.Gelu, bias=up_b[:, 0, m:m + 1]), t,
                                         gel.get(("used", par)))
                    return [gel["gelu"]]

                def take2(m, c, cc, ps, t):
                    a = dve.do(lambda e: e.scalar_tensor_tensor(pb, ps, up_b[:, 1, m:m + 1], gb, ALU.add, ALU.mult),
                               t, gel["gelu"], gel.get(("used", par)))
                    gel["used", par] = split(g, mid_hi[:, m], mid_lo[:, m], pb, a, down_read)
                    mid_t.append(gel["used", par])
                    return [a]

                f1[par] = linear(g, w["up1"], (y_hi, y_lo), [f], (4 + par,), take1, w_t["up1"], nn2, f1[par], only=half)
                f2[par] = linear(g, w["up2"], (y_hi, y_lo), [f], (6 + par,), take2, w_t["up2"], f2[par], only=half)

            def take_down(m, c, cc, ps, t):
                return [dve.do(lambda e: e.scalar_tensor_tensor(g.x[:, m, cc], ps, bias[:, DOWN, m:m + 1], g.x[:, m, cc],
                                                                ALU.add, ALU.add), t, x_t)]

            linear(g, w["down"], (mid_hi, mid_lo), range(KT), (2 * half, 2 * half + 1), take_down, w_t["down"], mid_t,
                   only=half, at=slice(0, HALF))
            down_read = [pe.last()]


T_E = 1024
TE_T = T_E // P


def ternary_weights(g, ins):
    pr = g.pr
    pe, dve, act, pool, sp = pr.pe, pr.dve, pr.act, pr.pool, pr.sp
    g.tern, g.scale = {}, pr.sb("t_scale", [P, 3, 3])
    for n, (name, kt, cols) in enumerate((("up", KT, T_E), ("gate", KT, T_E), ("down", TE_T, D))):
        g.tern[name] = pr.sb("t_" + name, [P, kt, cols], F32R)
    with pr.phase():
        part, avg = pr.sb("t_part", [P, 3]), pr.sb("t_avg", [P, P])
        a_t = dve.do(lambda e: e.memset(avg[:], 1.0 / (T_E * D)))
        for n, (name, kt, cols) in enumerate((("up", KT, T_E), ("gate", KT, T_E), ("down", TE_T, D))):
            raw, neg = pr.sb("t_raw_" + name, [P, kt, cols]), pr.sb("t_neg_" + name, [P, kt, cols])
            slot = pr.slot(f"t_{name}_loaded")
            l = sp.dma(slot, lambda: raw[:], lambda: ins["t_" + name])
            t = dve.do(lambda e: e.tensor_reduce(part[:, n:n + 1], raw[:], AX.XY, ALU.add, apply_absolute_value=True), l)
            t = pe.do(lambda e: e.matmul(g.ps[:, n, 0:1], avg[:], part[:, n:n + 1], start=True, stop=True), t, a_t)
            s = g.scale[:, n]
            t = dve.do(lambda e: e.tensor_scalar(s[:, 0:1], g.ps[:, n, 0:1], 1e-8, None, ALU.add), t)
            dve.do(lambda e: e.tensor_scalar(s[:, 1:2], s[:, 0:1], 0.5, None, ALU.mult), t)
            t = dve.do(lambda e: e.tensor_scalar(s[:, 2:3], s[:, 0:1], -0.5, None, ALU.mult), t)
            t = dve.do(lambda e: e.tensor_scalar(neg[:], raw[:], s[:, 2:3], None, ALU.is_lt), t)
            dve.do(lambda e: e.scalar_tensor_tensor(g.tern[name][:], raw[:], s[:, 1:2], neg[:], ALU.is_gt, ALU.subtract), t)


def ternary_ffn(g, ins, tag):
    pr = g.pr
    pe, dve, act, pool, sp = pr.pe, pr.dve, pr.act, pr.pool, pr.sp
    with pr.phase():
        h = pr.sb(tag + "_h", [P, KT, N])
        h_hi, h_lo = pr.sb(tag + "_h_hi", [P, KT, N], F32R), pr.sb(tag + "_h_lo", [P, KT, N], F32R)
        hn = normalise(g, tag + "_n", g.x, h, N, 1e-5, centre=True, split=(h_hi, h_lo))
        sg, hid = pr.sb(tag + "_sg", [P, 2, N]), pr.sb(tag + "_hid", [P, 2, N])
        hid_hi, hid_lo = pr.sb(tag + "_hid_hi", [P, TE_T, N], F32R), pr.sb(tag + "_hid_lo", [P, TE_T, N], F32R)
        s_up, s_gate, s_down = (g.scale[:, n, 0:1] for n in range(3))
        st, hid_t = {}, []
        for f in range(TE_T):
            par = f % 2

            def take_up(m, c, cc, ps, t):
                a = act.do(lambda e: e.activation(sg[:, par, cc], ps, ACT.Sigmoid, scale=s_up), t, st.get(("used", par)))
                b = dve.do(lambda e: e.scalar_tensor_tensor(sg[:, par, cc], ps, s_up, sg[:, par, cc], ALU.mult, ALU.mult), a)
                st[c] = b
                return [b]

            def take_gate(m, c, cc, ps, t):
                b = dve.do(lambda e: e.scalar_tensor_tensor(hid[:, par, cc], ps, s_gate, sg[:, par, cc], ALU.mult, ALU.mult),
                           t, st[c], st.get(("used", par)))
                s = split(g, hid_hi[:, m, cc], hid_lo[:, m, cc], hid[:, par, cc], b)
                st["used", par] = s
                hid_t.append(s)
                return [b]

            f1 = linear(g, (g.tern["up"], None), (h_hi, h_lo), [f], (4, 5) if par else (0, 1), take_up, hn, st.get(("f1", par)))
            f2 = linear(g, (g.tern["gate"], None), (h_hi, h_lo), [f], (6, 7) if par else (2, 3), take_gate,
                        st.get(("f2", par)))
            st["f1", par], st["f2", par] = f1, f2

        def take_down(m, c, cc, ps, t):
            return [dve.do(lambda e: e.scalar_tensor_tensor(g.x[:, m, cc], ps, s_down, g.x[:, m, cc], ALU.mult, ALU.add), t)]

        linear(g, (g.tern["down"], None), (hid_hi, hid_lo), range(KT), (0, 1, 2, 3), take_down, hid_t, f1, f2)


def ternary_first(g, ins):
    ternary_weights(g, ins)
    ternary_ffn(g, ins, "t1")


def ternary_second(g, ins):
    ternary_ffn(g, ins, "t2")


def build(nc, ins, out, stop=99):
    with ExitStack() as ctx:
        g = Env()
        pr = g.pr = Prog(nc, ctx)
        g.ps = ctx.enter_context(nc.psum_tensor("ps", [P, 8, HALF], F32))
        g.ps_flat = g.ps[:, :, :].rearrange("p b n -> p (b n)")
        g.bank = [g.ps[:, b, :] for b in range(8)]
        setup(g, ins, None)
        layers = LAYERS
        for layer in layers[:stop]:
            layer(g, ins)
        s_out = pr.slot("x_stored")
        pr.fence()
        pr.sp.wait(g.x_ready)
        t = pr.sp.dma(s_out, lambda: out.rearrange("(k p) n -> p k n", p=P), lambda: g.x[:])
        pr.sp.wait(t)


LAYERS = [attn_a, ffn_first, attn_b, ffn_second, recurrence, ternary_first, rglru, ternary_second]


def rope_tables(n, dim, theta=10000.0):
    inv = (1.0 / np.float32(theta) ** (np.arange(0, dim, 2, dtype=np.float32) / np.float32(dim))).astype(np.float32)
    ang = (np.arange(n, dtype=np.float32)[:, None] * inv[None, :]).astype(np.float32)
    return np.cos(ang).astype(np.float32), np.sin(ang).astype(np.float32)


def layout(i):
    a = {k: np.asarray(v) for k, v in i.items()}
    r = {}
    r["x"] = a["L0_attn_a_hidden_states"][0].T
    q = a["L0_attn_a_Wq"].T.reshape(D, A_KV, A_GRP * A_HD)
    k = a["L0_attn_a_Wk"].T.reshape(D, A_KV, A_HD)
    v = a["L0_attn_a_Wv"].T.reshape(D, A_KV, A_HD)
    r["a_w"] = np.concatenate([q, k, v], 2).reshape(KT, P, A_KV, A_W).transpose(2, 1, 0, 3)
    r["a_o"] = a["L0_attn_a_Wo"].T.reshape(A_KV, 2, P, D).transpose(0, 2, 1, 3)
    cos, sin = rope_tables(N, A_HD)
    r["a_cos"] = np.concatenate([cos, cos], 1).reshape(TT, P, A_HD).transpose(1, 0, 2)
    r["a_sin"] = np.concatenate([-sin, sin], 1).reshape(TT, P, A_HD).transpose(1, 0, 2)
    turns = B_HEADS // B_GRP
    qkv = [a["L0_attn_b_W_" + c].transpose(1, 0, 2).reshape(D, turns, B_C) for c in "QKV"]
    r["b_w"] = np.concatenate(qkv, 2).reshape(KT, P, turns, 3 * B_C).transpose(2, 1, 0, 3)
    r["b_o"] = a["L0_attn_b_W_O"].reshape(turns, B_GRP, B_HD, D).transpose(0, 2, 1, 3)
    r["b_bias"] = np.stack([a["L0_attn_b_b_" + c].reshape(turns, B_GRP, B_HD) for c in "QKV"]).transpose(3, 1, 0, 2)
    r["b_bias_out"] = a["L0_attn_b_b_O"].reshape(KT, P).T

    def tiles(w):
        return w.reshape(-1, P, w.shape[1]).transpose(1, 0, 2)

    f = {k[7:]: v for k, v in a.items() if k.startswith("L0_ffn_")}
    r["f_wr"] = f["w_router"].reshape(KT, P).T
    r["f_ln"] = np.stack([f["ln1_w"], f["ln2_w"]]).reshape(2, KT, P).transpose(2, 0, 1)
    r["f_bqk"] = np.concatenate([f["bq"], f["bk"]]).reshape(-1, P).T
    r["f_bv"] = f["bv"][None, :]
    for name, key in (("wq", "wq"), ("wk", "wk"), ("wv", "wv"), ("wo", "wo"), ("wg", "w_gate"), ("wu", "w_up"), ("wd", "w_down")):
        r["f_" + name] = tiles(f[key])
    cos, sin = rope_tables(N, F_HD)
    tab = np.stack([np.concatenate([cos, cos], 1), np.concatenate([sin, -sin], 1)], 1)
    r["f_rope"] = tab.reshape(TT, P, 2, P).transpose(1, 0, 2, 3)
    r["r_w"] = tiles(a["L1_attn_a_W"].T)
    r["r_b"] = a["L1_attn_a_b"].reshape(-1, P).T
    l = {k[10:]: v for k, v in a.items() if k.startswith("L1_attn_b_")}
    for name in ("left", "right", "ga", "gx", "out", "up1", "up2", "down"):
        r["l_" + name] = tiles(l[name + "_W"])
    vectors = ("left_b", "right_b", "conv_b", "ga_b", "gx_b", "a_param", "out_b", "down_b", "norm1_w", "norm2_w")
    r["l_bias"] = np.stack([l[v] for v in vectors]).reshape(len(vectors), KT, P).transpose(2, 0, 1)
    r["l_up_b"] = np.stack([l["up1_b"], l["up2_b"]]).reshape(2, RF_T, P).transpose(2, 0, 1)
    r["l_taps"] = l["conv_w"].reshape(R_TAPS, KT, P).transpose(2, 0, 1)
    for name in ("up", "gate", "down"):
        r["t_" + name] = tiles(a["L1_ffn_W_" + name].T)
    return r


def kernel(**inputs):
    import concourse.bacc as bacc
    from concourse.bass_utils import run_bass_kernel_spmd

    nc = bacc.Bacc("TRN2", target_bir_lowering=False, num_devices=1)
    arrays = {f"in_{k}": np.ascontiguousarray(v) for k, v in layout(inputs).items()}
    ins = {k[3:]: nc.dram_tensor(k, v.shape, mybir.dt.from_np(v.dtype), kind="ExternalInput").ap()
           for k, v in arrays.items()}
    out = nc.dram_tensor("out", (D, N), F32, kind="ExternalOutput").ap()
    build(nc, ins, out)
    got = run_bass_kernel_spmd(nc, [arrays], core_ids=[0])
    return np.ascontiguousarray(got.results[0]["out"].T).reshape(1, N, D)
```

```python
import math
from contextlib import ExitStack, contextmanager

import numpy as np

import concourse.bass as bass
from concourse import mybir
from concourse.alu_op_type import AluOpType as ALU

F32 = mybir.dt.float32
F32R = mybir.dt.float32r
ACT = mybir.ActivationFunctionType
AX = mybir.AxisListType

P = 128
N = 1024
D = 256
KT = D // P
TT = N // P
HALF = 512
NH2 = N // HALF
MASKED = -1e30


class Count:

    def __init__(self, prog, sem, start=0):
        self.prog, self.sem, self.n = prog, sem, start
        self.per = 0
        prog.counts.append(self)

    def add(self, k):
        self.n += k
        return Token(self, self.n, self.prog.loop)


class Token:

    def __init__(self, count, value, loop):
        self.count, self.value, self.loop = count, value, loop

    def prev(self):
        return Token(self.count, self.value - self.count.per, self.loop)

    def last(self):
        return Token(self.count, self.value + (self.loop.turns - 1) * self.loop.per[self.count], None)


class Loop:
    def __init__(self, turns):
        self.turns, self.i, self.per = turns, None, {}


class Lane:

    def __init__(self, prog, eng, sem, gate=None):
        self.prog, self.e, self.gate = prog, eng, gate
        self.count = Count(prog, sem, START)
        self.seen = {}
        prog.lanes.append(self)
        eng.sem_inc(sem, START)

    def wait(self, *tokens):
        prog, gated = self.prog, False
        for t in tokens:
            if t is None:
                continue
            if isinstance(t, (list, tuple)):
                self.wait(*t)
                continue
            key = (t.count, t.loop)
            if self.seen.get(key, -1) >= t.value:
                continue
            self.seen[key] = t.value
            if prog.dry:
                continue
            if t.loop is None:
                self.e.wait_ge(t.count.sem, t.value)
            else:
                self.e.wait_ge(t.count.sem, prog.loop.i * prog.loop.per[t.count] + t.value)
                gated = self.gate is not None
        if gated:
            self.e.sem_inc(self.gate, 1)

    def do(self, instruction, *tokens, signal=True):
        self.wait(*tokens)
        if self.prog.dry:
            return self.count.add(1) if signal else None
        ins = instruction(self.e)
        if not signal:
            return None
        ins.then_inc(self.count.sem, 1)
        return self.count.add(1)

    def last(self):
        return Token(self.count, self.count.n, self.prog.loop)

    def dma(self, slot, out, in_, *tokens):
        self.wait(*tokens)
        if not self.prog.dry:
            self.e.dma_start(out(), in_()).then_inc(slot.sem, 16)
        return slot.add(16)


START = 1024


class Prog:
    def __init__(self, nc, ctx):
        self.nc, self.ctx = nc, ctx
        self.counts, self.lanes = [], []
        self.loop, self.dry = None, False
        self.bufs = ctx
        self.readers = {}
        sem = self.sem
        self.pe = Lane(self, nc.tensor, sem("pe_done"))
        self.dve = Lane(self, nc.vector, sem("dve_done"))
        self.act = Lane(self, nc.scalar, sem("act_done"))
        self.pool = Lane(self, nc.gpsimd, sem("pool_done"), gate=sem("pool_gate"))
        self.sp = Lane(self, nc.sync, sem("sp_done"))

    def sem(self, name):
        return self.ctx.enter_context(self.nc.semaphore(name))

    def slot(self, name):
        return Count(self, self.sem(name))

    def sb(self, name, shape, dt=F32):
        return self.bufs.enter_context(self.nc.sbuf_tensor(name, shape, dt))

    def fence(self):
        ends = [Token(c, c.n, self.loop) for c in self.counts if c is not self.sp.count and c.n]
        for lane in self.lanes:
            lane.wait(*ends)

    @contextmanager
    def phase(self):
        outer = self.bufs
        with ExitStack() as bufs:
            self.bufs = bufs
            yield
            self.fence()
        self.bufs = outer

    def run_loop(self, turns, body):
        self.fence()
        self.readers.clear()
        loop = Loop(turns)
        base = {c: c.n for c in self.counts}
        held = [dict(lane.seen) for lane in self.lanes]
        self.loop, self.dry = loop, True
        body(0)
        self.dry = False
        for c in self.counts:
            c.per = loop.per[c] = c.n - base[c]
            assert c.per <= START
            c.n = base[c]
        for lane, seen in zip(self.lanes, held):
            lane.seen = seen
        for name, tokens in self.readers.items():
            self.readers[name] = [t.prev() for t in tokens]
        with self.nc.Fori(0, turns) as i:
            loop.i = i
            body(i)
        for c in self.counts:
            assert c.n == base[c] + c.per
            c.n = base[c] + turns * c.per
        self.loop = None
        self.readers.clear()
        self.fence()


def fr(ap):
    return ap.bitcast(F32)


class Env:
    pass


def setup(g, ins, x_tok):
    pr, pool, dve, sp = g.pr, g.pr.pool, g.pr.dve, g.pr.sp
    g.x = pr.sb("x", [P, KT, N])
    g.x_slot = pr.slot("x_loaded")
    g.x_ready = [sp.dma(g.x_slot, lambda: g.x[:], lambda: ins["x"].rearrange("(k p) n -> p k n", p=P))]
    g.ident = pr.sb("ident", [P, P])
    g.ident_r = pr.sb("ident_r", [P, P], F32R)
    g.mask = pr.sb("mask", [P, P])
    g.mask_r = pr.sb("mask_r", [P, P], F32R)
    g.avg = pr.sb("avg", [P, P])
    g.eps = pr.sb("eps", [P, 3])
    g.EPS = {1e-5: 0, 1e-6: 1, 1e-8: 2}
    z = pool.do(lambda e: e.memset(g.ident[:], 0.0))
    z2 = pool.do(lambda e: e.memset(g.mask[:], 0.0))
    t1 = pool.do(lambda e: e.affine_select(out=g.ident[:], in_=g.ident[:], compare_op=ALU.not_equal, fill=1.0,
                                           base=0, pattern=[[-1, P]], channel_multiplier=1), z)
    t2 = pool.do(lambda e: e.affine_select(out=g.mask[:], in_=g.mask[:], compare_op=ALU.is_ge, fill=MASKED,
                                           base=0, pattern=[[-1, P]], channel_multiplier=1), z2)
    dve.do(lambda e: e.memset(g.avg[:], 1.0 / D))
    for eps, c in g.EPS.items():
        dve.do(lambda e, c=c, eps=eps: e.memset(g.eps[:, c:c + 1], eps))
    dve.do(lambda e: e.tensor_copy(g.ident_r[:], g.ident[:]), t1)
    dve.do(lambda e: e.tensor_copy(g.mask_r[:], g.mask[:]), t2)
    pr.fence()


def norm_scratch(pr, name, cols):
    w = min(cols, HALF)
    return pr.sb(name + "_sq", [P, cols // w, KT, w]), pr.sb(name + "_inv", [P, cols // w, w])


def normalise(g, name, src, dst, cols, eps, src_ready=(), dst_free=(), centre=False, weight=None, split=None,
              scratch=None):
    pr, pe, dve, act = g.pr, g.pr.pe, g.pr.dve, g.pr.act
    w = min(cols, HALF)
    done = []
    sq, inv = scratch or norm_scratch(pr, name, cols)
    steps = []
    for b in range(cols // w):
        c = slice(b * w, b * w + w)
        ps_mean, ps_var = g.bank[2 * b][:, 0:w], g.bank[2 * b + 1][:, 0:w]
        base, ready = src, list(src_ready)
        if centre:
            for k in range(KT):
                t = pe.do(lambda e: e.matmul(ps_mean, g.avg[:], src[:, k, c], start=(k == 0), stop=(k == KT - 1)),
                          ready, signal=(k == KT - 1))
            t = dve.do(lambda e: e.tensor_tensor(dst[:, :, c], src[:, :, c],
                                                 ps_mean.unsqueeze(1).broadcast_to([P, KT, w]), ALU.subtract),
                       t, list(dst_free))
            base, ready = dst, [t]
        t = act.do(lambda e: e.activation(sq[:, b], base[:, :, c], ACT.Square), ready)
        for k in range(KT):
            t = pe.do(lambda e: e.matmul(ps_var, g.avg[:], sq[:, b, k], start=(k == 0), stop=(k == KT - 1)),
                      t, signal=(k == KT - 1))
        steps.append((b, c, ps_var, base, ready, t))
    for b, c, ps_var, base, ready, t in steps:
        k0 = g.EPS[eps]
        t = act.do(lambda e: e.activation(inv[:, b], ps_var, ACT.Sqrt, bias=g.eps[:, k0:k0 + 1]), t)
        t = dve.do(lambda e: e.reciprocal(inv[:, b], inv[:, b]), t)
        if weight is None:
            t = dve.do(lambda e: e.tensor_tensor(dst[:, :, c], base[:, :, c],
                                                 inv[:, b].unsqueeze(1).broadcast_to([P, KT, w]), ALU.mult),
                       t, ready, list(dst_free))
        else:
            for k in range(KT):
                t2 = dve.do(lambda e: e.scalar_tensor_tensor(dst[:, k, c], base[:, k, c], weight[:, k:k + 1],
                                                             inv[:, b], ALU.mult, ALU.mult),
                            t, ready, list(dst_free))
            t = t2
        out = [t]
        if split:
            hi, lo = split
            th = act.do(lambda e: e.activation(hi[:, :, c], dst[:, :, c], ACT.Copy), t)
            tl = dve.do(lambda e: e.tensor_tensor(lo[:, :, c], dst[:, :, c], fr(hi[:, :, c]), ALU.subtract), th)
            out += [th, tl]
        done.append(out)
    return done


def matmul3(lane, out, pairs, *tokens, start=True, stop=True, signal=True):
    passes = []
    for lh, ll, rh, rl in pairs:
        passes.append((lh, rh))
        if ll is not None:
            passes.append((ll, rh))
        if rl is not None:
            passes.append((lh, rl))
    for n, (a, b) in enumerate(passes):
        last = n == len(passes) - 1
        t = lane.do(lambda e: e.matmul(out, a, b, start=start and n == 0, stop=stop and last, skip_group_check=True),
                    *(tokens if n == 0 else ()), signal=signal and last)
    return t


class Item:

    def __init__(self, at, multiply, empty):
        self.at, self.multiply, self.empty = at, multiply, empty


ORDER = (0, 7, 1, 6, 2, 5, 3, 4)
SIDE = (6, 7, 1)
NPROB = 3
LAG = 4


def side_bank(g):
    b = SIDE[g.side % 3]
    g.side += 1
    return b, g.ps[:, b, :], g.pr.readers.get(f"side{b}")


class Softmax:

    def __init__(self, g, groups, heads, score_passes, value_passes, take_output, both=False):
        self.g, self.pr, self.both = g, g.pr, both
        self.score_passes, self.value_passes, self.take_output = score_passes, value_passes, take_output
        self.units = [(gr, h, i) for gr in range(groups) for h in range(heads) for i in ORDER]
        self.prob_ready, self.exp_done, self.pT_ready, self.turned, self.hi_done = {}, {}, {}, {}, {}
        self.chunk = 0

    def scores(self, u):
        g, pe, rd = self.g, self.pr.pe, self.pr.readers
        gr, h, i = self.units[u]
        bank, width, key = 2 * (u % 2), (i + 1) * P, f"scores{u % 2}"
        for c in range(0, width, HALF):
            n = min(HALF, width - c)
            matmul3(pe, g.ps[:, bank + c // HALF, 0:n], self.score_passes(gr, h, i, slice(c, c + n)),
                    rd.get(f"ready{gr % 2}"), rd.get(key), stop=(c + n != width), signal=False)
        d = width - P
        t = pe.do(lambda e: e.matmul(g.ps[:, bank + d // HALF, d % HALF:d % HALF + P], g.ident_r[:], g.mask_r[:],
                                     start=False, stop=True, skip_group_check=True))
        rd[f"scored{gr % 2}"] = [t]
        return t

    def maximum(self, u, t):
        g, rd = self.g, self.pr.readers
        bank, width, slot = 2 * (u % 2), (self.units[u][2] + 1) * P, u % NPROB
        src = g.ps_flat[:, bank * HALF:bank * HALF + width]
        return self.pr.dve.do(lambda e: e.tensor_reduce(g.negmax[:, slot:slot + 1], src, AX.X, ALU.max, negate=True),
                              t, rd.get(f"prob{slot}"))

    def exponential(self, u, t):
        g, rd = self.g, self.pr.readers
        bank, width, slot = 2 * (u % 2), (self.units[u][2] + 1) * P, u % NPROB
        src = g.ps_flat[:, bank * HALF:bank * HALF + width]
        te = self.pr.act.do(lambda e: e.activation(g.prob[:, slot, 0:width], src, ACT.Exp, bias=g.negmax[:, slot:slot + 1],
                                                   accum_out=g.rowsum[:, slot:slot + 1]), t, rd.get(f"prob{slot}"))
        rd[f"scores{u % 2}"] = [te]
        self.exp_done[u] = te

    def divide(self, u):
        g = self.g
        width, slot = (self.units[u][2] + 1) * P, u % NPROB
        inv, prob = g.rowinv[:, slot:slot + 1], g.prob[:, slot, 0:width]
        ti = self.pr.dve.do(lambda e: e.reciprocal(inv, g.rowsum[:, slot:slot + 1]), self.exp_done[u],
                            self.pr.readers.get(f"prob{slot}"))
        self.prob_ready[u] = self.pr.pool.do(lambda e: e.tensor_scalar(prob, prob, inv, 1.0, ALU.mult, ALU.mult), ti)

    def transposes(self, u):
        g, rd = self.g, self.pr.readers
        i, slot = self.units[u][2], u % NPROB
        self.turned[u] = []
        for j0 in range(0, i + 1, 4):
            n, b = min(4, i + 1 - j0), 4 + self.chunk % 2
            self.chunk += 1
            for j in range(n):
                t = self.pr.pe.do(lambda e: e.transpose(g.ps[:, b, j * P:j * P + P],
                                                        g.prob[:, slot, (j0 + j) * P:(j0 + j + 1) * P], g.ident[:]),
                                  self.prob_ready[u], rd.get(f"bank{b}"), signal=(j == n - 1))
            self.turned[u].append((j0, n, b, t))
        rd[f"prob{slot}"] = [t]

    def split_parts(self, u):
        g, i = self.g, self.units[u][2]
        qb, cols = i // 4, slice(i % 4 * P, i % 4 * P + P)
        for j0, n, b, t in self.turned[u]:
            src = g.ps[:, b, 0:n * P].rearrange("p (j q) -> p j q", j=n)
            yield b, src, g.pT_hi[qb][:, j0:j0 + n, cols], g.pT_lo[qb][:, j0:j0 + n, cols], t

    def split_hi(self, u):
        free = self.pr.readers.get(f"pT{self.units[u][2] // 4}")
        self.hi_done[u] = [self.pr.act.do(lambda e: e.activation(hi, src, ACT.Copy), t, free)
                           for b, src, hi, lo, t in self.split_parts(u)]

    def split_lo(self, u):
        gr, h, i = self.units[u]
        rd = self.pr.readers
        free = rd.get(f"pT{i // 4}")
        for (b, src, hi, lo, t), th in zip(self.split_parts(u), self.hi_done[u]):
            tl = self.pr.dve.do(lambda e: e.tensor_tensor(lo, src, fr(hi), ALU.subtract), th, free)
            rd[f"bank{b}"] = [th, tl]
            self.pT_ready.setdefault((gr, h, i // 4), []).extend([th, tl])

    def values(self, gr, h, qb):
        g, pe, rd = self.g, self.pr.pe, self.pr.readers
        tiles = 4 * qb + 4
        bank, out, free = side_bank(g)
        tokens = [self.pT_ready[gr, h, qb], free, rd.get(f"ready{gr % 2}")]
        for j in range(tiles):
            q = max(0, j - 4 * qb) * P
            passes = self.value_passes(gr, h, j, g.pT_hi[qb][:, j, q:HALF], g.pT_lo[qb][:, j, q:HALF])
            for n, (a, b) in enumerate(passes):
                end = j == tiles - 1 and n == len(passes) - 1
                t = pe.do(lambda e: e.matmul(out[:, q:HALF], a, b, start=(j == 0 and n == 0), stop=end,
                                             skip_group_check=True), *tokens, signal=end)
                tokens = []
        rd[f"pT{qb}"] = rd[f"attended{gr % 2}"] = [t]

        def empty():
            for free in self.take_output(gr, h, qb, out, t):
                if free:
                    rd[f"side{bank}"] = free
                yield

        return empty

    def run(self, items):
        n, items, due, s, scored = len(self.units), list(items), [], 0, {}
        new, old = [], []
        self.g.side = 0
        while s < n + LAG or due or items or new or old:
            if s < n:
                scored[s] = self.scores(s)
            old, new = new, []
            late = [e for e in old if next(e, self) is not self]
            if LAG <= s < n + LAG:
                self.split_hi(s - LAG)
            if 1 <= s <= n:
                self.exponential(s - 1, self.maximum(s - 1, scored[s - 1]))
            if 2 <= s <= n + 1:
                self.divide(s - 2)
            if LAG <= s < n + LAG:
                self.split_lo(s - LAG)
            old = [e for e in late if next(e, self) is not self]
            if due:
                new.append(self.values(*due.pop(0))())
            if items and items[0].at <= s and (self.both or not new):
                it = items.pop(0)
                it.multiply()
                new.append(it.empty())
            if 3 <= s <= n + 2:
                self.transposes(s - 3)
            if LAG <= s < n + LAG:
                gr, h, i = self.units[s - LAG]
                if i in (3, 4):
                    due.append((gr, h, i // 4))
            new = old + new
            s += 1


def softmax_buffers(g, tag):
    pr = g.pr
    g.prob = pr.sb(tag + "prob", [P, NPROB, N])
    g.negmax = pr.sb(tag + "negmax", [P, NPROB])
    g.rowsum = pr.sb(tag + "rowsum", [P, NPROB])
    g.rowinv = pr.sb(tag + "rowinv", [P, NPROB])
    g.pT_hi = [pr.sb(f"{tag}pT_hi{qb}", [P, 4 * qb + 4, HALF], F32R) for qb in range(NH2)]
    g.pT_lo = [pr.sb(f"{tag}pT_lo{qb}", [P, 4 * qb + 4, HALF], F32R) for qb in range(NH2)]


def project_out(g, wo, oT, tiles, at, tokens, name="oT"):
    pr = g.pr
    rd = pr.readers

    def item(m, qb):
        cc, mm = slice(qb * HALF, qb * HALF + HALF), slice(m * P, m * P + P)
        t = []

        def multiply():
            t.extend(side_bank(g))
            t.append(matmul3(pr.pe, t[1], [(wo[0][:, k, mm], wo[1][:, k, mm], oT[0][:, k, cc], oT[1][:, k, cc])
                                                       for k in range(tiles)], t[2], rd.get("o_split"), tokens))
            if (m, qb) == (KT - 1, NH2 - 1):
                rd[name] = rd["wo"] = [t[3]]

        def empty():
            yield
            tx = pr.dve.do(lambda e: e.tensor_tensor(g.x[:, m, cc], g.x[:, m, cc], t[1], ALU.add), t[3],
                           rd.get(f"x{m}{qb}"))
            rd[f"side{t[0]}"] = rd[f"x{m}{qb}"] = [tx]

        return Item(at, multiply, empty)

    return [item(m, qb) for m in range(KT) for qb in range(NH2)]


def pool_split(g, hi, lo, src, *tokens):
    a = g.pr.pool.do(lambda e: e.tensor_scalar(hi, src, 1.0, 1.0, ALU.mult, ALU.mult), *tokens)
    return g.pr.pool.do(lambda e: e.tensor_tensor(lo, src, fr(hi), ALU.subtract), a)


A_HEADS, A_KV, A_HD = 32, 8, 64
A_GRP = A_HEADS // A_KV
A_W = (A_GRP + 2) * A_HD


def attn_a(g, ins):
    pr = g.pr
    pe, dve, act, pool, sp, rd = pr.pe, pr.dve, pr.act, pr.pool, pr.sp, pr.readers
    with pr.phase():
        h_hi, h_lo = pr.sb("a_h_hi", [P, KT, N], F32R), pr.sb("a_h_lo", [P, KT, N], F32R)
        cos, sin = pr.sb("a_cos", [P, TT, A_HD]), pr.sb("a_sin", [P, TT, A_HD])
        w_raw, o_raw = pr.sb("a_w_raw", [P, KT, A_W]), pr.sb("a_o_raw", [P, 2, D])
        w_hi, w_lo = pr.sb("a_w_hi", [P, KT, A_W], F32R), pr.sb("a_w_lo", [P, KT, A_W], F32R)
        o_hi, o_lo = pr.sb("a_o_hi", [P, 2, D], F32R), pr.sb("a_o_lo", [P, 2, D], F32R)
        s_tab, s_w, s_o = pr.slot("a_tables"), pr.slot("a_w_loaded"), pr.slot("a_o_loaded")
        sp.dma(s_tab, lambda: cos[:], lambda: ins["a_cos"])
        sp.dma(s_tab, lambda: sin[:], lambda: ins["a_sin"])
        first = sp.dma(s_w, lambda: w_raw[:], lambda: ins["a_w"][0])
        sp.dma(s_o, lambda: o_raw[:], lambda: ins["a_o"][0])
        w_first = pool_split(g, w_hi[:], w_lo[:], w_raw[:], first)
        sp.dma(s_w, lambda: w_raw[:], lambda: ins["a_w"][1], w_first)
        with pr.phase():
            h = pr.sb("a_h", [P, KT, N])
            normalise(g, "a_n", g.x, h, N, 1e-5, src_ready=g.x_ready, centre=True, split=(h_hi, h_lo))

        two = range(2)
        q_st = [pr.sb(f"a_q{b}", [P, A_GRP, N], F32R) for b in two]
        k_hi = [pr.sb(f"a_k_hi{b}", [P, N], F32R) for b in two]
        k_lo = [pr.sb(f"a_k_lo{b}", [P, N], F32R) for b in two]
        v_st = [pr.sb(f"a_v{b}", [P, TT, 2 * A_HD], F32R) for b in two]
        t1, t2 = pr.sb("a_t1", [P, 2, (A_GRP + 1) * A_HD]), pr.sb("a_t2", [P, 2, (A_GRP + 1) * A_HD])
        qk = pr.sb("a_qk", [P, TT, A_W])
        o_low, o_sum = pr.sb("a_o_low", [P, HALF]), pr.sb("a_o_sum", [P, 2, HALF])
        oT_hi, oT_lo = pr.sb("a_oT_hi", [P, 2, N], F32R), pr.sb("a_oT_lo", [P, 2, N], F32R)
        softmax_buffers(g, "a_")
        heads, HH = A_GRP + 1, A_HD // 2
        rows = (slice(0, 64), slice(64, 128))

        def make_qkv(b, at, next_w):
            ready, qk_ready = [], {}

            def token_tile(t):
                par, tok, tp = t % 2, slice(t * P, t * P + P), []

                def multiply():
                    rd[f"ready{b}"] = ready
                    tp.extend(side_bank(g))
                    tp.append(matmul3(pe, tp[1][:, 0:A_W], [(h_hi[:, k, tok], h_lo[:, k, tok], w_hi[:, k], w_lo[:, k])
                                                            for k in range(KT)], rd.get("w_split"), tp[2]))

                def empty():
                    bank, out, _, made = tp
                    x3 = out[:, 0:heads * A_HD].rearrange("p (h d) -> p h d", d=A_HD)
                    c3 = cos[:, t].unsqueeze(1).broadcast_to([P, heads, A_HD])
                    s_low = sin[:, t, 0:HH].unsqueeze(1).broadcast_to([P, heads, HH])
                    s_high = sin[:, t, HH:].unsqueeze(1).broadcast_to([P, heads, HH])
                    r1, r2 = (x[:, par].rearrange("p (h d) -> p h d", d=A_HD) for x in (t1, t2))
                    vs, v = out[:, heads * A_HD:A_W], v_st[b]
                    vh = act.do(lambda e: e.activation(v[:, t, 0:A_HD], vs, ACT.Copy), made, rd.get(f"attended{b}"))
                    yield
                    a1 = dve.do(lambda e: e.tensor_tensor(r1, x3, c3, ALU.mult), vh, rd.get(f"rope{par}"))
                    dve.do(lambda e: e.tensor_tensor(r2[:, :, 0:HH], x3[:, :, HH:], s_low, ALU.mult))
                    a3 = dve.do(lambda e: e.tensor_tensor(r2[:, :, HH:], x3[:, :, 0:HH], s_high, ALU.mult))
                    vl = dve.do(lambda e: e.tensor_tensor(v[:, t, A_HD:], vs, fr(v[:, t, 0:A_HD]), ALU.subtract), vh)
                    pool.do(lambda e: e.tensor_tensor(qk[:, t, 0:heads * A_HD], t1[:, par], t2[:, par], ALU.add),
                            a1, a3, rd.get("qk"))
                    a5 = pool.do(lambda e: e.tensor_tensor(qk[:, t, heads * A_HD:], t1[:, par, A_GRP * A_HD:],
                                                           t2[:, par, A_GRP * A_HD:], ALU.add))
                    rd[f"rope{par}"], rd[f"side{bank}"], qk_ready[t] = [a5], [vl, vh], a5
                    ready.extend([vh, vl])
                    if t == TT - 1:
                        loaded = Token(s_w, s_w.n, pr.loop)
                        rd["w_split"] = [pool_split(g, w_hi[:], w_lo[:], w_raw[:], loaded, made)]
                        sp.dma(s_w, lambda: w_raw[:],
                               lambda: ins["a_w"][bass.ds(next_w(), 1)].rearrange("o p a b -> (o p) a b"), rd["w_split"])

                return Item(at, multiply, empty)

            def turned(c, pair):
                cc, tp = slice(c * HALF, c * HALF + HALF), []

                def multiply():
                    tp.extend(side_bank(g))
                    for t in range(4):
                        tt = c * 4 + t
                        x = pe.do(lambda e: e.transpose(tp[1][:, t * P:t * P + P], qk[:, tt, pair * P:pair * P + P], g.ident[:]),
                                  qk_ready[tt], tp[2], signal=(t == 3))
                    tp.append(x)
                    rd["qk"] = [x]

                def empty():
                    bank, out, _, made = tp
                    free = rd.get(f"attended{b}")
                    if pair < 2:
                        parts = [(q_st[b][:, 2 * pair + e2], rows[e2], rows[1 - e2]) for e2 in range(2)]
                        hi = [act.do(lambda e: e.activation(q[mine, cc], out[mine], ACT.Copy, scale=A_HD ** -0.5), made, free)
                              for q, mine, other in parts]
                        yield
                        lo = [dve.do(lambda e: e.scalar_tensor_tensor(q[other, cc], out[mine], A_HD ** -0.5, fr(q[mine, cc]),
                                                                      ALU.mult, ALU.subtract), hi, free)
                              for q, mine, other in parts]
                        used = hi + lo
                    else:
                        kh, kl = k_hi[b], k_lo[b]
                        hi = act.do(lambda e: e.activation(kh[:, cc], out, ACT.Copy), made, free)
                        yield
                        lo = dve.do(lambda e: e.tensor_tensor(kl[:, cc], out, fr(kh[:, cc]), ALU.subtract), hi, free)
                        used = [hi, lo]
                    rd[f"side{bank}"] = used
                    ready.extend(used)

                return Item(at, multiply, empty)

            return [token_tile(t) for t in range(TT)] + [turned(c, pair) for c in range(NH2) for pair in range(3)]

        def split_o(next_o):
            loaded = Token(s_o, s_o.n, pr.loop)
            rd["o_split"] = [pool_split(g, o_hi[:], o_lo[:], o_raw[:], loaded, rd.get("wo"))]
            sp.dma(s_o, lambda: o_raw[:], lambda: ins["a_o"][bass.ds(next_o(), 1)].rearrange("o p a b -> (o p) a b"),
                   rd["o_split"])

        def score_passes(b, hd, t, keys):
            q = q_st[b][:, hd, t * P:t * P + P]
            return [(q, None, k_hi[b][:, keys], None), (q, None, k_lo[b][:, keys], None)]

        def value_passes(b, hd, j, hi, lo):
            return [(v_st[b][:, j], hi), (v_st[b][:, j], lo)]

        def take_output(b, hd, qb, out, t):
            pair, half, cc = hd // 2, rows[hd % 2], slice(qb * HALF, qb * HALF + HALF)
            low = act.do(lambda e: e.activation(o_low[64:128], out[64:128], ACT.Copy), t, rd.get("o_low"))
            yield
            tot = dve.do(lambda e: e.tensor_tensor(o_sum[half, qb], out[0:64], o_low[64:128], ALU.add), low,
                         rd.get(f"o_sum{qb}"))
            rd["o_low"] = [tot]
            yield [tot]
            if hd % 2 == 1:
                hi = act.do(lambda e: e.activation(oT_hi[:, pair, cc], o_sum[:, qb], ACT.Copy), tot, rd.get("oT"))
                yield
                lo = pool.do(lambda e: e.tensor_tensor(oT_lo[:, pair, cc], o_sum[:, qb], fr(oT_hi[:, pair, cc]), ALU.subtract),
                             hi, rd.get("oT"))
                rd[f"o_sum{qb}"] = [hi, lo]
                out_ready[b] += [hi, lo]

        out_ready = {}
        units = A_GRP * TT
        after = LAG + 5

        def turn(i):
            out_ready[0], out_ready[1] = [], []
            wo, oT = (o_hi, o_lo), (oT_hi, oT_lo)

            def out_items(b, at):
                items = project_out(g, wo, oT, 2, at, out_ready[b])
                return items

            split_o(lambda: (2 * i + 1) % A_KV)
            items = make_qkv(1, 1, lambda: (2 * i + 3) % A_KV)
            out0 = out_items(0, units + after)
            last = out0[-1].multiply

            def last_then_split():
                last()
                split_o(lambda: (2 * i + 2) % A_KV)

            out0[-1].multiply = last_then_split
            items += out0
            items += make_qkv(0, units + after, lambda: (2 * i + 4) % A_KV)
            items += out_items(1, 2 * units + after)
            Softmax(g, 2, A_GRP, score_passes, value_passes, take_output).run(items)

        pr.fence()
        g.side = 0
        for it in make_qkv(0, 0, lambda: 2):
            it.multiply()
            list(it.empty())
        pr.run_loop(A_KV // 2, turn)


B_HEADS, B_HD = 16, 128
B_PAIR = 2
B_TURN = 4
B_SCALE = 1.0 / math.sqrt(B_HD)


def attn_b(g, ins):
    pr = g.pr
    pe, dve, act, pool, sp, rd = pr.pe, pr.dve, pr.act, pr.pool, pr.sp, pr.readers
    with pr.phase():
        h_hi, h_lo = pr.sb("b_h_hi", [P, KT, N], F32R), pr.sb("b_h_lo", [P, KT, N], F32R)
        w_raw, o_raw = pr.sb("b_w_raw", [P, KT, 3 * B_HD]), pr.sb("b_o_raw", [P, B_PAIR, D])
        w_hi, w_lo = pr.sb("b_w_hi", [P, KT, 3 * B_HD], F32R), pr.sb("b_w_lo", [P, KT, 3 * B_HD], F32R)
        o_hi, o_lo = pr.sb("b_o_hi", [P, B_PAIR, D], F32R), pr.sb("b_o_lo", [P, B_PAIR, D], F32R)
        bias = pr.sb("b_bias", [P, 3, B_HEADS])
        bias_qk, bias_v = pr.sb("b_bias_qk", [P, 2, 2]), pr.sb("b_bias_v", [P, 2])
        b_out = pr.sb("b_bias_out", [P, KT])
        s_b, s_w, s_o = pr.slot("b_bias_loaded"), pr.slot("b_w_loaded"), pr.slot("b_o_loaded")
        sp.dma(s_b, lambda: bias[:], lambda: ins["b_bias"])
        biases = sp.dma(s_b, lambda: b_out[:], lambda: ins["b_bias_out"])
        first = sp.dma(s_w, lambda: w_raw[:], lambda: ins["b_w"][0])
        sp.dma(s_o, lambda: o_raw[:], lambda: ins["b_o"][0])

        def split_w(*tokens):
            q = w_raw[:, :, 0:B_HD]
            a = pool.do(lambda e: e.tensor_scalar(q, q, B_SCALE, 1.0, ALU.mult, ALU.mult), *tokens)
            return pool_split(g, w_hi[:], w_lo[:], w_raw[:], a)

        w_first = split_w(first)
        sp.dma(s_w, lambda: w_raw[:], lambda: ins["b_w"][1], w_first)
        with pr.phase():
            h = pr.sb("b_h", [P, KT, N])
            normalise(g, "b_n", g.x, h, N, 1e-5, src_ready=g.x_ready, centre=True, split=(h_hi, h_lo))
            act.do(lambda e: e.activation(bias[:, 0], bias[:, 0], ACT.Copy, scale=B_SCALE), biases)
            for k in range(KT):
                dve.do(lambda e: e.tensor_scalar(g.x[:, k], g.x[:, k], b_out[:, k:k + 1], None, ALU.add), biases, dve.last())

        two = range(2)
        q_hi, q_lo, k_hi, k_lo = ([pr.sb(f"b_{n}{b}", [P, N], F32R) for b in two] for n in ("q_hi", "q_lo", "k_hi", "k_lo"))
        v_hi, v_lo = ([pr.sb(f"b_{n}{b}", [P, TT, B_HD], F32R) for b in two] for n in ("v_hi", "v_lo"))
        oT_hi, oT_lo = ([pr.sb(f"b_{n}{b}", [P, B_PAIR, N], F32R) for b in two] for n in ("oT_hi", "oT_lo"))
        softmax_buffers(g, "b_")

        def make_qkv(b, at, head, next_w):
            ready = []

            def take_bias(dst, which, name, free):
                src = lambda: bias[:, which, bass.ds(head(), 1)].rearrange("p a o -> p (a o)")
                rd[f"{name}{b}"] = [act.do(lambda e: e.activation(dst, src(), ACT.Copy), rd.get(f"{free}{b}"))]

            def qk_half(which, c):
                hi_t, lo_t = ((q_hi, q_lo), (k_hi, k_lo))[which]
                cc = slice(c * HALF, c * HALF + HALF)
                col, tp = slice(which * B_HD, (which + 1) * B_HD), []

                def multiply():
                    rd[f"ready{b}"] = ready
                    tp.extend(side_bank(g))
                    tp.append(matmul3(pe, tp[1], [(w_hi[:, k, col], w_lo[:, k, col], h_hi[:, k, cc], h_lo[:, k, cc])
                                                  for k in range(KT)], rd.get("w_split"), tp[2]))

                def empty():
                    bank, out, _, made = tp
                    if (which, c) == (0, 0):
                        take_bias(bias_qk[:, b], slice(0, 2), "bias", "biased")
                    bb, free = bias_qk[:, b, which:which + 1], rd.get(f"scored{b}")
                    hi = act.do(lambda e: e.activation(hi_t[b][:, cc], out, ACT.Identity, bias=bb), made,
                                rd[f"bias{b}"], free)
                    yield
                    lo = dve.do(lambda e: e.scalar_tensor_tensor(lo_t[b][:, cc], out, bb, fr(hi_t[b][:, cc]),
                                                                 ALU.add, ALU.subtract), hi, free)
                    rd[f"side{bank}"] = rd[f"biased{b}"] = [lo]
                    ready.extend([hi, lo])

                return Item(at, multiply, empty)

            def v_tiles(t0):
                tp = []

                def multiply():
                    tp.extend(side_bank(g))
                    for j in range(4):
                        tok = slice((t0 + j) * P, (t0 + j + 1) * P)
                        x = matmul3(pe, tp[1][:, j * B_HD:(j + 1) * B_HD],
                                    [(h_hi[:, k, tok], h_lo[:, k, tok], w_hi[:, k, 2 * B_HD:], w_lo[:, k, 2 * B_HD:])
                                     for k in range(KT)], tp[2])
                    tp.append(x)

                def empty():
                    bank, out, _, made = tp
                    free = rd.get(f"attended{b}")
                    vh, vl = (x[b][:, t0:t0 + 4].rearrange("p t n -> p (t n)") for x in (v_hi, v_lo))
                    hi = act.do(lambda e: e.activation(vh, out, ACT.Copy), made, free)
                    if t0 == 0:
                        take_bias(bias_v[:, b:b + 1], slice(2, 3), "v_bias", "v_biased")
                    yield
                    lo = dve.do(lambda e: e.tensor_tensor(vl, out, fr(vh), ALU.subtract), hi, free)
                    rd[f"side{bank}"] = [lo]
                    ready.extend([hi, lo])
                    if t0 == TT - 4:
                        loaded = Token(s_w, s_w.n, pr.loop)
                        rd["w_split"] = [split_w(loaded, made)]
                        sp.dma(s_w, lambda: w_raw[:],
                               lambda: ins["b_w"][bass.ds(next_w(), 1)].rearrange("o p a b -> (o p) a b"), rd["w_split"])

                return Item(at + LAG + 1, multiply, empty)

            return ([qk_half(which, c) for which in range(2) for c in range(NH2)]
                    + [v_tiles(t0) for t0 in range(0, TT, 4)])

        def split_o(next_o, loaded):
            rd["o_split"] = [pool_split(g, o_hi[:], o_lo[:], o_raw[:], loaded, rd.get("wo"))]
            sp.dma(s_o, lambda: o_raw[:], lambda: ins["b_o"][bass.ds(next_o(), 1)].rearrange("o p a b -> (o p) a b"),
                   rd["o_split"])

        def score_passes(hd, _, t, keys):
            b, tok = hd % 2, slice(t * P, t * P + P)
            return [(q_hi[b][:, tok], q_lo[b][:, tok], k_hi[b][:, keys], k_lo[b][:, keys])]

        def value_passes(hd, _, j, hi, lo):
            vh, vl = v_hi[hd % 2][:, j], v_lo[hd % 2][:, j]
            return [(vh, hi), (vh, lo), (vl, hi)]

        def take_output(hd, _, qb, out, t):
            cc, bb = slice(qb * HALF, qb * HALF + HALF), bias_v[:, hd % 2:hd % 2 + 1]
            pair, e2 = hd // B_PAIR % 2, hd % B_PAIR
            o, ol = oT_hi[pair][:, e2, cc], oT_lo[pair][:, e2, cc]
            hi = act.do(lambda e: e.activation(o, out, ACT.Identity, bias=bb), t, rd.get(f"oT{pair}"), rd.get(f"v_bias{hd % 2}"))
            yield
            lo = dve.do(lambda e: e.scalar_tensor_tensor(ol, out, bb, fr(o), ALU.add, ALU.subtract), hi, rd.get(f"oT{pair}"))
            rd[f"v_biased{hd % 2}"] = [lo]
            out_ready[hd // B_PAIR] += [hi, lo]
            yield [lo]

        out_ready = {}

        def turn(i):
            items, pairs = [], B_TURN // B_PAIR
            for hd in range(B_TURN):
                items += make_qkv((hd + 1) % 2, hd * TT, lambda hd=hd: (B_TURN * i + hd + 1) % B_HEADS,
                                  lambda hd=hd: (B_TURN * i + hd + 3) % B_HEADS)
            for p in range(pairs):
                out_ready[p] = []
                done = (p + 1) * B_PAIR * TT + LAG + 3
                wo = project_out(g, (o_hi, o_lo), (oT_hi[p % 2], oT_lo[p % 2]), B_PAIR, done, out_ready[p], f"oT{p % 2}")
                wo[2].at = wo[3].at = done + TT // 2 + 1

                def last_then_split(p=p, last=wo[-1].multiply):
                    last()
                    split_o(lambda: (pairs * i + p + 2) % (B_HEADS // B_PAIR), Token(s_o, s_o.n, pr.loop))

                wo[-1].multiply = last_then_split
                items += wo
            Softmax(g, B_TURN, 1, score_passes, value_passes, take_output, both=True).run(sorted(items, key=lambda it: it.at))

        split_o(lambda: 1, Token(s_o, s_o.n, None))
        pr.fence()
        g.side = 0
        for it in make_qkv(0, 0, lambda: 0, lambda: 2):
            it.multiply()
            list(it.empty())
        pr.run_loop(B_HEADS // B_TURN, turn)


F_HEADS, F_KV, F_HD, F_I = 16, 8, 128, 1024
F_S = int(N * 0.125)
F_SCALE = 1.0 / math.sqrt(F_HD)
FI_T = F_I // P


def ffn(g, ins, tag):
    assert F_S == P
    pr = g.pr
    pe, dve, act, pool, sp = pr.pe, pr.dve, pr.act, pr.pool, pr.sp
    ps = g.ps
    with pr.phase():
        def sb(name, shape, dt=F32):
            return pr.sb(f"{tag}_{name}", shape, dt)

        def load(name, shape):
            buf, slot = sb(name, shape), pr.slot(f"{tag}_{name}_loaded")
            return buf, sp.dma(slot, lambda: buf[:], lambda: ins["f_" + name])

        wr, l_wr = load("wr", [P, KT])
        trope, l_trope = load("rope", [P, TT, 2, P])
        ln, l_ln = load("ln", [P, 2, KT])
        bqk, l_bqk = load("bqk", [P, F_HEADS + F_KV])
        bv, l_bv = load("bv", [1, F_KV * F_HD])
        wq, l_wq = load("wq", [P, KT, F_HEADS * F_HD])
        wk, l_wk = load("wk", [P, KT, F_KV * F_HD])
        wv, l_wv = load("wv", [P, KT, F_KV * F_HD])
        wo, l_wo = load("wo", [P, F_HEADS, D])
        wg, l_wg = load("wg", [P, KT, F_I])
        wu, l_wu = load("wu", [P, KT, F_I])
        wd, l_wd = load("wd", [P, FI_T, D])

        tri, upper, ramp, ones = sb("tri", [P, P]), sb("upper", [P, P]), sb("ramp", [P, P]), sb("ones", [P, P])
        c0 = pool.do(lambda e: e.memset(tri[:], 1.0))
        c1 = pool.do(lambda e: e.memset(upper[:], 1.0))
        tri_t = pool.do(lambda e: e.affine_select(out=tri[:], in_=tri[:], compare_op=ALU.is_ge, fill=0.0, base=-1,
                                                  pattern=[[-1, P]], channel_multiplier=1), c0)
        upper_t = pool.do(lambda e: e.affine_select(out=upper[:], in_=upper[:], compare_op=ALU.is_ge, fill=0.0, base=-1,
                                                    pattern=[[1, P]], channel_multiplier=-1), c1)
        ramp_t = pool.do(lambda e: e.iota(ramp[:], pattern=[[1, P]], base=0, channel_multiplier=0,
                                          allow_small_or_imprecise_dtypes=True))
        ones_t = pool.do(lambda e: e.memset(ones[:], 1.0))

        h = sb("h", [P, KT, N])
        hn = normalise(g, f"{tag}_n0", g.x, h, N, 1e-5, centre=True)
        h_ready = [o[0] for o in hn]
        x_plus = pool.do(lambda e: e.tensor_tensor(g.x[:], g.x[:], h[:], ALU.add), h_ready)

        wrb = sb("wrb", [P, KT, P])
        t = dve.do(lambda e: e.tensor_copy(wrb[:], wr[:, :].unsqueeze(2).broadcast_to([P, KT, P])), l_wr)
        for c in range(NH2):
            for k in range(KT):
                s_mm = pe.do(lambda e: e.matmul(ps[:, 4 + c, :], wrb[:, k], h[:, k, c * HALF:(c + 1) * HALF],
                                                start=(k == 0), stop=(k == KT - 1)), t, h_ready)
        s = sb("s", [P, N])
        s_t = dve.do(lambda e: e.tensor_copy(s[:], g.ps_flat[:, 4 * HALF:6 * HALF]), s_mm)
        h_tok = sb("h_tok", [P, TT, D])
        h_tok_t = []
        for b in range(4):
            for j in range(4):
                c, k = 2 * b + j // 2, j % 2
                t = pe.do(lambda e: e.transpose(ps[:, b, j * P:j * P + P], h[:, k, c * P:c * P + P], g.ident[:]), h_ready)
            h_tok_t.append(act.do(lambda e: e.activation(h_tok[:, 2 * b:2 * b + 2].rearrange("p a b -> p (a b)"), ps[:, b, :],
                                                         ACT.Copy), t))
        diag, s_col = sb("diag", [P, TT, P]), sb("s_col", [P, TT])
        t = dve.do(lambda e: e.tensor_tensor(diag[:], s[:, :].rearrange("p (c q) -> p c q", q=P),
                                             g.ident[:].unsqueeze(1).broadcast_to([P, TT, P]), ALU.mult), s_t)
        t = dve.do(lambda e: e.tensor_reduce(s_col[:], diag[:], AX.X, ALU.add), t)
        junk, cnt = diag[:, :, :].rearrange("p c q -> p (c q)"), sb("cnt", [P, TT, 4])
        z = dve.do(lambda e: e.memset(cnt[:], 0.0))
        for c in range(TT):
            own, lo, up = s_col[:, c:c + 1], c * P, N - c * P
            if c:
                t = dve.do(lambda e: e.tensor_scalar(junk[:, 0:lo], s[:, 0:lo], own, None, ALU.is_ge, ALU.add,
                                                     accum_out=cnt[:, c, 0:1]), t, z)
            t = dve.do(lambda e: e.tensor_scalar(junk[:, lo:N], s[:, lo:N], own, None, ALU.is_gt, ALU.add,
                                                 accum_out=cnt[:, c, 1:2]), t, z)
            t = dve.do(lambda e: e.scalar_tensor_tensor(junk[:, lo:lo + P], s[:, lo:lo + P], own, tri[:],
                                                        ALU.is_equal, ALU.mult, accum_out=cnt[:, c, 2:3]), t, tri_t)
        rank, sel = sb("rank", [P, TT]), sb("sel", [P, TT])
        t = dve.do(lambda e: e.tensor_reduce(rank[:], cnt[:], AX.X, ALU.add), t)
        sel_t = dve.do(lambda e: e.tensor_scalar(sel[:], rank[:], F_S - 0.5, None, ALU.is_lt), t)
        within, total = ps[:, 6, 0:TT], ps[:, 7, 0:TT]
        t1 = pe.do(lambda e: e.matmul(within, upper[:], sel[:], start=True, stop=True), sel_t, upper_t)
        t2 = pe.do(lambda e: e.matmul(total, ones[:], sel[:], start=True, stop=True), ones_t)
        upto, pos = sb("upto", [P, TT]), sb("pos", [P, TT])
        t = dve.do(lambda e: e.tensor_tensor_scan(upto[:], ones[:, 0:TT], total, 0.0, ALU.mult, ALU.add), t2)
        t = dve.do(lambda e: e.tensor_tensor(upto[:], upto[:], total, ALU.subtract), t)
        t = dve.do(lambda e: e.tensor_tensor(pos[:], upto[:], within, ALU.add), t)
        take = sb("take", [P, TT, P])
        for c in range(TT):
            take_t = dve.do(lambda e: e.tensor_scalar(take[:, c], ramp[:], pos[:, c:c + 1], sel[:, c:c + 1],
                                                      ALU.is_equal, ALU.mult), t, ramp_t)
        t = None
        for m in range(4):
            for c in range(TT):
                lhs = h_tok[:, c, m * P:m * P + P] if m < 2 else trope[:, c, m - 2]
                t = pe.do(lambda e: e.matmul(ps[:, 0, m * P:m * P + P], lhs, take[:, c], start=(c == 0), stop=(c == TT - 1)),
                          take_t, h_tok_t, l_trope)
        xs, rope = sb("xs", [P, KT, P]), sb("ropes", [P, 2, P])
        flat2 = "p a b -> p (a b)"
        xs_t = dve.do(lambda e: e.tensor_copy(xs[:, :].rearrange(flat2), ps[:, 0, 0:2 * P]), t)
        rope_t = dve.do(lambda e: e.tensor_copy(rope[:, :].rearrange(flat2), ps[:, 0, 2 * P:]))
        takeT = sb("takeT", [P, N])
        for b in range(2):
            for j in range(4):
                t = pe.do(lambda e: e.transpose(ps[:, 1 + b, j * P:j * P + P], take[:, 4 * b + j], g.ident[:]), h_tok_t)
            takeT_t = act.do(lambda e: e.activation(takeT[:, b * HALF:(b + 1) * HALF], ps[:, 1 + b, :], ACT.Copy), t)
        gate = sb("gate", [P, P])
        for k in range(KT):
            gate_mm = pe.do(lambda e: e.matmul(ps[:, 6, 0:P], wrb[:, k], xs[:, k], start=(k == 0), stop=(k == KT - 1)), xs_t,
                            dve.last())

        def rms(name, src, ready, which):
            dst, sq, inv = sb(name, [P, KT, P]), sb(name + "_sq", [P, KT, P]), sb(name + "_inv", [P, P])
            t = act.do(lambda e: e.activation(sq[:], src[:], ACT.Square), ready)
            for k in range(KT):
                t = pe.do(lambda e: e.matmul(ps[:, 7, 0:P], g.avg[:], sq[:, k], start=(k == 0), stop=(k == KT - 1)), t,
                          dve.last())
            t = act.do(lambda e: e.activation(inv[:], ps[:, 7, 0:P], ACT.Sqrt, bias=g.eps[:, 1:2]), t)
            t = dve.do(lambda e: e.reciprocal(inv[:], inv[:]), t)
            for k in range(KT):
                t2 = dve.do(lambda e: e.scalar_tensor_tensor(dst[:, k], src[:, k], ln[:, which, k:k + 1], inv[:],
                                                             ALU.mult, ALU.mult), t, l_ln, ready)
            return dst, t2

        h1, h1_t = rms("h1", xs, xs_t, 0)

        nqk = F_HEADS + F_KV
        qk = sb("qk", [P, nqk, P])
        qkb, r1, r2 = sb("qkb", [P, 2, 4, P]), sb("r1", [P, 2, 4, P]), sb("r2", [P, 2, 4, P])
        rope_free, bank_free, qk_t = [None, None], {}, []
        up_rows, down_rows = slice(64, 128), slice(0, 64)
        for n in range(nqk // 4):
            b, par = (0, 3, 4, 5)[n % 4], n % 2
            for j in range(4):
                hd = 4 * n + j
                w, col = (wq, hd) if hd < F_HEADS else (wk, hd - F_HEADS)
                for k in range(KT):
                    t = pe.do(lambda e: e.matmul(ps[:, b, j * P:j * P + P], w[:, k, col * P:col * P + P], h1[:, k],
                                                 start=(k == 0), stop=(k == KT - 1)), h1_t, l_wq, l_wk, s_t, rope_t,
                              bank_free.get(b))
            t = dve.do(lambda e: e.tensor_tensor(qkb[:, par], ps[:, b, :].rearrange("p (j q) -> p j q", j=4),
                                                 bqk[:, 4 * n:4 * n + 4].unsqueeze(2).broadcast_to([P, 4, P]), ALU.add),
                       t, l_bqk, rope_free[par])
            bank_free[b] = t
            a1 = pool.do(lambda e: e.tensor_tensor(r1[:, par], qkb[:, par], rope[:, 0].unsqueeze(1).broadcast_to([P, 4, P]),
                                                   ALU.mult), t, rope_t)
            for src, dst in ((up_rows, down_rows), (down_rows, up_rows)):
                a2 = dve.do(lambda e: e.tensor_tensor(r2[dst, par], qkb[src, par],
                                                      rope[src, 1].unsqueeze(1).broadcast_to([64, 4, P]), ALU.mult), t, rope_t)
            t = pool.do(lambda e: e.tensor_tensor(qk[:, 4 * n:4 * n + 4], r1[:, par], r2[:, par], ALU.add), a1, a2)
            rope_free[par] = t
            qk_t.append(t)
        v = sb("v", [P, F_KV * F_HD])
        for c in range(2):
            cc = slice(c * HALF, (c + 1) * HALF)
            for k in range(KT):
                pe.do(lambda e: e.matmul(ps[:, 1 + c, :], h1[:, k], wv[:, k, cc], start=(k == 0), stop=False), l_wv, l_bv,
                      takeT_t)
            t = pe.do(lambda e: e.matmul(ps[:, 1 + c, :], ones[0:1, :], bv[0:1, cc], start=False, stop=True))
            v_t = act.do(lambda e: e.activation(v[:, cc], ps[:, 1 + c, :], ACT.Copy), t)

        prob, probT, oT = sb("prob", [P, F_HEADS, P]), sb("probT", [P, F_HEADS, P]), sb("oT", [P, F_HEADS, P])
        neg, rsum = sb("neg", [P, F_HEADS]), sb("rsum", [P, F_HEADS])
        nb = F_HEADS // 4
        stage = {}
        for n in range(nb):
            b, hs = (0, 3, 4, 5)[n], slice(4 * n, 4 * n + 4)
            for j in range(4):
                hd = 4 * n + j
                kv = F_HEADS + hd * F_KV // F_HEADS
                t = pe.do(lambda e: e.matmul(ps[:, b, j * P:j * P + P], qk[:, hd], qk[:, kv], start=True, stop=True),
                          qk_t, bank_free.get(b))
            t = dve.do(lambda e: e.tensor_tensor(prob[:, hs], ps[:, b, :].rearrange("p (j q) -> p j q", j=4),
                                                 g.mask[:].unsqueeze(1).broadcast_to([P, 4, P]), ALU.add), t)
            bank_free[b] = t
            stage[n] = t
        for n in range(nb):
            hs = slice(4 * n, 4 * n + 4)
            t = dve.do(lambda e: e.tensor_reduce(neg[:, hs], prob[:, hs], AX.X, ALU.max, negate=True), stage[n])
            stage[n] = dve.do(lambda e: e.tensor_scalar(neg[:, hs], neg[:, hs], F_SCALE, None, ALU.mult), t)
        for n in range(nb):
            hs = slice(4 * n, 4 * n + 4)
            for hd in range(4 * n, 4 * n + 4):
                t = act.do(lambda e: e.activation(prob[:, hd], prob[:, hd], ACT.Exp, bias=neg[:, hd:hd + 1], scale=F_SCALE,
                                                  accum_out=rsum[:, hd:hd + 1]), stage[n])
            t = dve.do(lambda e: e.reciprocal(rsum[:, hs], rsum[:, hs]), t)
            t = dve.do(lambda e: e.tensor_tensor(prob[:, hs], prob[:, hs], rsum[:, hs].unsqueeze(2).broadcast_to([P, 4, P]),
                                                 ALU.mult), t)
            b = (0, 3, 4, 5)[n]
            for j in range(4):
                t = pe.do(lambda e: e.transpose(ps[:, b, j * P:j * P + P], prob[:, 4 * n + j], g.ident[:]), t, bank_free.get(b))
            pT = act.do(lambda e: e.activation(probT[:, hs].rearrange(flat2), ps[:, b, :], ACT.Copy), t)
            stage[n] = pT
        for n in range(nb):
            b, hs = (0, 3, 4, 5)[n], slice(4 * n, 4 * n + 4)
            for j in range(4):
                hd = 4 * n + j
                kv = hd * F_KV // F_HEADS
                t = pe.do(lambda e: e.matmul(ps[:, b, j * P:j * P + P], v[:, kv * F_HD:(kv + 1) * F_HD], probT[:, hd],
                                             start=True, stop=True), stage[n], v_t)
            oT_t = dve.do(lambda e: e.tensor_copy(oT[:, hs].rearrange(flat2), ps[:, b, :]), t)
        for m in range(KT):
            for hd in range(F_HEADS):
                t = pe.do(lambda e: e.matmul(ps[:, 1, m * P:m * P + P], wo[:, hd, m * P:m * P + P], oT[:, hd],
                                             start=(hd == 0), stop=(hd == F_HEADS - 1)), oT_t, l_wo, v_t)
        x1 = sb("x1", [P, KT, P])
        x1_t = dve.do(lambda e: e.tensor_tensor(x1[:, :].rearrange(flat2), xs[:, :].rearrange(flat2), ps[:, 1, 0:2 * P],
                                                ALU.add), t)

        h2, h2_t = rms("h2", x1, x1_t, 1)
        sig_gate = act.do(lambda e: e.activation(gate[:], ps[:, 6, 0:P], ACT.Sigmoid), gate_mm)
        hid, sg = s[:, :].rearrange("p (f q) -> p f q", q=P), diag
        for half in range(2):
            fs = slice(4 * half, 4 * half + 4)
            bg, bu = (0, 3)[half], (4, 5)[half]
            for w, lw, b in ((wg, l_wg, bg), (wu, l_wu, bu)):
                for j in range(4):
                    f = 4 * half + j
                    for k in range(KT):
                        t = pe.do(lambda e: e.matmul(ps[:, b, j * P:j * P + P], w[:, k, f * P:f * P + P], h2[:, k],
                                                     start=(k == 0), stop=(k == KT - 1)), h2_t, lw, oT_t)
                if w is wg:
                    tg = act.do(lambda e: e.activation(sg[:, fs].rearrange(flat2), ps[:, b, :], ACT.Sigmoid), t)
            tg = dve.do(lambda e: e.tensor_tensor(sg[:, fs].rearrange(flat2), sg[:, fs].rearrange(flat2), ps[:, bg, :], ALU.mult), tg)
            hid_t = dve.do(lambda e: e.tensor_tensor(hid[:, fs].rearrange(flat2), sg[:, fs].rearrange(flat2), ps[:, bu, :],
                                                     ALU.mult), tg, t)
        for m in range(KT):
            for f in range(FI_T):
                t = pe.do(lambda e: e.matmul(ps[:, 2, m * P:m * P + P], wd[:, f, m * P:m * P + P], hid[:, f],
                                             start=(f == 0), stop=(f == FI_T - 1)), hid_t, l_wd, v_t)
        ch = sb("ch", [P, KT, P])
        a = pool.do(lambda e: e.tensor_tensor(ch[:], x1[:], xs[:], ALU.subtract), x1_t, xs_t)
        t = dve.do(lambda e: e.tensor_tensor(ch[:, :].rearrange(flat2), ch[:, :].rearrange(flat2), ps[:, 2, 0:2 * P], ALU.add), t, a)
        t = dve.do(lambda e: e.tensor_tensor(ch[:], ch[:], gate[:].unsqueeze(1).broadcast_to([P, KT, P]), ALU.mult), t, sig_gate)
        chT = sb("chT", [P, D])
        for m in range(KT):
            tp = pe.do(lambda e: e.transpose(ps[:, 6, m * P:m * P + P], ch[:, m], g.ident[:]), t)
        t = act.do(lambda e: e.activation(chT[:], ps[:, 6, 0:D], ACT.Copy), tp)
        for m in range(KT):
            for c in range(NH2):
                b, cc = (0, 3, 4, 5)[2 * m + c], slice(c * HALF, (c + 1) * HALF)
                tp = pe.do(lambda e: e.matmul(ps[:, b, :], chT[:, m * P:m * P + P], takeT[:, cc], start=True, stop=True),
                           t, takeT_t, hid_t)
                dve.do(lambda e: e.tensor_tensor(g.x[:, m, cc], g.x[:, m, cc], ps[:, b, :], ALU.add), tp, x_plus)


def ffn_first(g, ins):
    ffn(g, ins, "f1")


def ffn_second(g, ins):
    ffn(g, ins, "f2")


def halves():
    return [(c, slice(c * HALF, (c + 1) * HALF)) for c in range(NH2)]


def linear(g, w, acts, m_tiles, banks, take, *tokens, only=None, at=None):
    pe = g.pr.pe
    w_hi, w_lo = w
    a_hi, a_lo = acts
    free = {}
    n = 0
    for m in m_tiles:
        for c, cc in halves() if only is None else [halves()[only]]:
            b = banks[n % len(banks)]
            n += 1
            mm = slice(m * P, m * P + P)
            ac = at or cc
            t = matmul3(pe, g.ps[:, b, :],
                        [(w_hi[:, k, mm], None if w_lo is None else w_lo[:, k, mm], a_hi[:, k, ac], a_lo[:, k, ac])
                         for k in range(w_hi.shape[1])], tokens, free.get(b))
            free[b] = take(m, c, cc, g.ps[:, b, :], t)
    return [t for ts in free.values() for t in ts]


def split(g, hi, lo, src, *tokens):
    th = g.pr.act.do(lambda e: e.activation(hi, src, ACT.Copy), *tokens)
    return g.pr.dve.do(lambda e: e.tensor_tensor(lo, src, fr(hi), ALU.subtract), th, *tokens)


def recurrence(g, ins):
    pr = g.pr
    pe, dve, act, pool, sp = pr.pe, pr.dve, pr.act, pr.pool, pr.sp
    with pr.phase():
        h = pr.sb("r_h", [P, KT, N])
        h_hi, h_lo = pr.sb("r_h_hi", [P, KT, N], F32R), pr.sb("r_h_lo", [P, KT, N], F32R)
        w = pr.sb("r_w", [P, KT, 2 * D])
        w_hi, w_lo = pr.sb("r_w_hi", [P, KT, 2 * D], F32R), pr.sb("r_w_lo", [P, KT, 2 * D], F32R)
        bias = pr.sb("r_bias", [P, 2 * KT])
        gates, values, hidden = pr.sb("r_gates", [P, KT, N]), pr.sb("r_values", [P, KT, N]), pr.sb("r_hidden", [P, KT, N])
        s_w = pr.slot("r_loaded")
        sp.dma(s_w, lambda: bias[:], lambda: ins["r_b"])
        t = sp.dma(s_w, lambda: w[:], lambda: ins["r_w"])
        w_t = split(g, w_hi[:], w_lo[:], w[:], t)
        hn = normalise(g, "r_n", g.x, h, N, 1e-5, centre=True, split=(h_hi, h_lo))
        done = {}

        def take(m, c, cc, ps, t):
            dst, func = (gates, ACT.Sigmoid) if m < KT else (values, ACT.Tanh)
            a = act.do(lambda e: e.activation(dst[:, m % KT, cc], ps, func, bias=bias[:, m:m + 1]), t)
            done[m, c] = a
            if m >= KT:
                f = m - KT
                first = 0.0 if c == 0 else hidden[:, f, c * HALF - 1:c * HALF]
                s = dve.do(lambda e: e.tensor_tensor_scan(hidden[:, f, cc], gates[:, f, cc], values[:, f, cc], first,
                                                          ALU.mult, ALU.add), a, done[f, c], done.get(("scan", f, c - 1)))
                done["scan", f, c] = s
                dve.do(lambda e: e.tensor_tensor(g.x[:, f, cc], g.x[:, f, cc], hidden[:, f, cc], ALU.add), s)
            return [a]

        linear(g, (w_hi, w_lo), (h_hi, h_lo), (0, 2, 1, 3), (4, 5, 6, 7), take, w_t, hn)


R_F, R_TAPS, R_C = 768, 4, 8.0
RF_T = R_F // P


def rglru(g, ins):
    pr = g.pr
    pe, dve, act, pool, sp = pr.pe, pr.dve, pr.act, pr.pool, pr.sp
    with pr.phase():
        def sb(name, shape, dt=F32):
            return pr.sb("l_" + name, shape, dt)

        bias = sb("bias", [P, 10, KT])
        LEFT, RIGHT, CONV, GA, GX, AP, OUT, DOWN, NORM1, NORM2 = range(10)
        up_b = sb("up_b", [P, 2, RF_T])
        taps = sb("taps", [P, R_TAPS, KT])
        s_b = pr.slot("l_bias_loaded")
        sp.dma(s_b, lambda: bias[:], lambda: ins["l_bias"])
        sp.dma(s_b, lambda: up_b[:], lambda: ins["l_up_b"])
        b_t = sp.dma(s_b, lambda: taps[:], lambda: ins["l_taps"])

        raw = [sb("raw0", [P, KT * R_F]), sb("raw1", [P, KT * R_F])]
        raw_slot = [pr.slot("l_raw0_loaded"), pr.slot("l_raw1_loaded")]
        raw_free = [None, None]
        w, w_t = {}, {}
        for n, (name, kt, cols) in enumerate((("left", KT, D), ("right", KT, D), ("ga", KT, D), ("gx", KT, D), ("out", KT, D),
                                              ("up1", KT, R_F), ("up2", KT, R_F), ("down", RF_T, D))):
            r = raw[n % 2][:, 0:kt * cols].rearrange("p (k n) -> p k n", k=kt)
            hi, lo = sb(name + "_hi", [P, kt, cols], F32R), sb(name + "_lo", [P, kt, cols], F32R)
            t = sp.dma(raw_slot[n % 2], lambda: r, lambda: ins["l_" + name], raw_free[n % 2])
            th = pool.do(lambda e: e.tensor_copy(hi[:], r), t)
            tl = pool.do(lambda e: e.tensor_tensor(lo[:], r, fr(hi[:]), ALU.subtract), th)
            raw_free[n % 2] = [tl]
            w[name], w_t[name] = (hi, lo), tl

        sm = sb("softplus", [P, 6, KT])
        a_par = bias[:, AP]
        t = act.do(lambda e: e.activation(sm[:, 0], a_par, ACT.Abs), b_t)
        t = act.do(lambda e: e.activation(sm[:, 1], sm[:, 0], ACT.Exp, scale=-1.0), t)
        t = dve.do(lambda e: e.tensor_scalar(sm[:, 2], sm[:, 1], 1.0, None, ALU.add), t)
        tw = act.do(lambda e: e.activation(sm[:, 3], sm[:, 2], ACT.Ln), t)
        t = dve.do(lambda e: e.tensor_scalar(sm[:, 4], sm[:, 2], -1.0, None, ALU.add), t)
        t = dve.do(lambda e: e.tensor_scalar(sm[:, 5], sm[:, 4], 0.0, None, ALU.is_equal), t)
        t = dve.do(lambda e: e.tensor_tensor(sm[:, 4], sm[:, 4], sm[:, 5], ALU.add), t)
        t = dve.do(lambda e: e.reciprocal(sm[:, 4], sm[:, 4]), t)
        t = dve.do(lambda e: e.tensor_tensor(sm[:, 4], sm[:, 4], sm[:, 3], ALU.mult), t, tw)
        t = dve.do(lambda e: e.tensor_tensor(sm[:, 4], sm[:, 4], sm[:, 5], ALU.add), t)
        t = dve.do(lambda e: e.tensor_tensor(sm[:, 4], sm[:, 4], sm[:, 1], ALU.mult), t)
        t = dve.do(lambda e: e.scalar_tensor_tensor(sm[:, 0], a_par, 0.0, sm[:, 4], ALU.max, ALU.add), t)
        rate_t = dve.do(lambda e: e.tensor_scalar(sm[:, 0], sm[:, 0], -R_C, None, ALU.mult), t)
        rate = sm[:, 0]

        u = sb("u", [P, KT, N])
        xn, xn_hi, xn_lo = sb("xn", [P, KT, N]), sb("xn_hi", [P, KT, N], F32R), sb("xn_lo", [P, KT, N], F32R)
        scratch = norm_scratch(pr, "l_norm", N)
        un = normalise(g, "l_n0", g.x, u, N, 1e-5, centre=True, scratch=scratch)
        un = [o[0] for o in un]
        nn = normalise(g, "l_n1", u, xn, N, 1e-8, src_ready=un + [b_t], weight=bias[:, NORM1], split=(xn_hi, xn_lo),
                       scratch=scratch)
        left = sb("left", [P, KT, N])
        PAD = R_TAPS - 1
        right = sb("right", [P, KT, PAD + N])
        z = dve.do(lambda e: e.memset(right[:, :, 0:PAD], 0.0))
        left_t, right_t = [], [z]

        def take_left(m, c, cc, ps, t):
            a = act.do(lambda e: e.activation(left[:, m, cc], ps, ACT.Gelu, bias=bias[:, LEFT, m:m + 1]), t)
            left_t.append(a)
            return [a]

        def take_right(m, c, cc, ps, t):
            a = dve.do(lambda e: e.tensor_scalar(right[:, m, PAD + c * HALF:PAD + (c + 1) * HALF], ps,
                                                 bias[:, RIGHT, m:m + 1], None, ALU.add), t)
            right_t.append(a)
            return [a]

        linear(g, w["right"], (xn_hi, xn_lo), range(KT), (4, 5, 6, 7), take_right, w_t["right"], nn)
        linear(g, w["left"], (xn_hi, xn_lo), range(KT), (0, 1, 2, 3), take_left, w_t["left"])
        xn_read = pe.last()
        y = xn
        y_hi, y_lo = xn_hi, xn_lo
        y_t = []
        for m in range(KT):
            t = dve.do(lambda e: e.tensor_scalar(y[:, m], right[:, m, 0:N], taps[:, 0, m:m + 1], bias[:, CONV, m:m + 1],
                                                 ALU.mult, ALU.add), right_t, nn)
            for j in range(1, R_TAPS):
                t = dve.do(lambda e: e.scalar_tensor_tensor(y[:, m], right[:, m, j:j + N], taps[:, j, m:m + 1], y[:, m],
                                                            ALU.mult, ALU.add), t)
            y_t.append(split(g, y_hi[:, m], y_lo[:, m], y[:, m], t, xn_read))
        rg, ig, th = sb("rg", [P, KT, N]), sb("ig", [P, KT, N]), right[:, :, PAD:]
        a_ = scratch[0][:, :, :, :].rearrange("p a k w -> p (a k w)").rearrange("p (k n) -> p k n", k=KT)
        sig_t = []
        for dst, name, bb, banks in ((rg, "ga", GA, (0, 1, 2, 3)), (ig, "gx", GX, (4, 5, 6, 7))):
            def take(m, c, cc, ps, t):
                a = act.do(lambda e: e.activation(dst[:, m, cc], ps, ACT.Sigmoid, bias=bias[:, bb, m:m + 1]), t)
                sig_t.append(a)
                return [a]
            linear(g, w[name], (y_hi, y_lo), range(KT), banks, take, w_t[name], y_t, left_t)
        for m in range(KT):
            ta = act.do(lambda e: e.activation(a_[:, m], rg[:, m], ACT.Exp, scale=rate[:, m:m + 1]), sig_t, rate_t)
            tt = act.do(lambda e: e.activation(th[:, m], rg[:, m], ACT.Tanh, scale=rate[:, m:m + 1]), y_t)
            tr = dve.do(lambda e: e.tensor_tensor(rg[:, m], a_[:, m], a_[:, m], ALU.mult), ta, tt)
            t = dve.do(lambda e: e.scalar_tensor_tensor(rg[:, m], rg[:, m], 1.0, th[:, m], ALU.add, ALU.mult), tr, tt)
            sig_t.append(t)
            ti = pool.do(lambda e: e.tensor_tensor(ig[:, m], ig[:, m], y[:, m], ALU.mult), sig_t[:-1], y_t)
            sig_t.append(ti)
        prod_t = []
        for m in range(KT):
            t = act.do(lambda e: e.activation(rg[:, m], rg[:, m], ACT.Sqrt, scale=-1.0), sig_t)
            t = dve.do(lambda e: e.tensor_tensor(ig[:, m], ig[:, m], rg[:, m], ALU.mult), t, sig_t)
            t = dve.do(lambda e: e.tensor_tensor_scan(th[:, m], a_[:, m], ig[:, m], 0.0, ALU.mult, ALU.add), t)
            t = dve.do(lambda e: e.tensor_tensor(left[:, m], left[:, m], th[:, m], ALU.mult), t, left_t)
            prod_t.append(split(g, y_hi[:, m], y_lo[:, m], left[:, m], t, sig_t))
        x1, x1_t = y, []

        def take_out(m, c, cc, ps, t):
            a = dve.do(lambda e: e.scalar_tensor_tensor(x1[:, m, cc], ps, bias[:, OUT, m:m + 1], u[:, m, cc],
                                                        ALU.add, ALU.add), t)
            x1_t.append(a)
            return [a]

        linear(g, w["out"], (y_hi, y_lo), range(KT), (0, 1, 2, 3), take_out, w_t["out"], prod_t)
        out_read = pe.last()
        x_t = pool.do(lambda e: e.tensor_tensor(g.x[:], g.x[:], x1[:], ALU.add), x1_t)
        nn2 = normalise(g, "l_n2", x1, left, N, 1e-8, src_ready=x1_t, dst_free=[out_read] + prod_t,
                        weight=bias[:, NORM2], split=(y_hi, y_lo), scratch=scratch)
        mid_hi, mid_lo = sb("mid_hi", [P, RF_T, HALF], F32R), sb("mid_lo", [P, RF_T, HALF], F32R)
        gel, down_read, free = {}, None, [x_t, None]
        bufs = [rg[:, 0], ig[:, 0]], [rg[:, 1], ig[:, 1]]
        f1 = {0: None, 1: None}
        f2 = {0: None, 1: None}
        for half in range(NH2):
            mid_t = []
            for f in range(RF_T):
                par = f % 2
                gb, pb = bufs[0][par][:, 0:HALF], bufs[1][par][:, 0:HALF]

                def take1(m, c, cc, ps, t):
                    gel["gelu"] = act.do(lambda e: e.activation(gb, ps, ACT.Gelu, bias=up_b[:, 0, m:m + 1]), t,
                                         gel.get(("used", par)))
                    return [gel["gelu"]]

                def take2(m, c, cc, ps, t):
                    a = dve.do(lambda e: e.scalar_tensor_tensor(pb, ps, up_b[:, 1, m:m + 1], gb, ALU.add, ALU.mult),
                               t, gel["gelu"], gel.get(("used", par)))
                    gel["used", par] = split(g, mid_hi[:, m], mid_lo[:, m], pb, a, down_read)
                    mid_t.append(gel["used", par])
                    return [a]

                f1[par] = linear(g, w["up1"], (y_hi, y_lo), [f], (4 + par,), take1, w_t["up1"], nn2, f1[par], only=half)
                f2[par] = linear(g, w["up2"], (y_hi, y_lo), [f], (6 + par,), take2, w_t["up2"], f2[par], only=half)

            def take_down(m, c, cc, ps, t):
                return [dve.do(lambda e: e.scalar_tensor_tensor(g.x[:, m, cc], ps, bias[:, DOWN, m:m + 1], g.x[:, m, cc],
                                                                ALU.add, ALU.add), t, x_t)]

            linear(g, w["down"], (mid_hi, mid_lo), range(KT), (2 * half, 2 * half + 1), take_down, w_t["down"], mid_t,
                   only=half, at=slice(0, HALF))
            down_read = [pe.last()]


T_E = 1024
TE_T = T_E // P


def ternary_weights(g, ins):
    pr = g.pr
    pe, dve, act, pool, sp = pr.pe, pr.dve, pr.act, pr.pool, pr.sp
    g.tern, g.scale = {}, pr.sb("t_scale", [P, 3, 3])
    for n, (name, kt, cols) in enumerate((("up", KT, T_E), ("gate", KT, T_E), ("down", TE_T, D))):
        g.tern[name] = pr.sb("t_" + name, [P, kt, cols], F32R)
    with pr.phase():
        part, avg = pr.sb("t_part", [P, 3]), pr.sb("t_avg", [P, P])
        a_t = dve.do(lambda e: e.memset(avg[:], 1.0 / (T_E * D)))
        for n, (name, kt, cols) in enumerate((("up", KT, T_E), ("gate", KT, T_E), ("down", TE_T, D))):
            raw, neg = pr.sb("t_raw_" + name, [P, kt, cols]), pr.sb("t_neg_" + name, [P, kt, cols])
            slot = pr.slot(f"t_{name}_loaded")
            l = sp.dma(slot, lambda: raw[:], lambda: ins["t_" + name])
            t = dve.do(lambda e: e.tensor_reduce(part[:, n:n + 1], raw[:], AX.XY, ALU.add, apply_absolute_value=True), l)
            t = pe.do(lambda e: e.matmul(g.ps[:, n, 0:1], avg[:], part[:, n:n + 1], start=True, stop=True), t, a_t)
            s = g.scale[:, n]
            t = dve.do(lambda e: e.tensor_scalar(s[:, 0:1], g.ps[:, n, 0:1], 1e-8, None, ALU.add), t)
            dve.do(lambda e: e.tensor_scalar(s[:, 1:2], s[:, 0:1], 0.5, None, ALU.mult), t)
            t = dve.do(lambda e: e.tensor_scalar(s[:, 2:3], s[:, 0:1], -0.5, None, ALU.mult), t)
            t = dve.do(lambda e: e.tensor_scalar(neg[:], raw[:], s[:, 2:3], None, ALU.is_lt), t)
            dve.do(lambda e: e.scalar_tensor_tensor(g.tern[name][:], raw[:], s[:, 1:2], neg[:], ALU.is_gt, ALU.subtract), t)


def ternary_ffn(g, ins, tag):
    pr = g.pr
    pe, dve, act, pool, sp = pr.pe, pr.dve, pr.act, pr.pool, pr.sp
    with pr.phase():
        h = pr.sb(tag + "_h", [P, KT, N])
        h_hi, h_lo = pr.sb(tag + "_h_hi", [P, KT, N], F32R), pr.sb(tag + "_h_lo", [P, KT, N], F32R)
        hn = normalise(g, tag + "_n", g.x, h, N, 1e-5, centre=True, split=(h_hi, h_lo))
        sg, hid = pr.sb(tag + "_sg", [P, 2, N]), pr.sb(tag + "_hid", [P, 2, N])
        hid_hi, hid_lo = pr.sb(tag + "_hid_hi", [P, TE_T, N], F32R), pr.sb(tag + "_hid_lo", [P, TE_T, N], F32R)
        s_up, s_gate, s_down = (g.scale[:, n, 0:1] for n in range(3))
        st, hid_t = {}, []
        for f in range(TE_T):
            par = f % 2

            def take_up(m, c, cc, ps, t):
                a = act.do(lambda e: e.activation(sg[:, par, cc], ps, ACT.Sigmoid, scale=s_up), t, st.get(("used", par)))
                b = dve.do(lambda e: e.scalar_tensor_tensor(sg[:, par, cc], ps, s_up, sg[:, par, cc], ALU.mult, ALU.mult), a)
                st[c] = b
                return [b]

            def take_gate(m, c, cc, ps, t):
                b = dve.do(lambda e: e.scalar_tensor_tensor(hid[:, par, cc], ps, s_gate, sg[:, par, cc], ALU.mult, ALU.mult),
                           t, st[c], st.get(("used", par)))
                s = split(g, hid_hi[:, m, cc], hid_lo[:, m, cc], hid[:, par, cc], b)
                st["used", par] = s
                hid_t.append(s)
                return [b]

            f1 = linear(g, (g.tern["up"], None), (h_hi, h_lo), [f], (4, 5) if par else (0, 1), take_up, hn, st.get(("f1", par)))
            f2 = linear(g, (g.tern["gate"], None), (h_hi, h_lo), [f], (6, 7) if par else (2, 3), take_gate,
                        st.get(("f2", par)))
            st["f1", par], st["f2", par] = f1, f2

        def take_down(m, c, cc, ps, t):
            return [dve.do(lambda e: e.scalar_tensor_tensor(g.x[:, m, cc], ps, s_down, g.x[:, m, cc], ALU.mult, ALU.add), t)]

        linear(g, (g.tern["down"], None), (hid_hi, hid_lo), range(KT), (0, 1, 2, 3), take_down, hid_t, f1, f2)


def ternary_first(g, ins):
    ternary_weights(g, ins)
    ternary_ffn(g, ins, "t1")


def ternary_second(g, ins):
    ternary_ffn(g, ins, "t2")


def build(nc, ins, out, stop=99):
    with ExitStack() as ctx:
        g = Env()
        pr = g.pr = Prog(nc, ctx)
        g.ps = ctx.enter_context(nc.psum_tensor("ps", [P, 8, HALF], F32))
        g.ps_flat = g.ps[:, :, :].rearrange("p b n -> p (b n)")
        g.bank = [g.ps[:, b, :] for b in range(8)]
        setup(g, ins, None)
        layers = LAYERS
        for layer in layers[:stop]:
            layer(g, ins)
        s_out = pr.slot("x_stored")
        pr.fence()
        pr.sp.wait(g.x_ready)
        t = pr.sp.dma(s_out, lambda: out.rearrange("(k p) n -> p k n", p=P), lambda: g.x[:])
        pr.sp.wait(t)


LAYERS = [attn_a, ffn_first, attn_b, ffn_second, recurrence, ternary_first, rglru, ternary_second]


def rope_tables(n, dim, theta=10000.0):
    inv = (1.0 / np.float32(theta) ** (np.arange(0, dim, 2, dtype=np.float32) / np.float32(dim))).astype(np.float32)
    ang = (np.arange(n, dtype=np.float32)[:, None] * inv[None, :]).astype(np.float32)
    return np.cos(ang).astype(np.float32), np.sin(ang).astype(np.float32)


def layout(i):
    a = {k: np.asarray(v) for k, v in i.items()}
    r = {}
    r["x"] = a["L0_attn_a_hidden_states"][0].T
    q = a["L0_attn_a_Wq"].T.reshape(D, A_KV, A_GRP * A_HD)
    k = a["L0_attn_a_Wk"].T.reshape(D, A_KV, A_HD)
    v = a["L0_attn_a_Wv"].T.reshape(D, A_KV, A_HD)
    r["a_w"] = np.concatenate([q, k, v], 2).reshape(KT, P, A_KV, A_W).transpose(2, 1, 0, 3)
    r["a_o"] = a["L0_attn_a_Wo"].T.reshape(A_KV, 2, P, D).transpose(0, 2, 1, 3)
    cos, sin = rope_tables(N, A_HD)
    r["a_cos"] = np.concatenate([cos, cos], 1).reshape(TT, P, A_HD).transpose(1, 0, 2)
    r["a_sin"] = np.concatenate([-sin, sin], 1).reshape(TT, P, A_HD).transpose(1, 0, 2)
    qkv = [a["L0_attn_b_W_" + c].transpose(1, 0, 2) for c in "QKV"]
    r["b_w"] = np.concatenate(qkv, 2).reshape(KT, P, B_HEADS, 3 * B_HD).transpose(2, 1, 0, 3)
    r["b_o"] = a["L0_attn_b_W_O"].reshape(B_HEADS // B_PAIR, B_PAIR, B_HD, D).transpose(0, 2, 1, 3)
    r["b_bias"] = np.stack([a["L0_attn_b_b_" + c] for c in "QKV"]).transpose(2, 0, 1)
    r["b_bias_out"] = a["L0_attn_b_b_O"].reshape(KT, P).T

    def tiles(w):
        return w.reshape(-1, P, w.shape[1]).transpose(1, 0, 2)

    f = {k[7:]: v for k, v in a.items() if k.startswith("L0_ffn_")}
    r["f_wr"] = f["w_router"].reshape(KT, P).T
    r["f_ln"] = np.stack([f["ln1_w"], f["ln2_w"]]).reshape(2, KT, P).transpose(2, 0, 1)
    r["f_bqk"] = np.concatenate([f["bq"], f["bk"]]).reshape(-1, P).T
    r["f_bv"] = f["bv"][None, :]
    for name, key in (("wq", "wq"), ("wk", "wk"), ("wv", "wv"), ("wo", "wo"), ("wg", "w_gate"), ("wu", "w_up"), ("wd", "w_down")):
        r["f_" + name] = tiles(f[key])
    cos, sin = rope_tables(N, F_HD)
    tab = np.stack([np.concatenate([cos, cos], 1), np.concatenate([sin, -sin], 1)], 1)
    r["f_rope"] = tab.reshape(TT, P, 2, P).transpose(1, 0, 2, 3)
    r["r_w"] = tiles(a["L1_attn_a_W"].T)
    r["r_b"] = a["L1_attn_a_b"].reshape(-1, P).T
    l = {k[10:]: v for k, v in a.items() if k.startswith("L1_attn_b_")}
    for name in ("left", "right", "ga", "gx", "out", "up1", "up2", "down"):
        r["l_" + name] = tiles(l[name + "_W"])
    vectors = ("left_b", "right_b", "conv_b", "ga_b", "gx_b", "a_param", "out_b", "down_b", "norm1_w", "norm2_w")
    r["l_bias"] = np.stack([l[v] for v in vectors]).reshape(len(vectors), KT, P).transpose(2, 0, 1)
    r["l_up_b"] = np.stack([l["up1_b"], l["up2_b"]]).reshape(2, RF_T, P).transpose(2, 0, 1)
    r["l_taps"] = l["conv_w"].reshape(R_TAPS, KT, P).transpose(2, 0, 1)
    for name in ("up", "gate", "down"):
        r["t_" + name] = tiles(a["L1_ffn_W_" + name].T)
    return r


def kernel(**inputs):
    import concourse.bacc as bacc
    from concourse.bass_utils import run_bass_kernel_spmd

    nc = bacc.Bacc("TRN2", target_bir_lowering=False, num_devices=1)
    arrays = {f"in_{k}": np.ascontiguousarray(v) for k, v in layout(inputs).items()}
    ins = {k[3:]: nc.dram_tensor(k, v.shape, mybir.dt.from_np(v.dtype), kind="ExternalInput").ap()
           for k, v in arrays.items()}
    out = nc.dram_tensor("out", (D, N), F32, kind="ExternalOutput").ap()
    build(nc, ins, out)
    got = run_bass_kernel_spmd(nc, [arrays], core_ids=[0])
    return np.ascontiguousarray(got.results[0]["out"].T).reshape(1, N, D)
```

```python
import math
from contextlib import ExitStack, contextmanager

import numpy as np

import concourse.bass as bass
from concourse import mybir
from concourse.alu_op_type import AluOpType as ALU

F32 = mybir.dt.float32
F32R = mybir.dt.float32r
BF16 = mybir.dt.bfloat16
ACT = mybir.ActivationFunctionType
AX = mybir.AxisListType

P = 128
N = 1024
D = 256
KT = D // P
TT = N // P
HALF = 512
NH2 = N // HALF
MASKED = -1e30


class Count:

    def __init__(self, prog, sem, start=0):
        self.prog, self.sem, self.n = prog, sem, start
        self.per = 0
        prog.counts.append(self)

    def add(self, k):
        self.n += k
        return Token(self, self.n, self.prog.loop)


class Token:

    def __init__(self, count, value, loop):
        self.count, self.value, self.loop = count, value, loop

    def prev(self):
        return Token(self.count, self.value - self.count.per, self.loop)

    def last(self):
        return Token(self.count, self.value + (self.loop.turns - 1) * self.loop.per[self.count], None)


class Loop:
    def __init__(self, turns):
        self.turns, self.i, self.per = turns, None, {}


class Lane:

    def __init__(self, prog, eng, sem, gate=None):
        self.prog, self.e, self.gate = prog, eng, gate
        self.count = Count(prog, sem, START)
        self.seen = {}
        prog.lanes.append(self)
        eng.sem_inc(sem, START)

    def wait(self, *tokens):
        prog, gated = self.prog, False
        for t in tokens:
            if t is None:
                continue
            if isinstance(t, (list, tuple)):
                self.wait(*t)
                continue
            key = (t.count, t.loop)
            if self.seen.get(key, -1) >= t.value:
                continue
            self.seen[key] = t.value
            if prog.dry:
                continue
            if t.loop is None:
                self.e.wait_ge(t.count.sem, t.value)
            else:
                self.e.wait_ge(t.count.sem, prog.loop.i * prog.loop.per[t.count] + t.value)
                gated = self.gate is not None
        if gated:
            self.e.sem_inc(self.gate, 1)

    def do(self, instruction, *tokens, signal=True):
        self.wait(*tokens)
        if self.prog.dry:
            return self.count.add(1) if signal else None
        ins = instruction(self.e)
        if not signal:
            return None
        ins.then_inc(self.count.sem, 1)
        return self.count.add(1)

    def last(self):
        return Token(self.count, self.count.n, self.prog.loop)

    def dma(self, slot, out, in_, *tokens):
        self.wait(*tokens)
        if not self.prog.dry:
            self.e.dma_start(out(), in_()).then_inc(slot.sem, 16)
        return slot.add(16)


START = 1024


class Prog:
    def __init__(self, nc, ctx):
        self.nc, self.ctx = nc, ctx
        self.counts, self.lanes = [], []
        self.loop, self.dry = None, False
        self.bufs = ctx
        self.readers = {}
        sem = self.sem
        self.pe = Lane(self, nc.tensor, sem("pe_done"))
        self.dve = Lane(self, nc.vector, sem("dve_done"))
        self.act = Lane(self, nc.scalar, sem("act_done"))
        self.pool = Lane(self, nc.gpsimd, sem("pool_done"), gate=sem("pool_gate"))
        self.sp = Lane(self, nc.sync, sem("sp_done"))

    def sem(self, name):
        return self.ctx.enter_context(self.nc.semaphore(name))

    def slot(self, name):
        return Count(self, self.sem(name))

    def sb(self, name, shape, dt=F32):
        return self.bufs.enter_context(self.nc.sbuf_tensor(name, shape, dt))

    def fence(self):
        ends = [Token(c, c.n, self.loop) for c in self.counts if c is not self.sp.count and c.n]
        for lane in self.lanes:
            lane.wait(*ends)

    @contextmanager
    def phase(self):
        outer = self.bufs
        with ExitStack() as bufs:
            self.bufs = bufs
            yield
            self.fence()
        self.bufs = outer

    def run_loop(self, turns, body):
        self.fence()
        self.readers.clear()
        loop = Loop(turns)
        base = {c: c.n for c in self.counts}
        held = [dict(lane.seen) for lane in self.lanes]
        self.loop, self.dry = loop, True
        body(0)
        self.dry = False
        for c in self.counts:
            c.per = loop.per[c] = c.n - base[c]
            assert c.per <= START
            c.n = base[c]
        for lane, seen in zip(self.lanes, held):
            lane.seen = seen
        for name, tokens in self.readers.items():
            self.readers[name] = [t.prev() for t in tokens]
        with self.nc.Fori(0, turns) as i:
            loop.i = i
            body(i)
        for c in self.counts:
            assert c.n == base[c] + c.per
            c.n = base[c] + turns * c.per
        self.loop = None
        self.readers.clear()
        self.fence()


def fr(ap):
    return ap.bitcast(F32)


class Env:
    pass


def setup(g, ins):
    pr, pool, dve, sp = g.pr, g.pr.pool, g.pr.dve, g.pr.sp
    g.x = pr.sb("x", [P, KT, N])
    g.x_slot = pr.slot("x_loaded")
    g.x_ready = [sp.dma(g.x_slot, lambda: g.x[:], lambda: ins["x"].rearrange("(k p) n -> p k n", p=P))]
    g.ident = pr.sb("ident", [P, P])
    g.ident_b = pr.sb("ident_b", [P, P], BF16)
    g.mask = pr.sb("mask", [P, P])
    g.mask_b = pr.sb("mask_b", [P, P], BF16)
    g.avg = pr.sb("avg", [P, P])
    g.ones = pr.sb("ones", [P, P])
    g.warm, g.warm_t = pr.sb("warm", [P, 1]), None
    g.eps = pr.sb("eps", [P, 3])
    g.EPS = {1e-5: 0, 1e-6: 1, 1e-8: 2}
    z = pool.do(lambda e: e.memset(g.ident[:], 0.0))
    z2 = pool.do(lambda e: e.memset(g.mask[:], 0.0))
    t1 = pool.do(lambda e: e.affine_select(out=g.ident[:], in_=g.ident[:], compare_op=ALU.not_equal, fill=1.0,
                                           base=0, pattern=[[-1, P]], channel_multiplier=1), z)
    t2 = pool.do(lambda e: e.affine_select(out=g.mask[:], in_=g.mask[:], compare_op=ALU.is_ge, fill=MASKED,
                                           base=0, pattern=[[-1, P]], channel_multiplier=1), z2)
    dve.do(lambda e: e.memset(g.avg[:], 1.0 / D))
    dve.do(lambda e: e.memset(g.ones[:], 1.0))
    for eps, c in g.EPS.items():
        dve.do(lambda e, c=c, eps=eps: e.memset(g.eps[:, c:c + 1], eps))
    dve.do(lambda e: e.tensor_copy(g.ident_b[:], g.ident[:]), t1)
    dve.do(lambda e: e.tensor_copy(g.mask_b[:], g.mask[:]), t2)
    pr.fence()


def norm_scratch(pr, name, cols):
    w = min(cols, HALF)
    return (pr.sb(name + "_sq", [P, cols // w, KT, w]), pr.sb(name + "_diag", [P, cols // w, w]),
            pr.sb(name + "_std", [P, cols // w, w // P]))


def normalise(g, name, src, dst, cols, eps, src_ready=(), dst_free=(), centre=False, weight=None, split=None,
              scratch=None):
    pr, pe, dve, act = g.pr, g.pr.pe, g.pr.dve, g.pr.act
    w = min(cols, HALF)
    tiles = w // P
    done = []
    sq, diag, std = scratch or norm_scratch(pr, name, cols)
    blocks = [(b, slice(b * w, b * w + w), g.bank[2 * b], g.bank[2 * b + 1]) for b in range(cols // w)]
    k0 = g.EPS[eps]
    g.warm_t = act.do(lambda e: e.activation(g.warm[:], g.eps[:, k0:k0 + 1], ACT.Sqrt), g.warm_t)
    mean_t, base_t, sq_t = {}, {}, {}
    for b, c, ps, _ in blocks:
        if centre:
            for k in range(KT):
                mean_t[b] = pe.do(lambda e: e.matmul(ps[:, 0:w], g.avg[:], src[:, k, c], start=(k == 0), stop=(k == KT - 1)),
                                  list(src_ready), signal=(k == KT - 1))
    for b, c, ps, _ in blocks:
        base, base_t[b] = src, list(src_ready)
        if centre:
            base = dst
            base_t[b] = [dve.do(lambda e: e.tensor_tensor(dst[:, :, c], src[:, :, c],
                                                          ps[:, 0:w].unsqueeze(1).broadcast_to([P, KT, w]), ALU.subtract),
                                mean_t[b], list(dst_free))]
        sq_t[b] = act.do(lambda e: e.activation(sq[:, b], base[:, :, c], ACT.Square), base_t[b])
    inv_t = {}
    for b, c, ps, _ in blocks:
        for j in range(tiles):
            for k in range(KT):
                t = pe.do(lambda e: e.matmul(ps[:, j:j + 1], sq[:, b, k, j * P:j * P + P], g.avg[:, 0:1],
                                             start=(k == 0), stop=(k == KT - 1)), sq_t[b],
                          signal=(j == tiles - 1 and k == KT - 1))
        t = act.do(lambda e: e.activation(std[:, b], ps[:, 0:tiles], ACT.Sqrt, bias=g.eps[:, k0:k0 + 1]), t)
        t = dve.do(lambda e: e.reciprocal(std[:, b], std[:, b]), t)
        d3 = diag[:, b].rearrange("p (j q) -> p j q", q=P)
        inv_t[b] = dve.do(lambda e: e.tensor_tensor(d3, g.ident[:].unsqueeze(1).broadcast_to([P, tiles, P]),
                                                    std[:, b].unsqueeze(2).broadcast_to([P, tiles, P]), ALU.mult), t)
    for b, c, _, ps in blocks:
        t = pe.do(lambda e: e.matmul(ps[:, 0:w], g.ones[:], diag[:, b], start=True, stop=True), inv_t[b])
        inv = ps[:, 0:w]
        if weight is None:
            t = dve.do(lambda e: e.tensor_tensor(dst[:, :, c], base[:, :, c], inv.unsqueeze(1).broadcast_to([P, KT, w]), ALU.mult),
                       t, base_t[b], list(dst_free))
        else:
            for k in range(KT):
                t2 = dve.do(lambda e: e.scalar_tensor_tensor(dst[:, k, c], base[:, k, c], weight[:, k:k + 1],
                                                             inv, ALU.mult, ALU.mult),
                            t, base_t[b], list(dst_free))
            t = t2
        out = [t]
        if split:
            hi, lo = split
            th = act.do(lambda e: e.activation(hi[:, :, c], dst[:, :, c], ACT.Copy), t)
            tl = dve.do(lambda e: e.tensor_tensor(lo[:, :, c], dst[:, :, c], fr(hi[:, :, c]), ALU.subtract), th)
            out += [th, tl]
        done.append(out)
    return done


def matmul3(lane, out, pairs, *tokens, start=True, stop=True, signal=True):
    passes = []
    for lh, ll, rh, rl in pairs:
        passes.append((lh, rh))
        if ll is not None:
            passes.append((ll, rh))
        if rl is not None:
            passes.append((lh, rl))
    for n, (a, b) in enumerate(passes):
        last = n == len(passes) - 1
        t = lane.do(lambda e: e.matmul(out, a, b, start=start and n == 0, stop=stop and last, skip_group_check=True),
                    *(tokens if n == 0 else ()), signal=signal and last)
    return t


class Item:

    def __init__(self, at, multiply, empty):
        self.at, self.multiply, self.empty = at, multiply, empty


ORDER = (0, 4, 1, 5, 2, 6, 3, 7)
LAST = [max(half, key=ORDER.index) for half in (range(0, 4), range(4, 8))]
SIDE = (6, 7)
NPROB = 4
LAG = 4


def side_bank(g):
    b = SIDE[g.side % 2]
    g.side += 1
    return b, g.ps[:, b, :], g.pr.readers.get(f"side{b}")


class Softmax:

    def __init__(self, g, groups, heads, score_passes, value_passes, take_output, both=False):
        self.g, self.pr, self.both = g, g.pr, both
        self.score_passes, self.value_passes, self.take_output = score_passes, value_passes, take_output
        self.units = [(gr, h, i) for gr in range(groups) for h in range(heads) for i in ORDER]
        self.prob_ready, self.exp_done, self.pT_ready, self.turned, self.hi_done = {}, {}, {}, {}, {}

    def scores(self, u):
        g, pe, rd = self.g, self.pr.pe, self.pr.readers
        gr, h, i = self.units[u]
        bank, width, key = 2 * (u % 2), (i + 1) * P, f"scores{u % 2}"
        for c in range(0, width, HALF):
            n = min(HALF, width - c)
            matmul3(pe, g.ps[:, bank + c // HALF, 0:n], self.score_passes(gr, h, i, slice(c, c + n)),
                    rd.get(f"ready{gr % 2}"), rd.get(key), stop=(c + n != width), signal=False)
        d = width - P
        t = pe.do(lambda e: e.matmul(g.ps[:, bank + d // HALF, d % HALF:d % HALF + P], g.ident_b[:], g.mask_b[:],
                                     start=False, stop=True, skip_group_check=True))
        rd[f"scored{gr % 2}"] = [t]
        return t

    def maximum(self, u, t):
        g, rd = self.g, self.pr.readers
        bank, width, slot = 2 * (u % 2), (self.units[u][2] + 1) * P, u % NPROB
        src = g.ps_flat[:, bank * HALF:bank * HALF + width]
        return self.pr.dve.do(lambda e: e.tensor_reduce(g.negmax[:, slot:slot + 1], src, AX.X, ALU.max, negate=True),
                              t, rd.get(f"prob{slot}"))

    def exponential(self, u, t):
        g, rd = self.g, self.pr.readers
        bank, width, slot = 2 * (u % 2), (self.units[u][2] + 1) * P, u % NPROB
        src = g.ps_flat[:, bank * HALF:bank * HALF + width]
        te = self.pr.act.do(lambda e: e.activation(g.prob[:, slot, 0:width], src, ACT.Exp, bias=g.negmax[:, slot:slot + 1],
                                                   accum_out=g.rowsum[:, slot:slot + 1]), t, rd.get(f"prob{slot}"))
        rd[f"scores{u % 2}"] = [te]
        self.exp_done[u] = te

    def divide(self, u):
        g = self.g
        width, slot = (self.units[u][2] + 1) * P, u % NPROB
        inv, prob = g.rowinv[:, slot:slot + 1], g.prob[:, slot, 0:width]
        ti = self.pr.dve.do(lambda e: e.reciprocal(inv, g.rowsum[:, slot:slot + 1]), self.exp_done[u],
                            self.pr.readers.get(f"prob{slot}"))
        self.prob_ready[u] = self.pr.pool.do(lambda e: e.tensor_scalar(prob, prob, inv, 1.0, ALU.mult, ALU.mult), ti)

    def transposes(self, u):
        g, rd = self.g, self.pr.readers
        i, slot = self.units[u][2], u % NPROB
        self.turned[u] = []
        for j0 in range(0, i + 1, 4):
            n, b = min(4, i + 1 - j0), (4 + j0 // 4 if i >= 4 else 1)
            for j in range(n):
                t = self.pr.pe.do(lambda e: e.transpose(g.ps[:, b, j * P:j * P + P],
                                                        g.prob[:, slot, (j0 + j) * P:(j0 + j + 1) * P], g.ident[:]),
                                  self.prob_ready[u], rd.get(f"bank{b}"), signal=(j == n - 1))
            self.turned[u].append((j0, n, b, t))
        rd[f"prob{slot}"] = [t]

    def split_parts(self, u):
        g, i = self.g, self.units[u][2]
        qb, cols = i // 4, slice(i % 4 * P, i % 4 * P + P)
        for j0, n, b, t in self.turned[u]:
            src = g.ps[:, b, 0:n * P].rearrange("p (j q) -> p j q", j=n)
            yield b, src, g.pT_hi[qb][:, j0:j0 + n, cols], g.pT_lo[qb][:, j0:j0 + n, cols], t

    def split_hi(self, u):
        free = self.pr.readers.get(f"pT{self.units[u][2] // 4}")
        self.hi_done[u] = [self.pr.act.do(lambda e: e.activation(hi, src, ACT.Copy), t, free)
                           for b, src, hi, lo, t in self.split_parts(u)]

    def split_lo(self, u):
        gr, h, i = self.units[u]
        rd = self.pr.readers
        free = rd.get(f"pT{i // 4}")
        for (b, src, hi, lo, t), th in zip(self.split_parts(u), self.hi_done[u]):
            tl = self.pr.dve.do(lambda e: e.tensor_tensor(lo, src, fr(hi), ALU.subtract), th, free)
            rd[f"bank{b}"] = [th, tl]
            self.pT_ready.setdefault((gr, h, i // 4), []).extend([th, tl])

    def values(self, gr, h, qb):
        g, pe, rd = self.g, self.pr.pe, self.pr.readers
        tiles = 4 * qb + 4
        bank, out, free = side_bank(g)
        tokens = [self.pT_ready[gr, h, qb], free, rd.get(f"ready{gr % 2}"), rd.get("v_ready")]
        for j in range(tiles):
            q = max(0, j - 4 * qb) * P
            passes = self.value_passes(gr, h, j, g.pT_hi[qb][:, j, q:HALF], g.pT_lo[qb][:, j, q:HALF])
            for n, (a, b) in enumerate(passes):
                end = j == tiles - 1 and n == len(passes) - 1
                t = pe.do(lambda e: e.matmul(out[:, q:HALF], a, b, start=(j == 0 and n == 0), stop=end,
                                             skip_group_check=True), *tokens, signal=end)
                tokens = []
        rd[f"pT{qb}"] = rd[f"attended{gr % 2}"] = [t]

        def empty():
            for free in self.take_output(gr, h, qb, out, t):
                if free:
                    rd[f"side{bank}"] = free
                yield

        return empty

    def run(self, items):
        n, items, due, s, scored = len(self.units), list(items), [], 0, {}
        new, old = [], []
        self.g.side = 0
        while s < n + LAG or due or items or new or old:
            if s < n:
                scored[s] = self.scores(s)
            old, new = new, []
            late = [e for e in old if next(e, self) is not self]
            if LAG <= s < n + LAG:
                self.split_hi(s - LAG)
            if 1 <= s <= n:
                self.exponential(s - 1, self.maximum(s - 1, scored[s - 1]))
            if 2 <= s <= n + 1:
                self.divide(s - 2)
            if LAG <= s < n + LAG:
                self.split_lo(s - LAG)
            old = [e for e in late if next(e, self) is not self]
            if due:
                new.append(self.values(*due.pop(0))())
            if items and items[0].at <= s and (self.both or not new):
                it = items.pop(0)
                it.multiply()
                new.append(it.empty())
            if 3 <= s <= n + 2:
                self.transposes(s - 3)
            if LAG <= s < n + LAG:
                gr, h, i = self.units[s - LAG]
                if i in LAST:
                    due.append((gr, h, i // 4))
            new = old + new
            s += 1


def softmax_buffers(g, tag):
    pr = g.pr
    g.prob = pr.sb(tag + "prob", [P, NPROB, N])
    g.negmax = pr.sb(tag + "negmax", [P, NPROB])
    g.rowsum = pr.sb(tag + "rowsum", [P, NPROB])
    g.rowinv = pr.sb(tag + "rowinv", [P, NPROB])
    g.pT_hi = [pr.sb(f"{tag}pT_hi{qb}", [P, 4 * qb + 4, HALF], F32R) for qb in range(NH2)]
    g.pT_lo = [pr.sb(f"{tag}pT_lo{qb}", [P, 4 * qb + 4, HALF], F32R) for qb in range(NH2)]


def project_out(g, wo, oT, tiles, at, tokens, name="oT"):
    pr = g.pr
    rd = pr.readers

    def item(m, qb):
        cc, mm = slice(qb * HALF, qb * HALF + HALF), slice(m * P, m * P + P)
        t = []

        def multiply():
            t.extend(side_bank(g))
            t.append(matmul3(pr.pe, t[1], [(wo[0][:, k, mm], wo[1][:, k, mm], oT[0][:, k, cc], oT[1][:, k, cc])
                                                       for k in range(tiles)], t[2], rd.get("o_split"), tokens))
            if (m, qb) == (KT - 1, NH2 - 1):
                rd[name] = rd["wo"] = [t[3]]

        def empty():
            yield
            tx = pr.dve.do(lambda e: e.tensor_tensor(g.x[:, m, cc], g.x[:, m, cc], t[1], ALU.add), t[3],
                           rd.get(f"x{m}{qb}"))
            rd[f"side{t[0]}"] = rd[f"x{m}{qb}"] = [tx]

        return Item(at, multiply, empty)

    return [item(m, qb) for m in range(KT) for qb in range(NH2)]


def pool_split(g, hi, lo, src, *tokens):
    a = g.pr.pool.do(lambda e: e.tensor_scalar(hi, src, 1.0, 1.0, ALU.mult, ALU.mult), *tokens)
    return g.pr.pool.do(lambda e: e.tensor_tensor(lo, src, fr(hi), ALU.subtract), a)


A_HEADS, A_KV, A_HD = 32, 8, 64
A_GRP = A_HEADS // A_KV
A_W = (A_GRP + 2) * A_HD


def attn_a(g, ins):
    pr = g.pr
    pe, dve, act, pool, sp, rd = pr.pe, pr.dve, pr.act, pr.pool, pr.sp, pr.readers
    with pr.phase():
        h_hi, h_lo = pr.sb("a_h_hi", [P, KT, N], F32R), pr.sb("a_h_lo", [P, KT, N], F32R)
        cos, sin = pr.sb("a_cos", [P, TT, A_HD]), pr.sb("a_sin", [P, TT, A_HD])
        w_raw, o_raw = pr.sb("a_w_raw", [P, KT, A_W]), pr.sb("a_o_raw", [P, 2, D])
        w_hi, w_lo = pr.sb("a_w_hi", [P, KT, A_W], F32R), pr.sb("a_w_lo", [P, KT, A_W], F32R)
        o_hi, o_lo = pr.sb("a_o_hi", [P, 2, D], F32R), pr.sb("a_o_lo", [P, 2, D], F32R)
        s_tab, s_w, s_o = pr.slot("a_tables"), pr.slot("a_w_loaded"), pr.slot("a_o_loaded")
        sp.dma(s_tab, lambda: cos[:], lambda: ins["a_cos"])
        sp.dma(s_tab, lambda: sin[:], lambda: ins["a_sin"])
        first = sp.dma(s_w, lambda: w_raw[:], lambda: ins["a_w"][0])
        sp.dma(s_o, lambda: o_raw[:], lambda: ins["a_o"][0])
        w_first = pool_split(g, w_hi[:], w_lo[:], w_raw[:], first)
        sp.dma(s_w, lambda: w_raw[:], lambda: ins["a_w"][1], w_first)
        with pr.phase():
            h = pr.sb("a_h", [P, KT, N])
            normalise(g, "a_n", g.x, h, N, 1e-5, src_ready=g.x_ready, centre=True, split=(h_hi, h_lo))

        two = range(2)
        q_st = [pr.sb(f"a_q{b}", [P, A_GRP, N], F32R) for b in two]
        k_hi = [pr.sb(f"a_k_hi{b}", [P, N], F32R) for b in two]
        k_lo = [pr.sb(f"a_k_lo{b}", [P, N], F32R) for b in two]
        v_st = [pr.sb(f"a_v{b}", [P, TT, 2 * A_HD], F32R) for b in two]
        t1, t2 = pr.sb("a_t1", [P, 2, (A_GRP + 1) * A_HD]), pr.sb("a_t2", [P, 2, (A_GRP + 1) * A_HD])
        qk = pr.sb("a_qk", [P, TT, A_W])
        o_low, o_sum = pr.sb("a_o_low", [P, HALF]), pr.sb("a_o_sum", [P, 2, HALF])
        oT_hi, oT_lo = pr.sb("a_oT_hi", [P, 2, N], F32R), pr.sb("a_oT_lo", [P, 2, N], F32R)
        softmax_buffers(g, "a_")
        heads, HH = A_GRP + 1, A_HD // 2
        rows = (slice(0, 64), slice(64, 128))

        def make_qkv(b, at, next_w):
            ready, qk_ready = [], {}

            def token_tile(t):
                par, tok, tp = t % 2, slice(t * P, t * P + P), []

                def multiply():
                    rd[f"ready{b}"] = ready
                    tp.extend(side_bank(g))
                    tp.append(matmul3(pe, tp[1][:, 0:A_W], [(h_hi[:, k, tok], h_lo[:, k, tok], w_hi[:, k], w_lo[:, k])
                                                            for k in range(KT)], rd.get("w_split"), tp[2]))

                def empty():
                    bank, out, _, made = tp
                    x3 = out[:, 0:heads * A_HD].rearrange("p (h d) -> p h d", d=A_HD)
                    c3 = cos[:, t].unsqueeze(1).broadcast_to([P, heads, A_HD])
                    s_low = sin[:, t, 0:HH].unsqueeze(1).broadcast_to([P, heads, HH])
                    s_high = sin[:, t, HH:].unsqueeze(1).broadcast_to([P, heads, HH])
                    r1, r2 = (x[:, par].rearrange("p (h d) -> p h d", d=A_HD) for x in (t1, t2))
                    vs, v = out[:, heads * A_HD:A_W], v_st[b]
                    vh = act.do(lambda e: e.activation(v[:, t, 0:A_HD], vs, ACT.Copy), made, rd.get(f"attended{b}"))
                    yield
                    a1 = dve.do(lambda e: e.tensor_tensor(r1, x3, c3, ALU.mult), vh, rd.get(f"rope{par}"))
                    dve.do(lambda e: e.tensor_tensor(r2[:, :, 0:HH], x3[:, :, HH:], s_low, ALU.mult))
                    a3 = dve.do(lambda e: e.tensor_tensor(r2[:, :, HH:], x3[:, :, 0:HH], s_high, ALU.mult))
                    vl = dve.do(lambda e: e.tensor_tensor(v[:, t, A_HD:], vs, fr(v[:, t, 0:A_HD]), ALU.subtract), vh)
                    pool.do(lambda e: e.tensor_tensor(qk[:, t, 0:heads * A_HD], t1[:, par], t2[:, par], ALU.add),
                            a1, a3, rd.get("qk"))
                    a5 = pool.do(lambda e: e.tensor_tensor(qk[:, t, heads * A_HD:], t1[:, par, A_GRP * A_HD:],
                                                           t2[:, par, A_GRP * A_HD:], ALU.add))
                    rd[f"rope{par}"], rd[f"side{bank}"], qk_ready[t] = [a5], [vl, vh], a5
                    ready.extend([vh, vl])
                    if t == TT - 1:
                        loaded = Token(s_w, s_w.n, pr.loop)
                        rd["w_split"] = [pool_split(g, w_hi[:], w_lo[:], w_raw[:], loaded, made)]
                        sp.dma(s_w, lambda: w_raw[:],
                               lambda: ins["a_w"][bass.ds(next_w(), 1)].rearrange("o p a b -> (o p) a b"), rd["w_split"])

                return Item(at, multiply, empty)

            def turned(c, pair):
                cc, tp = slice(c * HALF, c * HALF + HALF), []

                def multiply():
                    tp.extend(side_bank(g))
                    for t in range(4):
                        tt = c * 4 + t
                        x = pe.do(lambda e: e.transpose(tp[1][:, t * P:t * P + P], qk[:, tt, pair * P:pair * P + P], g.ident[:]),
                                  qk_ready[tt], tp[2], signal=(t == 3))
                    tp.append(x)
                    rd["qk"] = [x]

                def empty():
                    bank, out, _, made = tp
                    free = rd.get(f"attended{b}")
                    if pair < 2:
                        parts = [(q_st[b][:, 2 * pair + e2], rows[e2], rows[1 - e2]) for e2 in range(2)]
                        hi = [act.do(lambda e: e.activation(q[mine, cc], out[mine], ACT.Copy, scale=A_HD ** -0.5), made, free)
                              for q, mine, other in parts]
                        yield
                        lo = [dve.do(lambda e: e.scalar_tensor_tensor(q[other, cc], out[mine], A_HD ** -0.5, fr(q[mine, cc]),
                                                                      ALU.mult, ALU.subtract), hi, free)
                              for q, mine, other in parts]
                        used = hi + lo
                    else:
                        kh, kl = k_hi[b], k_lo[b]
                        hi = act.do(lambda e: e.activation(kh[:, cc], out, ACT.Copy), made, free)
                        yield
                        lo = dve.do(lambda e: e.tensor_tensor(kl[:, cc], out, fr(kh[:, cc]), ALU.subtract), hi, free)
                        used = [hi, lo]
                    rd[f"side{bank}"] = used
                    ready.extend(used)

                return Item(at, multiply, empty)

            return [token_tile(t) for t in range(TT)] + [turned(c, pair) for c in range(NH2) for pair in range(3)]

        def split_o(next_o):
            loaded = Token(s_o, s_o.n, pr.loop)
            rd["o_split"] = [pool_split(g, o_hi[:], o_lo[:], o_raw[:], loaded, rd.get("wo"))]
            sp.dma(s_o, lambda: o_raw[:], lambda: ins["a_o"][bass.ds(next_o(), 1)].rearrange("o p a b -> (o p) a b"),
                   rd["o_split"])

        def score_passes(b, hd, t, keys):
            q = q_st[b][:, hd, t * P:t * P + P]
            return [(q, None, k_hi[b][:, keys], None), (q, None, k_lo[b][:, keys], None)]

        def value_passes(b, hd, j, hi, lo):
            return [(v_st[b][:, j], hi), (v_st[b][:, j], lo)]

        def take_output(b, hd, qb, out, t):
            pair, half, cc = hd // 2, rows[hd % 2], slice(qb * HALF, qb * HALF + HALF)
            low = act.do(lambda e: e.activation(o_low[64:128], out[64:128], ACT.Copy), t, rd.get("o_low"))
            yield
            tot = dve.do(lambda e: e.tensor_tensor(o_sum[half, qb], out[0:64], o_low[64:128], ALU.add), low,
                         rd.get(f"o_sum{qb}"))
            rd["o_low"] = [tot]
            yield [tot]
            if hd % 2 == 1:
                hi = act.do(lambda e: e.activation(oT_hi[:, pair, cc], o_sum[:, qb], ACT.Copy), tot, rd.get("oT"))
                yield
                lo = pool.do(lambda e: e.tensor_tensor(oT_lo[:, pair, cc], o_sum[:, qb], fr(oT_hi[:, pair, cc]), ALU.subtract),
                             hi, rd.get("oT"))
                rd[f"o_sum{qb}"] = [hi, lo]
                out_ready[b] += [hi, lo]

        out_ready = {}
        units = A_GRP * TT
        after = LAG + 5

        def turn(i):
            out_ready[0], out_ready[1] = [], []
            wo, oT = (o_hi, o_lo), (oT_hi, oT_lo)

            def out_items(b, at):
                items = project_out(g, wo, oT, 2, at, out_ready[b])
                return items

            split_o(lambda: (2 * i + 1) % A_KV)
            items = make_qkv(1, 1, lambda: (2 * i + 3) % A_KV)
            out0 = out_items(0, units + after)
            last = out0[-1].multiply

            def last_then_split():
                last()
                split_o(lambda: (2 * i + 2) % A_KV)

            out0[-1].multiply = last_then_split
            items += out0
            items += make_qkv(0, units + after, lambda: (2 * i + 4) % A_KV)
            items += out_items(1, 2 * units + after)
            Softmax(g, 2, A_GRP, score_passes, value_passes, take_output).run(items)

        pr.fence()
        g.side = 0
        for it in make_qkv(0, 0, lambda: 2):
            it.multiply()
            list(it.empty())
        pr.run_loop(A_KV // 2, turn)


B_HEADS, B_HD = 16, 128
B_PAIR = 2
B_TURN = 4
B_SCALE = 1.0 / math.sqrt(B_HD)


def attn_b(g, ins):
    pr = g.pr
    pe, dve, act, pool, sp, rd = pr.pe, pr.dve, pr.act, pr.pool, pr.sp, pr.readers
    with pr.phase():
        h_hi, h_lo = pr.sb("b_h_hi", [P, KT, N], F32R), pr.sb("b_h_lo", [P, KT, N], F32R)
        w_raw, wv_raw, o_raw = (pr.sb("b_" + n, [P, 2, D]) for n in ("w_raw", "wv_raw", "o_raw"))
        w_hi, w_lo, wv_hi, wv_lo = (pr.sb("b_" + n, [P, KT, 2 * B_HD], F32R) for n in ("w_hi", "w_lo", "wv_hi", "wv_lo"))
        o_hi, o_lo = pr.sb("b_o_hi", [P, B_PAIR, D], F32R), pr.sb("b_o_lo", [P, B_PAIR, D], F32R)
        bias = pr.sb("b_bias", [P, 3, B_HEADS])
        bias_qk, bias_v = pr.sb("b_bias_qk", [P, 2, 2]), pr.sb("b_bias_v", [P, 2])
        b_out = pr.sb("b_bias_out", [P, KT])
        s_b, s_o = pr.slot("b_bias_loaded"), pr.slot("b_o_loaded")
        s_w, s_wv = pr.slot("b_qk_loaded"), pr.slot("b_v_loaded")
        sp.dma(s_b, lambda: bias[:], lambda: ins["b_bias"])
        biases = sp.dma(s_b, lambda: b_out[:], lambda: ins["b_bias_out"])
        first = sp.dma(s_w, lambda: w_raw[:], lambda: ins["b_qk"][0])
        first_v = sp.dma(s_wv, lambda: wv_raw[:], lambda: ins["b_v"][0])
        sp.dma(s_o, lambda: o_raw[:], lambda: ins["b_o"][0])

        def load(slot, raw, name, which, *tokens):
            sp.dma(slot, lambda: raw[:], lambda: ins[name][bass.ds(which(), 1)].rearrange("o p a b -> (o p) a b"), *tokens)

        def split_w(*tokens):
            q = w_raw[:, :, 0:B_HD]
            a = pool.do(lambda e: e.tensor_scalar(q, q, B_SCALE, 1.0, ALU.mult, ALU.mult), *tokens)
            return pool_split(g, w_hi[:], w_lo[:], w_raw[:], a)

        load(s_w, w_raw, "b_qk", lambda: 1, split_w(first))
        load(s_wv, wv_raw, "b_v", lambda: 1, pool_split(g, wv_hi[:], wv_lo[:], wv_raw[:], first_v))
        with pr.phase():
            h = pr.sb("b_h", [P, KT, N])
            normalise(g, "b_n", g.x, h, N, 1e-5, src_ready=g.x_ready, centre=True, split=(h_hi, h_lo))
            act.do(lambda e: e.activation(bias[:, 0], bias[:, 0], ACT.Copy, scale=B_SCALE), biases)
            for k in range(KT):
                dve.do(lambda e: e.tensor_scalar(g.x[:, k], g.x[:, k], b_out[:, k:k + 1], None, ALU.add), biases, dve.last())

        two = range(2)
        q_hi, q_lo, k_hi, k_lo = ([pr.sb(f"b_{n}{b}", [P, N], F32R) for b in two] for n in ("q_hi", "q_lo", "k_hi", "k_lo"))
        v_hi, v_lo = (pr.sb("b_" + n, [P, TT, B_PAIR * B_HD], F32R) for n in ("v_hi", "v_lo"))
        oT_hi, oT_lo = ([pr.sb(f"b_{n}{b}", [P, B_PAIR, N], F32R) for b in two] for n in ("oT_hi", "oT_lo"))
        softmax_buffers(g, "b_")

        def make_qk(b, at, head, next_w):
            ready = []

            def qk_half(which, c):
                hi_t, lo_t = ((q_hi, q_lo), (k_hi, k_lo))[which]
                cc = slice(c * HALF, c * HALF + HALF)
                col, tp = slice(which * B_HD, (which + 1) * B_HD), []

                def multiply():
                    rd[f"ready{b}"] = ready
                    tp.extend(side_bank(g))
                    tp.append(matmul3(pe, tp[1], [(w_hi[:, k, col], w_lo[:, k, col], h_hi[:, k, cc], h_lo[:, k, cc])
                                                  for k in range(KT)], rd.get("w_split"), tp[2]))
                    if (which, c) == (1, NH2 - 1):
                        rd["w_split"] = [split_w(Token(s_w, s_w.n, pr.loop), tp[3])]
                        load(s_w, w_raw, "b_qk", next_w, rd["w_split"])

                def empty():
                    bank, out, _, made = tp
                    if (which, c) == (0, 0):
                        src = lambda: bias[:, 0:2, bass.ds(head(), 1)].rearrange("p a o -> p (a o)")
                        rd[f"bias{b}"] = [act.do(lambda e: e.activation(bias_qk[:, b], src(), ACT.Copy), rd.get(f"biased{b}"))]
                    bb, free = bias_qk[:, b, which:which + 1], rd.get(f"scored{b}")
                    hi = act.do(lambda e: e.activation(hi_t[b][:, cc], out, ACT.Identity, bias=bb), made,
                                rd[f"bias{b}"], free)
                    yield
                    lo = dve.do(lambda e: e.scalar_tensor_tensor(lo_t[b][:, cc], out, bb, fr(hi_t[b][:, cc]),
                                                                 ALU.add, ALU.subtract), hi, free)
                    rd[f"side{bank}"] = rd[f"biased{b}"] = [lo]
                    ready.extend([hi, lo])

                return Item(at, multiply, empty)

            return [qk_half(which, c) for which in range(2) for c in range(NH2)]

        def make_v(at, pair, next_w):

            def v_tiles(t0):
                tp = []

                def multiply():
                    tp.extend(side_bank(g))
                    for j in range(2):
                        tok = slice((t0 + j) * P, (t0 + j + 1) * P)
                        x = matmul3(pe, tp[1][:, j * D:(j + 1) * D],
                                    [(h_hi[:, k, tok], h_lo[:, k, tok], wv_hi[:, k], wv_lo[:, k]) for k in range(KT)],
                                    rd.get("wv_split"), tp[2])
                    tp.append(x)
                    if t0 == TT - 2:
                        rd["wv_split"] = [pool_split(g, wv_hi[:], wv_lo[:], wv_raw[:], Token(s_wv, s_wv.n, pr.loop), x)]
                        load(s_wv, wv_raw, "b_v", next_w, rd["wv_split"])

                def empty():
                    bank, out, _, made = tp
                    free = [rd.get("attended0"), rd.get("attended1")]
                    vh, vl = (x[:, t0:t0 + 2].rearrange("p t n -> p (t n)") for x in (v_hi, v_lo))
                    hi = act.do(lambda e: e.activation(vh, out, ACT.Copy), made, free)
                    if t0 == 0:
                        src = lambda: bias[:, 2, bass.ds(pair() * B_PAIR, B_PAIR)]
                        rd["v_bias"] = [act.do(lambda e: e.activation(bias_v[:], src(), ACT.Copy), rd.get("v_biased"))]
                    yield
                    lo = dve.do(lambda e: e.tensor_tensor(vl, out, fr(vh), ALU.subtract), hi, free)
                    rd[f"side{bank}"] = [lo]
                    rd["v_ready"] = [hi, lo]

                return Item(at, multiply, empty)

            return [v_tiles(t0) for t0 in range(0, TT, 2)]

        def split_o(next_o, loaded):
            rd["o_split"] = [pool_split(g, o_hi[:], o_lo[:], o_raw[:], loaded, rd.get("wo"))]
            load(s_o, o_raw, "b_o", next_o, rd["o_split"])

        def score_passes(hd, _, t, keys):
            b, tok = hd % 2, slice(t * P, t * P + P)
            return [(q_hi[b][:, tok], q_lo[b][:, tok], k_hi[b][:, keys], k_lo[b][:, keys])]

        def value_passes(hd, _, j, hi, lo):
            e2 = hd % B_PAIR
            vh, vl = v_hi[:, j, e2 * B_HD:(e2 + 1) * B_HD], v_lo[:, j, e2 * B_HD:(e2 + 1) * B_HD]
            return [(vh, hi), (vh, lo), (vl, hi)]

        def take_output(hd, _, qb, out, t):
            cc, bb = slice(qb * HALF, qb * HALF + HALF), bias_v[:, hd % 2:hd % 2 + 1]
            pair, e2 = hd // B_PAIR % 2, hd % B_PAIR
            o, ol = oT_hi[pair][:, e2, cc], oT_lo[pair][:, e2, cc]
            hi = act.do(lambda e: e.activation(o, out, ACT.Identity, bias=bb), t, rd.get(f"oT{pair}"), rd.get("v_bias"))
            yield
            lo = dve.do(lambda e: e.scalar_tensor_tensor(ol, out, bb, fr(o), ALU.add, ALU.subtract), hi, rd.get(f"oT{pair}"))
            rd["v_biased"] = [lo]
            out_ready[hd // B_PAIR] += [hi, lo]
            yield [lo]

        out_ready = {}

        def turn(i):
            items, pairs = [], B_TURN // B_PAIR
            for hd in range(B_TURN):
                items += make_qk((hd + 1) % 2, hd * TT, lambda hd=hd: (B_TURN * i + hd + 1) % B_HEADS,
                                 lambda hd=hd: (B_TURN * i + hd + 3) % B_HEADS)
            for p in range(pairs):
                out_ready[p] = []
                items += make_v(p * B_PAIR * TT + (LAG + 2 if p else 0), lambda p=p: (pairs * i + p) % (B_HEADS // B_PAIR),
                                lambda p=p: (pairs * i + p + 2) % (B_HEADS // B_PAIR))
                done = (p + 1) * B_PAIR * TT + LAG + 3
                wo = project_out(g, (o_hi, o_lo), (oT_hi[p % 2], oT_lo[p % 2]), B_PAIR, done, out_ready[p], f"oT{p % 2}")
                wo[2].at = wo[3].at = done + TT // 2 + 1

                def last_then_split(p=p, last=wo[-1].multiply):
                    last()
                    split_o(lambda: (pairs * i + p + 2) % (B_HEADS // B_PAIR), Token(s_o, s_o.n, pr.loop))

                wo[-1].multiply = last_then_split
                items += wo
            Softmax(g, B_TURN, 1, score_passes, value_passes, take_output).run(sorted(items, key=lambda it: it.at))

        split_o(lambda: 1, Token(s_o, s_o.n, None))
        pr.fence()
        g.side = 0
        for it in make_qk(0, 0, lambda: 0, lambda: 2):
            it.multiply()
            list(it.empty())
        pr.run_loop(B_HEADS // B_TURN, turn)


F_HEADS, F_KV, F_HD, F_I = 16, 8, 128, 1024
F_S = int(N * 0.125)
F_SCALE = 1.0 / math.sqrt(F_HD)
FI_T = F_I // P


def ffn(g, ins, tag):
    assert F_S == P
    pr = g.pr
    pe, dve, act, pool, sp = pr.pe, pr.dve, pr.act, pr.pool, pr.sp
    ps = g.ps
    with pr.phase():
        def sb(name, shape, dt=F32):
            return pr.sb(f"{tag}_{name}", shape, dt)

        def load(name, shape):
            buf, slot = sb(name, shape), pr.slot(f"{tag}_{name}_loaded")
            return buf, sp.dma(slot, lambda: buf[:], lambda: ins["f_" + name])

        wr, l_wr = load("wr", [P, KT])
        trope, l_trope = load("rope", [P, TT, 2, P])
        ln, l_ln = load("ln", [P, 2, KT])
        bqk, l_bqk = load("bqk", [P, F_HEADS + F_KV])
        bv, l_bv = load("bv", [1, F_KV * F_HD])
        wq, l_wq = load("wq", [P, KT, F_HEADS * F_HD])
        wk, l_wk = load("wk", [P, KT, F_KV * F_HD])
        wv, l_wv = load("wv", [P, KT, F_KV * F_HD])
        wo, l_wo = load("wo", [P, F_HEADS, D])
        wg, l_wg = load("wg", [P, KT, F_I])
        wu, l_wu = load("wu", [P, KT, F_I])
        wd, l_wd = load("wd", [P, FI_T, D])

        upper, ramp, ones_b = sb("upper", [P, P]), sb("ramp", [P, P]), sb("ones_b", [P, 1], BF16)
        c1 = pool.do(lambda e: e.memset(upper[:], 1.0))
        upper_t = pool.do(lambda e: e.affine_select(out=upper[:], in_=upper[:], compare_op=ALU.is_ge, fill=0.0, base=-1,
                                                    pattern=[[1, P]], channel_multiplier=-1), c1)
        ramp_t = pool.do(lambda e: e.iota(ramp[:], pattern=[[1, P]], base=0, channel_multiplier=0,
                                          allow_small_or_imprecise_dtypes=True))
        ones_t = pool.do(lambda e: e.memset(ones_b[:], 1.0))

        h = sb("h", [P, KT, N])
        hn = normalise(g, f"{tag}_n0", g.x, h, N, 1e-5, centre=True)
        h_ready = [o[0] for o in hn]
        x_plus = pool.do(lambda e: e.tensor_tensor(g.x[:], g.x[:], h[:], ALU.add), h_ready)

        wrb = sb("wrb", [P, KT, P])
        t = dve.do(lambda e: e.tensor_copy(wrb[:], wr[:, :].unsqueeze(2).broadcast_to([P, KT, P])), l_wr)
        for c in range(NH2):
            for k in range(KT):
                s_mm = pe.do(lambda e: e.matmul(ps[:, 4 + c, :], wrb[:, k], h[:, k, c * HALF:(c + 1) * HALF],
                                                start=(k == 0), stop=(k == KT - 1)), t, h_ready)
        s = sb("s", [P, N])
        s_t = dve.do(lambda e: e.tensor_copy(s[:], g.ps_flat[:, 4 * HALF:6 * HALF]), s_mm)
        h_tok = sb("h_tok", [P, TT, D])
        h_tok_t = []
        for b in range(4):
            for j in range(4):
                c, k = 2 * b + j // 2, j % 2
                t = pe.do(lambda e: e.transpose(ps[:, b, j * P:j * P + P], h[:, k, c * P:c * P + P], g.ident[:]), h_ready)
            h_tok_t.append(act.do(lambda e: e.activation(h_tok[:, 2 * b:2 * b + 2].rearrange("p a b -> p (a b)"), ps[:, b, :],
                                                         ACT.Copy), t))
        diag, s_col = sb("diag", [P, TT, P]), sb("s_col", [P, TT])
        t = dve.do(lambda e: e.tensor_tensor(diag[:], s[:, :].rearrange("p (c q) -> p c q", q=P),
                                             g.ident[:].unsqueeze(1).broadcast_to([P, TT, P]), ALU.mult), s_t)
        t = dve.do(lambda e: e.tensor_reduce(s_col[:], diag[:], AX.X, ALU.add), t)
        prob, probT = sb("prob", [P, F_HEADS, P]), sb("probT", [P, F_HEADS, P])
        beats = [x[:].rearrange("p a b -> p (a b)").bitcast(BF16).rearrange("p (j q) -> p j q", q=N) for x in (prob, probT)]
        ties = sb("ties", [P, TT, P], BF16)
        ranks, beats_t = ps[:, 5, 0:TT], []
        for j in range(TT):
            own, hi, lane = s_col[:, j:j + 1], (j + 1) * P, (pool if j % 4 == 3 else dve)
            b_t = [lane.do(lambda e: e.tensor_scalar(beats[j // 4][:, j % 4, 0:hi], s[:, 0:hi], own, None, ALU.is_lt), t)]
            if hi < N:
                b_t.append(lane.do(lambda e: e.tensor_scalar(beats[j // 4][:, j % 4, hi:N], s[:, hi:N], own, None, ALU.is_le), t))
            b_t.append(dve.do(lambda e: e.scalar_tensor_tensor(ties[:, j], s[:, j * P:hi], own, upper[:],
                                                               ALU.is_equal, ALU.mult), t, upper_t))
            beats_t += b_t
        for c in range(TT):
            for j in range(TT):
                pe.do(lambda e: e.matmul(ranks[:, c:c + 1], beats[j // 4][:, j % 4, c * P:c * P + P], ones_b[:],
                                         start=(j == 0), stop=False), beats_t, ones_t, s_t)
            rank_t = pe.do(lambda e: e.matmul(ranks[:, c:c + 1], ties[:, c], ones_b[:], start=False, stop=True))
        sel = sb("sel", [P, TT])
        sel_t = dve.do(lambda e: e.tensor_scalar(sel[:], ranks, F_S - 0.5, None, ALU.is_lt), rank_t)
        within, total = ps[:, 6, 0:TT], ps[:, 7, 0:TT]
        t1 = pe.do(lambda e: e.matmul(within, upper[:], sel[:], start=True, stop=True), sel_t, upper_t)
        t2 = pe.do(lambda e: e.matmul(total, g.ones[:], sel[:], start=True, stop=True))
        upto, pos = sb("upto", [P, TT]), sb("pos", [P, TT])
        t = dve.do(lambda e: e.tensor_tensor_scan(upto[:], g.ones[:, 0:TT], total, 0.0, ALU.mult, ALU.add), t2)
        t = dve.do(lambda e: e.tensor_tensor(upto[:], upto[:], total, ALU.subtract), t)
        t = dve.do(lambda e: e.tensor_tensor(pos[:], upto[:], within, ALU.add), t)
        take = sb("take", [P, TT, P])
        for c in range(TT):
            take_t = dve.do(lambda e: e.tensor_scalar(take[:, c], ramp[:], pos[:, c:c + 1], sel[:, c:c + 1],
                                                      ALU.is_equal, ALU.mult), t, ramp_t)
        t = None
        for m in range(4):
            for c in range(TT):
                lhs = h_tok[:, c, m * P:m * P + P] if m < 2 else trope[:, c, m - 2]
                t = pe.do(lambda e: e.matmul(ps[:, 0, m * P:m * P + P], lhs, take[:, c], start=(c == 0), stop=(c == TT - 1)),
                          take_t, h_tok_t, l_trope)
        xs, rope = sb("xs", [P, KT, P]), sb("ropes", [P, 2, P])
        flat2 = "p a b -> p (a b)"
        xs_t = dve.do(lambda e: e.tensor_copy(xs[:, :].rearrange(flat2), ps[:, 0, 0:2 * P]), t)
        rope_t = dve.do(lambda e: e.tensor_copy(rope[:, :].rearrange(flat2), ps[:, 0, 2 * P:]))
        takeT = sb("takeT", [P, N])
        for b in range(2):
            for j in range(4):
                t = pe.do(lambda e: e.transpose(ps[:, 1 + b, j * P:j * P + P], take[:, 4 * b + j], g.ident[:]), h_tok_t)
            takeT_t = act.do(lambda e: e.activation(takeT[:, b * HALF:(b + 1) * HALF], ps[:, 1 + b, :], ACT.Copy), t)
        gate = sb("gate", [P, P])
        for k in range(KT):
            gate_mm = pe.do(lambda e: e.matmul(ps[:, 6, 0:P], wrb[:, k], xs[:, k], start=(k == 0), stop=(k == KT - 1)), xs_t,
                            dve.last())

        def rms(name, src, ready, which):
            dst, sq, inv = sb(name, [P, KT, P]), sb(name + "_sq", [P, KT, P]), sb(name + "_inv", [P, P])
            t = act.do(lambda e: e.activation(sq[:], src[:], ACT.Square), ready)
            for k in range(KT):
                t = pe.do(lambda e: e.matmul(ps[:, 7, 0:P], g.avg[:], sq[:, k], start=(k == 0), stop=(k == KT - 1)), t,
                          dve.last())
            t = act.do(lambda e: e.activation(inv[:], ps[:, 7, 0:P], ACT.Sqrt, bias=g.eps[:, 1:2]), t)
            t = dve.do(lambda e: e.reciprocal(inv[:], inv[:]), t)
            for k in range(KT):
                t2 = dve.do(lambda e: e.scalar_tensor_tensor(dst[:, k], src[:, k], ln[:, which, k:k + 1], inv[:],
                                                             ALU.mult, ALU.mult), t, l_ln, ready)
            return dst, t2

        h1, h1_t = rms("h1", xs, xs_t, 0)

        nqk = F_HEADS + F_KV
        qk = sb("qk", [P, nqk, P])
        qkb, r1, r2 = sb("qkb", [P, 2, 4, P]), sb("r1", [P, 2, 4, P]), sb("r2", [P, 2, 4, P])
        rope_free, bank_free, qk_t = [None, None], {}, []
        up_rows, down_rows = slice(64, 128), slice(0, 64)
        for n in range(nqk // 4):
            b, par = (0, 3, 4, 5)[n % 4], n % 2
            for j in range(4):
                hd = 4 * n + j
                w, col = (wq, hd) if hd < F_HEADS else (wk, hd - F_HEADS)
                for k in range(KT):
                    t = pe.do(lambda e: e.matmul(ps[:, b, j * P:j * P + P], w[:, k, col * P:col * P + P], h1[:, k],
                                                 start=(k == 0), stop=(k == KT - 1)), h1_t, l_wq, l_wk, s_t, rope_t,
                              bank_free.get(b))
            for j in range(4):
                t2 = act.do(lambda e: e.activation(qkb[:, par, j], ps[:, b, j * P:j * P + P], ACT.Identity,
                                                   bias=bqk[:, 4 * n + j:4 * n + j + 1]), t, l_bqk, rope_free[par])
            t = t2
            bank_free[b] = t
            a1 = dve.do(lambda e: e.tensor_tensor(r1[:, par], qkb[:, par], rope[:, 0].unsqueeze(1).broadcast_to([P, 4, P]),
                                                  ALU.mult), t, rope_t, rope_free[par])
            for src, dst in ((up_rows, down_rows), (down_rows, up_rows)):
                a2 = dve.do(lambda e: e.tensor_tensor(r2[dst, par], qkb[src, par],
                                                      rope[src, 1].unsqueeze(1).broadcast_to([64, 4, P]), ALU.mult), t, rope_t)
            t = pool.do(lambda e: e.tensor_tensor(qk[:, 4 * n:4 * n + 4], r1[:, par], r2[:, par], ALU.add), a1, a2)
            rope_free[par] = t
            qk_t.append(t)
        v = sb("v", [P, F_KV * F_HD])
        for c in range(2):
            cc = slice(c * HALF, (c + 1) * HALF)
            for k in range(KT):
                pe.do(lambda e: e.matmul(ps[:, 1 + c, :], h1[:, k], wv[:, k, cc], start=(k == 0), stop=False), l_wv, l_bv,
                      takeT_t)
            t = pe.do(lambda e: e.matmul(ps[:, 1 + c, :], g.ones[0:1, :], bv[0:1, cc], start=False, stop=True))
            v_t = act.do(lambda e: e.activation(v[:, cc], ps[:, 1 + c, :], ACT.Copy), t)

        oT = sb("oT", [P, F_HEADS, P])
        neg, rsum = sb("neg", [P, F_HEADS]), sb("rsum", [P, F_HEADS])
        nb = F_HEADS // 4
        stage = {}
        for n in range(nb):
            b, hs = (0, 3, 4, 5)[n], slice(4 * n, 4 * n + 4)
            for j in range(4):
                hd = 4 * n + j
                kv = F_HEADS + hd * F_KV // F_HEADS
                t = pe.do(lambda e: e.matmul(ps[:, b, j * P:j * P + P], qk[:, hd], qk[:, kv], start=True, stop=True),
                          qk_t, bank_free.get(b))
            t = dve.do(lambda e: e.tensor_tensor(prob[:, hs], ps[:, b, :].rearrange("p (j q) -> p j q", j=4),
                                                 g.mask[:].unsqueeze(1).broadcast_to([P, 4, P]), ALU.add), t)
            bank_free[b] = t
            stage[n] = t
        for n in range(nb):
            hs = slice(4 * n, 4 * n + 4)
            t = dve.do(lambda e: e.tensor_reduce(neg[:, hs], prob[:, hs], AX.X, ALU.max, negate=True), stage[n])
            stage[n] = dve.do(lambda e: e.tensor_scalar(neg[:, hs], neg[:, hs], F_SCALE, None, ALU.mult), t)
        for hd in range(F_HEADS):
            t = act.do(lambda e: e.activation(prob[:, hd], prob[:, hd], ACT.Exp, bias=neg[:, hd:hd + 1], scale=F_SCALE,
                                              accum_out=rsum[:, hd:hd + 1]), stage[hd // 4])
            if hd % 4 == 3:
                stage[hd // 4] = t
        for n in range(nb):
            hs = slice(4 * n, 4 * n + 4)
            t = dve.do(lambda e: e.reciprocal(rsum[:, hs], rsum[:, hs]), stage[n])
            t = dve.do(lambda e: e.tensor_tensor(prob[:, hs], prob[:, hs], rsum[:, hs].unsqueeze(2).broadcast_to([P, 4, P]),
                                                 ALU.mult), t)
            b = (0, 3, 4, 5)[n]
            for j in range(4):
                t = pe.do(lambda e: e.transpose(ps[:, b, j * P:j * P + P], prob[:, 4 * n + j], g.ident[:]), t, bank_free.get(b))
            stage[n] = act.do(lambda e: e.activation(probT[:, hs].rearrange(flat2), ps[:, b, :], ACT.Copy), t)
        for n in range(nb):
            b, hs = (0, 3, 4, 5)[n], slice(4 * n, 4 * n + 4)
            for j in range(4):
                hd = 4 * n + j
                kv = hd * F_KV // F_HEADS
                t = pe.do(lambda e: e.matmul(ps[:, b, j * P:j * P + P], v[:, kv * F_HD:(kv + 1) * F_HD], probT[:, hd],
                                             start=True, stop=True), stage[n], v_t)
            oT_t = dve.do(lambda e: e.tensor_copy(oT[:, hs].rearrange(flat2), ps[:, b, :]), t)
        for m in range(KT):
            for hd in range(F_HEADS):
                t = pe.do(lambda e: e.matmul(ps[:, 1, m * P:m * P + P], wo[:, hd, m * P:m * P + P], oT[:, hd],
                                             start=(hd == 0), stop=(hd == F_HEADS - 1)), oT_t, l_wo, v_t)
        x1 = sb("x1", [P, KT, P])
        x1_t = dve.do(lambda e: e.tensor_tensor(x1[:, :].rearrange(flat2), xs[:, :].rearrange(flat2), ps[:, 1, 0:2 * P],
                                                ALU.add), t)

        h2, h2_t = rms("h2", x1, x1_t, 1)
        sig_gate = act.do(lambda e: e.activation(gate[:], ps[:, 6, 0:P], ACT.Sigmoid), gate_mm)
        hid, sg = s[:, :].rearrange("p (f q) -> p f q", q=P), diag
        for half in range(2):
            fs = slice(4 * half, 4 * half + 4)
            bg, bu = (0, 3)[half], (4, 5)[half]
            for w, lw, b in ((wg, l_wg, bg), (wu, l_wu, bu)):
                for j in range(4):
                    f = 4 * half + j
                    for k in range(KT):
                        t = pe.do(lambda e: e.matmul(ps[:, b, j * P:j * P + P], w[:, k, f * P:f * P + P], h2[:, k],
                                                     start=(k == 0), stop=(k == KT - 1)), h2_t, lw, oT_t)
                if w is wg:
                    tg = act.do(lambda e: e.activation(sg[:, fs].rearrange(flat2), ps[:, b, :], ACT.Sigmoid), t)
            tg = dve.do(lambda e: e.tensor_tensor(sg[:, fs].rearrange(flat2), sg[:, fs].rearrange(flat2), ps[:, bg, :], ALU.mult), tg)
            hid_t = dve.do(lambda e: e.tensor_tensor(hid[:, fs].rearrange(flat2), sg[:, fs].rearrange(flat2), ps[:, bu, :],
                                                     ALU.mult), tg, t)
        for m in range(KT):
            for f in range(FI_T):
                t = pe.do(lambda e: e.matmul(ps[:, 2, m * P:m * P + P], wd[:, f, m * P:m * P + P], hid[:, f],
                                             start=(f == 0), stop=(f == FI_T - 1)), hid_t, l_wd, v_t)
        ch = sb("ch", [P, KT, P])
        a = pool.do(lambda e: e.tensor_tensor(ch[:], x1[:], xs[:], ALU.subtract), x1_t, xs_t)
        t = dve.do(lambda e: e.tensor_tensor(ch[:, :].rearrange(flat2), ch[:, :].rearrange(flat2), ps[:, 2, 0:2 * P], ALU.add), t, a)
        t = dve.do(lambda e: e.tensor_tensor(ch[:], ch[:], gate[:].unsqueeze(1).broadcast_to([P, KT, P]), ALU.mult), t, sig_gate)
        chT = sb("chT", [P, D])
        for m in range(KT):
            tp = pe.do(lambda e: e.transpose(ps[:, 6, m * P:m * P + P], ch[:, m], g.ident[:]), t)
        t = act.do(lambda e: e.activation(chT[:], ps[:, 6, 0:D], ACT.Copy), tp)
        for m in range(KT):
            for c in range(NH2):
                b, cc = (0, 3, 4, 5)[2 * m + c], slice(c * HALF, (c + 1) * HALF)
                tp = pe.do(lambda e: e.matmul(ps[:, b, :], chT[:, m * P:m * P + P], takeT[:, cc], start=True, stop=True),
                           t, takeT_t, hid_t)
                dve.do(lambda e: e.tensor_tensor(g.x[:, m, cc], g.x[:, m, cc], ps[:, b, :], ALU.add), tp, x_plus)


def ffn_first(g, ins):
    ffn(g, ins, "f1")


def ffn_second(g, ins):
    ffn(g, ins, "f2")


def halves():
    return [(c, slice(c * HALF, (c + 1) * HALF)) for c in range(NH2)]


def linear(g, w, acts, m_tiles, banks, take, *tokens, only=None, at=None):
    pe = g.pr.pe
    w_hi, w_lo = w
    a_hi, a_lo = acts
    free = {}
    n = 0
    for m in m_tiles:
        for c, cc in halves() if only is None else [halves()[only]]:
            b = banks[n % len(banks)]
            n += 1
            mm = slice(m * P, m * P + P)
            ac = at or cc
            t = matmul3(pe, g.ps[:, b, :],
                        [(w_hi[:, k, mm], None if w_lo is None else w_lo[:, k, mm], a_hi[:, k, ac], a_lo[:, k, ac])
                         for k in range(w_hi.shape[1])], tokens, free.get(b))
            free[b] = take(m, c, cc, g.ps[:, b, :], t)
    return [t for ts in free.values() for t in ts]


def split(g, hi, lo, src, *tokens):
    th = g.pr.act.do(lambda e: e.activation(hi, src, ACT.Copy), *tokens)
    return g.pr.dve.do(lambda e: e.tensor_tensor(lo, src, fr(hi), ALU.subtract), th, *tokens)


T_E = 1024
TE_T = T_E // P
TERNARY = (("up", KT, T_E), ("gate", KT, T_E), ("down", TE_T, D))


def ternary_load(g, ins):
    pr = g.pr
    g.t_raw, g.t_loaded = {}, {}
    for name, kt, cols in TERNARY:
        g.t_raw[name] = pr.sb("t_raw_" + name, [P, kt, cols])
        slot = pr.slot(f"t_{name}_loaded")
        g.t_loaded[name] = pr.sp.dma(slot, lambda: g.t_raw[name][:], lambda: ins["t_" + name])
    g.t_part, g.t_avg, g.t_neg = pr.sb("t_part", [P, 3]), pr.sb("t_avg", [P, P]), pr.sb("t_neg", [P, KT * T_E])
    g.t_avg_t = pr.dve.do(lambda e: e.memset(g.t_avg[:], 1.0 / (T_E * D)))


def ternary_weights(g):
    pr = g.pr
    pe, dve, act, pool = pr.pe, pr.dve, pr.act, pr.pool
    free = None
    for n, (name, kt, cols) in enumerate(TERNARY):
        raw = g.t_raw[name][:, :, :].rearrange("p a b -> p (a b)")
        tern = g.tern[name][:, :, :].rearrange("p a b -> p (a b)")
        t = act.do(lambda e: e.activation(g.t_neg[:], raw, ACT.Abs, accum_out=g.t_part[:, n:n + 1]), g.t_loaded[name], free)
        t = pe.do(lambda e: e.matmul(g.ps[:, n, 0:1], g.t_avg[:], g.t_part[:, n:n + 1], start=True, stop=True), t, g.t_avg_t)
        s = g.scale[:, n]
        t = dve.do(lambda e: e.tensor_scalar(s[:, 0:1], g.ps[:, n, 0:1], 1e-8, None, ALU.add), t)
        dve.do(lambda e: e.tensor_scalar(s[:, 1:2], s[:, 0:1], 0.5, None, ALU.mult), t)
        t = dve.do(lambda e: e.tensor_scalar(s[:, 2:3], s[:, 0:1], -0.5, None, ALU.mult), t)
        t = dve.do(lambda e: e.tensor_scalar(g.t_neg[:], raw, s[:, 2:3], None, ALU.is_lt), t)
        free = dve.do(lambda e: e.scalar_tensor_tensor(tern, raw, s[:, 1:2], g.t_neg[:], ALU.is_gt, ALU.subtract), t)


def recurrence(g, ins):
    pr = g.pr
    pe, dve, act, pool, sp = pr.pe, pr.dve, pr.act, pr.pool, pr.sp
    g.tern = {name: pr.sb("t_" + name, [P, kt, cols], F32R) for name, kt, cols in TERNARY}
    g.scale = pr.sb("t_scale", [P, 3, 3])
    with pr.phase():
        h = pr.sb("r_h", [P, KT, N])
        h_hi, h_lo = pr.sb("r_h_hi", [P, KT, N], F32R), pr.sb("r_h_lo", [P, KT, N], F32R)
        w = pr.sb("r_w", [P, KT, 2 * D])
        w_hi, w_lo = pr.sb("r_w_hi", [P, KT, 2 * D], F32R), pr.sb("r_w_lo", [P, KT, 2 * D], F32R)
        bias = pr.sb("r_bias", [P, 2 * KT])
        gates, values, hidden = pr.sb("r_gates", [P, KT, N]), pr.sb("r_values", [P, KT, N]), pr.sb("r_hidden", [P, KT, N])
        s_w = pr.slot("r_loaded")
        sp.dma(s_w, lambda: bias[:], lambda: ins["r_b"])
        t = sp.dma(s_w, lambda: w[:], lambda: ins["r_w"])
        ternary_load(g, ins)
        w_t = split(g, w_hi[:], w_lo[:], w[:], t)
        hn = normalise(g, "r_n", g.x, h, N, 1e-5, centre=True, split=(h_hi, h_lo))
        done = {}

        def take(m, c, cc, ps, t):
            dst, func = (gates, ACT.Sigmoid) if m < KT else (values, ACT.Tanh)
            a = act.do(lambda e: e.activation(dst[:, m % KT, cc], ps, func, bias=bias[:, m:m + 1]), t)
            done[m, c] = a
            if m >= KT:
                f = m - KT
                first = 0.0 if c == 0 else hidden[:, f, c * HALF - 1:c * HALF]
                s = dve.do(lambda e: e.tensor_tensor_scan(hidden[:, f, cc], gates[:, f, cc], values[:, f, cc], first,
                                                          ALU.mult, ALU.add), a, done[f, c], done.get(("scan", f, c - 1)))
                done["scan", f, c] = s
                dve.do(lambda e: e.tensor_tensor(g.x[:, f, cc], g.x[:, f, cc], hidden[:, f, cc], ALU.add), s)
            return [a]

        linear(g, (w_hi, w_lo), (h_hi, h_lo), (0, 2, 1, 3), (4, 5, 6, 7), take, w_t, hn)
        ternary_weights(g)


R_F, R_TAPS, R_C = 768, 4, 8.0
RF_T = R_F // P


def rglru(g, ins):
    pr = g.pr
    pe, dve, act, pool, sp = pr.pe, pr.dve, pr.act, pr.pool, pr.sp
    with pr.phase():
        def sb(name, shape, dt=F32):
            return pr.sb("l_" + name, shape, dt)

        bias = sb("bias", [P, 10, KT])
        LEFT, RIGHT, CONV, GA, GX, AP, OUT, DOWN, NORM1, NORM2 = range(10)
        up_b = sb("up_b", [P, 2, RF_T])
        taps = sb("taps", [P, R_TAPS, KT])
        s_b = pr.slot("l_bias_loaded")
        sp.dma(s_b, lambda: bias[:], lambda: ins["l_bias"])
        sp.dma(s_b, lambda: up_b[:], lambda: ins["l_up_b"])
        b_t = sp.dma(s_b, lambda: taps[:], lambda: ins["l_taps"])

        raw = [sb("raw0", [P, KT * R_F]), sb("raw1", [P, KT * R_F])]
        raw_slot = [pr.slot("l_raw0_loaded"), pr.slot("l_raw1_loaded")]
        raw_free = [None, None]
        w, w_t = {}, {}
        for n, (name, kt, cols) in enumerate((("left", KT, D), ("right", KT, D), ("ga", KT, D), ("gx", KT, D), ("out", KT, D),
                                              ("up1", KT, R_F), ("up2", KT, R_F), ("down", RF_T, D))):
            r = raw[n % 2][:, 0:kt * cols].rearrange("p (k n) -> p k n", k=kt)
            hi, lo = sb(name + "_hi", [P, kt, cols], F32R), sb(name + "_lo", [P, kt, cols], F32R)
            t = sp.dma(raw_slot[n % 2], lambda: r, lambda: ins["l_" + name], raw_free[n % 2])
            tl = pool_split(g, hi[:], lo[:], r, t)
            raw_free[n % 2] = [tl]
            w[name], w_t[name] = (hi, lo), tl

        sm = sb("softplus", [P, 6, KT])
        a_par = bias[:, AP]
        t = act.do(lambda e: e.activation(sm[:, 0], a_par, ACT.Abs), b_t)
        t = act.do(lambda e: e.activation(sm[:, 1], sm[:, 0], ACT.Exp, scale=-1.0), t)
        t = dve.do(lambda e: e.tensor_scalar(sm[:, 2], sm[:, 1], 1.0, None, ALU.add), t)
        tw = act.do(lambda e: e.activation(sm[:, 3], sm[:, 2], ACT.Ln), t)
        t = dve.do(lambda e: e.tensor_scalar(sm[:, 4], sm[:, 2], -1.0, None, ALU.add), t)
        t = dve.do(lambda e: e.tensor_scalar(sm[:, 5], sm[:, 4], 0.0, None, ALU.is_equal), t)
        t = dve.do(lambda e: e.tensor_tensor(sm[:, 4], sm[:, 4], sm[:, 5], ALU.add), t)
        t = dve.do(lambda e: e.reciprocal(sm[:, 4], sm[:, 4]), t)
        t = dve.do(lambda e: e.tensor_tensor(sm[:, 4], sm[:, 4], sm[:, 3], ALU.mult), t, tw)
        t = dve.do(lambda e: e.tensor_tensor(sm[:, 4], sm[:, 4], sm[:, 5], ALU.add), t)
        t = dve.do(lambda e: e.tensor_tensor(sm[:, 4], sm[:, 4], sm[:, 1], ALU.mult), t)
        t = dve.do(lambda e: e.scalar_tensor_tensor(sm[:, 0], a_par, 0.0, sm[:, 4], ALU.max, ALU.add), t)
        rate_t = dve.do(lambda e: e.tensor_scalar(sm[:, 0], sm[:, 0], -R_C, None, ALU.mult), t)
        rate = sm[:, 0]

        u = sb("u", [P, KT, N])
        xn, xn_hi, xn_lo = sb("xn", [P, KT, N]), sb("xn_hi", [P, KT, N], F32R), sb("xn_lo", [P, KT, N], F32R)
        scratch = norm_scratch(pr, "l_norm", N)
        un = normalise(g, "l_n0", g.x, u, N, 1e-5, centre=True, scratch=scratch)
        un = [o[0] for o in un]
        nn = normalise(g, "l_n1", u, xn, N, 1e-8, src_ready=un + [b_t], weight=bias[:, NORM1], split=(xn_hi, xn_lo),
                       scratch=scratch)
        left = sb("left", [P, KT, N])
        PAD = R_TAPS - 1
        right = sb("right", [P, KT, PAD + N])
        z = dve.do(lambda e: e.memset(right[:, :, 0:PAD], 0.0))
        left_t, right_t = [], [z]

        def take_left(m, c, cc, ps, t):
            a = act.do(lambda e: e.activation(left[:, m, cc], ps, ACT.Gelu, bias=bias[:, LEFT, m:m + 1]), t)
            left_t.append(a)
            return [a]

        def take_right(m, c, cc, ps, t):
            a = dve.do(lambda e: e.tensor_scalar(right[:, m, PAD + c * HALF:PAD + (c + 1) * HALF], ps,
                                                 bias[:, RIGHT, m:m + 1], None, ALU.add), t)
            right_t.append(a)
            return [a]

        linear(g, w["right"], (xn_hi, xn_lo), range(KT), (4, 5, 6, 7), take_right, w_t["right"], nn)
        linear(g, w["left"], (xn_hi, xn_lo), range(KT), (0, 1, 2, 3), take_left, w_t["left"])
        xn_read = pe.last()
        y = xn
        y_hi, y_lo = xn_hi, xn_lo
        y_t = []
        for m in range(KT):
            t = dve.do(lambda e: e.tensor_scalar(y[:, m], right[:, m, 0:N], taps[:, 0, m:m + 1], bias[:, CONV, m:m + 1],
                                                 ALU.mult, ALU.add), right_t, nn)
            for j in range(1, R_TAPS):
                t = dve.do(lambda e: e.scalar_tensor_tensor(y[:, m], right[:, m, j:j + N], taps[:, j, m:m + 1], y[:, m],
                                                            ALU.mult, ALU.add), t)
            y_t.append(split(g, y_hi[:, m], y_lo[:, m], y[:, m], t, xn_read))
        rg, ig, th = sb("rg", [P, KT, N]), sb("ig", [P, KT, N]), right[:, :, PAD:]
        a_ = scratch[0][:, :, :, :].rearrange("p a k w -> p (a k w)").rearrange("p (k n) -> p k n", k=KT)
        sig_t = []
        for dst, name, bb, banks in ((rg, "ga", GA, (0, 1, 2, 3)), (ig, "gx", GX, (4, 5, 6, 7))):
            def take(m, c, cc, ps, t):
                a = act.do(lambda e: e.activation(dst[:, m, cc], ps, ACT.Sigmoid, bias=bias[:, bb, m:m + 1]), t)
                sig_t.append(a)
                return [a]
            linear(g, w[name], (y_hi, y_lo), range(KT), banks, take, w_t[name], y_t, left_t)
        for m in range(KT):
            ta = act.do(lambda e: e.activation(a_[:, m], rg[:, m], ACT.Exp, scale=rate[:, m:m + 1]), sig_t, rate_t)
            tt = act.do(lambda e: e.activation(th[:, m], rg[:, m], ACT.Tanh, scale=rate[:, m:m + 1]), y_t)
            tr = dve.do(lambda e: e.tensor_tensor(rg[:, m], a_[:, m], a_[:, m], ALU.mult), ta, tt)
            t = dve.do(lambda e: e.scalar_tensor_tensor(rg[:, m], rg[:, m], 1.0, th[:, m], ALU.add, ALU.mult), tr, tt)
            sig_t.append(t)
            ti = pool.do(lambda e: e.tensor_tensor(ig[:, m], ig[:, m], y[:, m], ALU.mult), sig_t[:-1], y_t)
            sig_t.append(ti)
        prod_t = []
        for m in range(KT):
            t = act.do(lambda e: e.activation(rg[:, m], rg[:, m], ACT.Sqrt, scale=-1.0), sig_t)
            t = dve.do(lambda e: e.tensor_tensor(ig[:, m], ig[:, m], rg[:, m], ALU.mult), t, sig_t)
            t = dve.do(lambda e: e.tensor_tensor_scan(th[:, m], a_[:, m], ig[:, m], 0.0, ALU.mult, ALU.add), t)
            t = dve.do(lambda e: e.tensor_tensor(left[:, m], left[:, m], th[:, m], ALU.mult), t, left_t)
            prod_t.append(split(g, y_hi[:, m], y_lo[:, m], left[:, m], t, sig_t))
        x1, x1_t = y, []

        def take_out(m, c, cc, ps, t):
            a = dve.do(lambda e: e.scalar_tensor_tensor(x1[:, m, cc], ps, bias[:, OUT, m:m + 1], u[:, m, cc],
                                                        ALU.add, ALU.add), t)
            x1_t.append(a)
            return [a]

        linear(g, w["out"], (y_hi, y_lo), range(KT), (0, 1, 2, 3), take_out, w_t["out"], prod_t)
        out_read = pe.last()
        x_t = pool.do(lambda e: e.tensor_tensor(g.x[:], g.x[:], x1[:], ALU.add), x1_t)
        nn2 = normalise(g, "l_n2", x1, left, N, 1e-8, src_ready=x1_t, dst_free=[out_read] + prod_t,
                        weight=bias[:, NORM2], split=(y_hi, y_lo), scratch=scratch)
        mid_hi, mid_lo = sb("mid_hi", [P, RF_T, HALF], F32R), sb("mid_lo", [P, RF_T, HALF], F32R)
        gel, down_read = {}, None
        bufs = [rg[:, 0], ig[:, 0]], [rg[:, 1], ig[:, 1]]
        f1 = {0: None, 1: None}
        f2 = {0: None, 1: None}
        for half in range(NH2):
            mid_t = []
            for f in range(RF_T):
                par = f % 2
                gb, pb = bufs[0][par][:, 0:HALF], bufs[1][par][:, 0:HALF]

                def take1(m, c, cc, ps, t):
                    gel["gelu"] = act.do(lambda e: e.activation(gb, ps, ACT.Gelu, bias=up_b[:, 0, m:m + 1]), t,
                                         gel.get(("used", par)))
                    return [gel["gelu"]]

                def take2(m, c, cc, ps, t):
                    a = dve.do(lambda e: e.scalar_tensor_tensor(pb, ps, up_b[:, 1, m:m + 1], gb, ALU.add, ALU.mult),
                               t, gel["gelu"], gel.get(("used", par)))
                    gel["used", par] = split(g, mid_hi[:, m], mid_lo[:, m], pb, a, down_read)
                    mid_t.append(gel["used", par])
                    return [a]

                f1[par] = linear(g, w["up1"], (y_hi, y_lo), [f], (4 + par,), take1, w_t["up1"], nn2, f1[par], only=half)
                f2[par] = linear(g, w["up2"], (y_hi, y_lo), [f], (6 + par,), take2, w_t["up2"], f2[par], only=half)

            def take_down(m, c, cc, ps, t):
                return [dve.do(lambda e: e.scalar_tensor_tensor(g.x[:, m, cc], ps, bias[:, DOWN, m:m + 1], g.x[:, m, cc],
                                                                ALU.add, ALU.add), t, x_t)]

            linear(g, w["down"], (mid_hi, mid_lo), range(KT), (2 * half, 2 * half + 1), take_down, w_t["down"], mid_t,
                   only=half, at=slice(0, HALF))
            down_read = [pe.last()]


def ternary_ffn(g, ins, tag):
    pr = g.pr
    pe, dve, act, pool, sp = pr.pe, pr.dve, pr.act, pr.pool, pr.sp
    with pr.phase():
        h = pr.sb(tag + "_h", [P, KT, N])
        h_hi, h_lo = pr.sb(tag + "_h_hi", [P, KT, N], F32R), pr.sb(tag + "_h_lo", [P, KT, N], F32R)
        hn = normalise(g, tag + "_n", g.x, h, N, 1e-5, centre=True, split=(h_hi, h_lo))
        sg, hid = pr.sb(tag + "_sg", [P, 2, N]), pr.sb(tag + "_hid", [P, 3, N])
        hid_hi, hid_lo = pr.sb(tag + "_hid_hi", [P, TE_T, N], F32R), pr.sb(tag + "_hid_lo", [P, TE_T, N], F32R)
        s_up, s_gate, s_down = (g.scale[:, n, 0:1] for n in range(3))
        st, hid_t = {}, []

        def split_hidden(f):
            his = [act.do(lambda e: e.activation(hid_hi[:, f, cc], hid[:, f % 3, cc], ACT.Copy), st["made", f, c])
                   for c, cc in halves()]
            los = [lane.do(lambda e: e.tensor_tensor(hid_lo[:, f, cc], hid[:, f % 3, cc], fr(hid_hi[:, f, cc]), ALU.subtract),
                           his[c], st["made", f, c]) for (c, cc), lane in zip(halves(), (dve, pool))]
            st["used", f % 3] = his + los
            hid_t.extend(his + los)

        for f in range(TE_T):
            par = f % 2

            def take_up(m, c, cc, ps, t):
                a = act.do(lambda e: e.activation(sg[:, par, cc], ps, ACT.Sigmoid, scale=s_up), t, st.get(("made", f - 2, c)))
                b = dve.do(lambda e: e.scalar_tensor_tensor(sg[:, par, cc], ps, s_up, sg[:, par, cc], ALU.mult, ALU.mult), a)
                st[c] = b
                return [b]

            def take_gate(m, c, cc, ps, t):
                b = dve.do(lambda e: e.scalar_tensor_tensor(hid[:, f % 3, cc], ps, s_gate, sg[:, par, cc], ALU.mult, ALU.mult),
                           t, st[c], st.get(("used", f % 3)))
                st["made", f, c] = b
                return [b]

            f1 = linear(g, (g.tern["up"], None), (h_hi, h_lo), [f], (4, 5) if par else (0, 1), take_up, hn, st.get(("f1", par)))
            f2 = linear(g, (g.tern["gate"], None), (h_hi, h_lo), [f], (6, 7) if par else (2, 3), take_gate,
                        st.get(("f2", par)))
            st["f1", par], st["f2", par] = f1, f2
            if f:
                split_hidden(f - 1)
        split_hidden(TE_T - 1)

        def take_down(m, c, cc, ps, t):
            return [dve.do(lambda e: e.scalar_tensor_tensor(g.x[:, m, cc], ps, s_down, g.x[:, m, cc], ALU.mult, ALU.add), t)]

        linear(g, (g.tern["down"], None), (hid_hi, hid_lo), range(KT), (0, 1, 2, 3), take_down, hid_t, f1, f2)


def ternary_first(g, ins):
    ternary_ffn(g, ins, "t1")


def ternary_second(g, ins):
    ternary_ffn(g, ins, "t2")


def build(nc, ins, out):
    with ExitStack() as ctx:
        g = Env()
        pr = g.pr = Prog(nc, ctx)
        g.ps = ctx.enter_context(nc.psum_tensor("ps", [P, 8, HALF], F32))
        g.ps_flat = g.ps[:, :, :].rearrange("p b n -> p (b n)")
        g.bank = [g.ps[:, b, :] for b in range(8)]
        setup(g, ins)
        for layer in LAYERS:
            layer(g, ins)
        s_out = pr.slot("x_stored")
        pr.fence()
        pr.sp.wait(g.x_ready)
        t = pr.sp.dma(s_out, lambda: out.rearrange("(k p) n -> p k n", p=P), lambda: g.x[:])
        pr.sp.wait(t)


LAYERS = [attn_a, ffn_first, attn_b, ffn_second, recurrence, ternary_first, rglru, ternary_second]


def rope_tables(n, dim, theta=10000.0):
    inv = (1.0 / np.float32(theta) ** (np.arange(0, dim, 2, dtype=np.float32) / np.float32(dim))).astype(np.float32)
    ang = (np.arange(n, dtype=np.float32)[:, None] * inv[None, :]).astype(np.float32)
    return np.cos(ang).astype(np.float32), np.sin(ang).astype(np.float32)


def layout(i):
    a = {k: np.asarray(v) for k, v in i.items()}
    r = {}
    r["x"] = a["L0_attn_a_hidden_states"][0].T
    q = a["L0_attn_a_Wq"].T.reshape(D, A_KV, A_GRP * A_HD)
    k = a["L0_attn_a_Wk"].T.reshape(D, A_KV, A_HD)
    v = a["L0_attn_a_Wv"].T.reshape(D, A_KV, A_HD)
    r["a_w"] = np.concatenate([q, k, v], 2).reshape(KT, P, A_KV, A_W).transpose(2, 1, 0, 3)
    r["a_o"] = a["L0_attn_a_Wo"].T.reshape(A_KV, 2, P, D).transpose(0, 2, 1, 3)
    cos, sin = rope_tables(N, A_HD)
    r["a_cos"] = np.concatenate([cos, cos], 1).reshape(TT, P, A_HD).transpose(1, 0, 2)
    r["a_sin"] = np.concatenate([-sin, sin], 1).reshape(TT, P, A_HD).transpose(1, 0, 2)
    q, k, v = (a["L0_attn_b_W_" + c].transpose(1, 0, 2) for c in "QKV")
    r["b_qk"] = np.concatenate([q, k], 2).reshape(KT, P, B_HEADS, 2 * B_HD).transpose(2, 1, 0, 3)
    r["b_v"] = v.reshape(KT, P, B_HEADS // B_PAIR, B_PAIR * B_HD).transpose(2, 1, 0, 3)
    r["b_o"] = a["L0_attn_b_W_O"].reshape(B_HEADS // B_PAIR, B_PAIR, B_HD, D).transpose(0, 2, 1, 3)
    r["b_bias"] = np.stack([a["L0_attn_b_b_" + c] for c in "QKV"]).transpose(2, 0, 1)
    r["b_bias_out"] = a["L0_attn_b_b_O"].reshape(KT, P).T

    def tiles(w):
        return w.reshape(-1, P, w.shape[1]).transpose(1, 0, 2)

    f = {k[7:]: v for k, v in a.items() if k.startswith("L0_ffn_")}
    r["f_wr"] = f["w_router"].reshape(KT, P).T
    r["f_ln"] = np.stack([f["ln1_w"], f["ln2_w"]]).reshape(2, KT, P).transpose(2, 0, 1)
    r["f_bqk"] = np.concatenate([f["bq"], f["bk"]]).reshape(-1, P).T
    r["f_bv"] = f["bv"][None, :]
    for name, key in (("wq", "wq"), ("wk", "wk"), ("wv", "wv"), ("wo", "wo"), ("wg", "w_gate"), ("wu", "w_up"), ("wd", "w_down")):
        r["f_" + name] = tiles(f[key])
    cos, sin = rope_tables(N, F_HD)
    tab = np.stack([np.concatenate([cos, cos], 1), np.concatenate([sin, -sin], 1)], 1)
    r["f_rope"] = tab.reshape(TT, P, 2, P).transpose(1, 0, 2, 3)
    r["r_w"] = tiles(a["L1_attn_a_W"].T)
    r["r_b"] = a["L1_attn_a_b"].reshape(-1, P).T
    l = {k[10:]: v for k, v in a.items() if k.startswith("L1_attn_b_")}
    for name in ("left", "right", "ga", "gx", "out", "up1", "up2", "down"):
        r["l_" + name] = tiles(l[name + "_W"])
    vectors = ("left_b", "right_b", "conv_b", "ga_b", "gx_b", "a_param", "out_b", "down_b", "norm1_w", "norm2_w")
    r["l_bias"] = np.stack([l[v] for v in vectors]).reshape(len(vectors), KT, P).transpose(2, 0, 1)
    r["l_up_b"] = np.stack([l["up1_b"], l["up2_b"]]).reshape(2, RF_T, P).transpose(2, 0, 1)
    r["l_taps"] = l["conv_w"].reshape(R_TAPS, KT, P).transpose(2, 0, 1)
    for name in ("up", "gate", "down"):
        r["t_" + name] = tiles(a["L1_ffn_W_" + name].T)
    return r


def kernel(**inputs):
    import concourse.bacc as bacc
    from concourse.bass_utils import run_bass_kernel_spmd

    nc = bacc.Bacc("TRN2", target_bir_lowering=False, num_devices=1)
    arrays = {f"in_{k}": np.ascontiguousarray(v) for k, v in layout(inputs).items()}
    ins = {k[3:]: nc.dram_tensor(k, v.shape, mybir.dt.from_np(v.dtype), kind="ExternalInput").ap()
           for k, v in arrays.items()}
    out = nc.dram_tensor("out", (D, N), F32, kind="ExternalOutput").ap()
    build(nc, ins, out)
    got = run_bass_kernel_spmd(nc, [arrays], core_ids=[0])
    return np.ascontiguousarray(got.results[0]["out"].T).reshape(1, N, D)
```
